# Optimizing a Trainium2 kernel written in Bass

```python
import numpy as np
import jax
import jax.numpy as jnp

def _softmax(x, axis=-1):
    return jax.nn.softmax(x, axis=axis)

def _gelu(x):
    return jax.nn.gelu(x, approximate=True)

def _silu(x):
    return jax.nn.silu(x)

def _sigmoid(x):
    return jax.nn.sigmoid(x)

def _layernorm(x, axis=-1, eps=1e-05):
    m = jnp.mean(x, axis=axis, keepdims=True)
    v = jnp.var(x, axis=axis, keepdims=True)
    return (x - m) / jnp.sqrt(v + eps)

def _scatter_add(tgt, idx, src, axis=0):
    return tgt.at[idx].add(src)

def _segment_sum(src, seg, n):
    return jax.ops.segment_sum(src, seg, n)
kernel_name = 'mk_decoder_preln_d2_seqx_r4_66f58d'

def setup_inputs(seed: int=0):
    np.random.seed(seed)
    _w = jnp.asarray

    def _rec_inputs():
        import jax
        import jax.numpy as jnp
        _rk = jax.random.key(seed)
        x = 7.22e-05 + 1 * jax.random.normal(jax.random.fold_in(_rk, 1), (8, 512, 256), jnp.float32)
        _lenS = 512 - jax.random.randint(jax.random.fold_in(_rk, 7), (8,), 0, max(1, 512 // 4) + 1, jnp.int32)
        _lenS2 = 512 - jax.random.randint(jax.random.fold_in(_rk, 8), (8,), 0, max(1, 512 // 4) + 1, jnp.int32)
        _ctx_1024P = jax.random.normal(jax.random.fold_in(_rk, 11), (8, 16, 256), jnp.float32)
        _ctx_1024c = jax.random.dirichlet(jax.random.fold_in(_rk, 511), 0.3 * jnp.ones((16,), jnp.float32), (8, 512))
        _ctx_1024t = jnp.einsum('bsk,bkd->bsd', _ctx_1024c, _ctx_1024P)
        _ctx_1024t = _ctx_1024t * jax.lax.rsqrt(jnp.mean(jnp.square(_ctx_1024t)) + 1e-12) * 0.953939
        ctx_1024 = 4.13588e-05 + 0.999923 * (_ctx_1024t + 0.3 * jax.random.normal(jax.random.fold_in(_rk, 611), (8, 512, 256), jnp.float32))
        _validS = jnp.arange(512)[None, :] < _lenS[:, None]
        _validS2 = jnp.arange(512)[None, :] < _lenS2[:, None]
        _causal = jnp.tril(jnp.ones((512, 512), dtype=bool))
        mask_BxS2_bf1 = jnp.ones((8, 512), dtype=bool)
        return (x, ctx_1024, mask_BxS2_bf1)
    x, ctx_1024, mask_BxS2_bf1 = _rec_inputs()

    def _L0_attn_setup():
        import jax, jax.numpy as jnp
        import numpy as np
        B, S, D = (2, 1024, 256)
        LOOKBACK = 64
        TOPK = 16
        CHUNK = 32
        NEG = -1e+30

        def _phrase_states(h):
            b, seq, d = h.shape
            hc = h.reshape(b, seq // CHUNK, CHUNK, d)
            pref = jnp.cumsum(hc, axis=2)
            denom = jnp.arange(1, CHUNK + 1, dtype=h.dtype).reshape(1, 1, CHUNK, 1)
            return (pref / denom).reshape(b, seq, d)

        def _shift1(x):
            return jnp.pad(x, ((0, 0), (1, 0), (0, 0)))[:, :-1]
        key = jax.random.key(seed)
        ks = jax.random.split(key, 11)
        s = 0.02
        inp = {'h': jax.random.normal(ks[0], (B, S, D), jnp.float32)}
        names = ['q_w', 'k_w', 'v_w', 'pk_w', 'pv_w']
        for i, n in enumerate(names):
            inp[n] = jax.random.normal(ks[1 + i], (D, D), jnp.float32) * s
            inp[n.replace('_w', '_b')] = jax.random.normal(ks[6 + i], (D,), jnp.float32) * s
        return inp
    _L0_attn_all = _L0_attn_setup()
    _L0_attn_in = {k: v for k, v in _L0_attn_all.items() if k in ('q_w', 'q_b', 'k_w', 'k_b', 'v_w', 'v_b', 'pk_w', 'pk_b', 'pv_w', 'pv_b')}
    del _L0_attn_all

    def _L0_xattn_setup():
        import jax, jax.numpy as jnp
        import numpy as np
        THETA = 10000.0

        def _rope_tables(T, head_dim, dtype):
            exps = jnp.arange(1, head_dim + 1, 2, dtype=jnp.float32)[:head_dim // 2] / head_dim
            w = 1.0 / THETA ** exps
            t = jnp.arange(1, T + 1, dtype=jnp.float32)
            angles = t[:, None] * w[None, :]
            return (jnp.sin(angles).astype(dtype), jnp.cos(angles).astype(dtype))

        def _rotate(x, sin, cos):
            x1 = x[..., ::2]
            x2 = x[..., 1::2]
            x1p = x1 * cos - x2 * sin
            x2p = x1 * sin + x2 * cos
            return jnp.stack((x1p, x2p), axis=-1).reshape(x.shape)
        key = jax.random.key(seed)
        B, Tq, Tkv, C = (4, 512, 512, 256)
        k1, k2, k3, k4, k5 = jax.random.split(key, 5)
        s = 1.0 / np.sqrt(C)
        return {'x_q': jax.random.normal(k1, (B, Tq, C), dtype=jnp.float32), 'x_kv': jax.random.normal(k2, (B, Tkv, C), dtype=jnp.float32), 'q_tok_mask': jnp.ones((B, Tq), dtype=bool), 'kv_tok_mask': jnp.ones((B, Tkv), dtype=bool), 'W_q': jax.random.normal(k3, (C, C), dtype=jnp.float32) * s, 'W_kv': jax.random.normal(k4, (C, 2 * C), dtype=jnp.float32) * s, 'W_c': jax.random.normal(k5, (C, C), dtype=jnp.float32) * s}
    _L0_xattn_all = _L0_xattn_setup()
    _L0_xattn_in = {k: v for k, v in _L0_xattn_all.items() if k in ('W_q', 'W_kv', 'W_c')}
    del _L0_xattn_all

    def _L0_ffn_setup():
        import jax, jax.numpy as jnp
        import numpy as np
        HIDDEN = 256
        INNER = 1024

        def _weight_quant(w):
            scale = 1.0 / jnp.clip(jnp.mean(jnp.abs(w)), 1e-05)
            wq = jnp.clip(jnp.round(w * scale), -1.0, 1.0) / scale
            return w + jax.lax.stop_gradient(wq - w)

        def _act_quant(x):
            scale = 127.0 / jnp.clip(jnp.max(jnp.abs(x), axis=-1, keepdims=True), 1e-05)
            xq = jnp.clip(jnp.round(x * scale), -128.0, 127.0) / scale
            return x + jax.lax.stop_gradient(xq - x)

        def _bitlinear(x, w):
            return jnp.einsum('bsi,oi->bso', _act_quant(x), _weight_quant(w))
        key = jax.random.key(seed)
        k0, k1, k2, k3 = jax.random.split(key, 4)
        x = jax.random.normal(k0, (4, 512, HIDDEN), dtype=jnp.float32)
        w_gate = jax.random.normal(k1, (INNER, HIDDEN), dtype=jnp.float32) / np.sqrt(HIDDEN)
        w_up = jax.random.normal(k2, (INNER, HIDDEN), dtype=jnp.float32) / np.sqrt(HIDDEN)
        w_down = jax.random.normal(k3, (HIDDEN, INNER), dtype=jnp.float32) / np.sqrt(INNER)
        return {'x': x, 'w_gate': w_gate, 'w_up': w_up, 'w_down': w_down}
    _L0_ffn_all = _L0_ffn_setup()
    _L0_ffn_in = {k: v for k, v in _L0_ffn_all.items() if k in ('w_gate', 'w_up', 'w_down')}
    del _L0_ffn_all

    def _L1_attn_setup():
        import jax, jax.numpy as jnp
        import numpy as np
        D_MODEL, D_QKV, N_HEADS = (256, 64, 16)
        key = jax.random.key(seed)
        k_x, k_qkv, k_out = jax.random.split(key, 3)
        X = jax.random.normal(k_x, (2, 512, D_MODEL), dtype=jnp.float32)
        W_qkv = jax.random.normal(k_qkv, (D_MODEL, 3 * D_QKV * N_HEADS), dtype=jnp.float32) * D_MODEL ** (-0.5)
        W_out = jax.random.normal(k_out, (D_QKV * N_HEADS, D_MODEL), dtype=jnp.float32) * (D_QKV * N_HEADS) ** (-0.5)
        return {'X': X, 'W_qkv': W_qkv, 'W_out': W_out}
    _L1_attn_all = _L1_attn_setup()
    _L1_attn_in = {k: v for k, v in _L1_attn_all.items() if k in ('W_qkv', 'W_out')}
    del _L1_attn_all

    def _L1_xattn_setup():
        import jax, jax.numpy as jnp
        import numpy as np
        EMBED_DIM = 256
        NUM_HEADS = 16
        HEAD_DIM = EMBED_DIM // NUM_HEADS
        WINDOW = 128
        B, S_Q, S_K = (2, 512, 512)

        def apply_rope(x):
            Dh = x.shape[-1]
            half = Dh // 2
            pos = jnp.arange(x.shape[2], dtype=jnp.float32)
            inv_freq = 1.0 / 10000.0 ** (jnp.arange(0, half, dtype=jnp.float32) / half)
            ang = pos[:, None] * inv_freq[None, :]
            cos = jnp.cos(ang)[None, None, :, :].astype(x.dtype)
            sin = jnp.sin(ang)[None, None, :, :].astype(x.dtype)
            x1, x2 = (x[..., :half], x[..., half:])
            return jnp.concatenate([x1 * cos - x2 * sin, x1 * sin + x2 * cos], axis=-1)
        key = jax.random.key(seed)
        ks = jax.random.split(key, 11)
        scale = 1.0 / np.sqrt(EMBED_DIM)
        inp = {'query': jax.random.normal(ks[0], (B, S_Q, EMBED_DIM), jnp.float32), 'key': jax.random.normal(ks[1], (B, S_K, EMBED_DIM), jnp.float32), 'value': jax.random.normal(ks[2], (B, S_K, EMBED_DIM), jnp.float32), 'Wq': jax.random.normal(ks[3], (EMBED_DIM, EMBED_DIM), jnp.float32) * scale, 'bq': jnp.zeros((EMBED_DIM,), jnp.float32), 'Wk': jax.random.normal(ks[4], (EMBED_DIM, EMBED_DIM), jnp.float32) * scale, 'bk': jnp.zeros((EMBED_DIM,), jnp.float32), 'Wv': jax.random.normal(ks[5], (EMBED_DIM, EMBED_DIM), jnp.float32) * scale, 'bv': jnp.zeros((EMBED_DIM,), jnp.float32), 'Wo': jax.random.normal(ks[6], (EMBED_DIM, EMBED_DIM), jnp.float32) * scale, 'bo': jnp.zeros((EMBED_DIM,), jnp.float32)}
        return inp
    _L1_xattn_all = _L1_xattn_setup()
    _L1_xattn_in = {k: v for k, v in _L1_xattn_all.items() if k in ('Wq', 'bq', 'Wk', 'bk', 'Wv', 'bv', 'Wo', 'bo')}
    del _L1_xattn_all

    def _L1_ffn_setup():
        import jax, jax.numpy as jnp
        import numpy as np
        D_MODEL = 256
        D_FF = 1024
        N_EXPERTS = 8
        INIT_SCALE = 0.1

        def _trunc_normal(key, shape, std):
            return std * jax.random.truncated_normal(key, -2.0, 2.0, shape, dtype=jnp.float32)
        key = jax.random.key(seed)
        ks = jax.random.split(key, 5)
        x = jax.random.normal(ks[0], (4, 256, D_MODEL), dtype=jnp.float32)
        router_W = _trunc_normal(ks[1], (D_MODEL, N_EXPERTS), INIT_SCALE / np.sqrt(D_MODEL))
        router_b = jnp.zeros((N_EXPERTS,), dtype=jnp.float32)
        W1 = _trunc_normal(ks[2], (N_EXPERTS, D_MODEL, D_FF), INIT_SCALE / np.sqrt(D_MODEL))
        b1 = jnp.zeros((N_EXPERTS, D_FF), dtype=jnp.float32)
        W2 = _trunc_normal(ks[3], (N_EXPERTS, D_FF, D_MODEL), INIT_SCALE / np.sqrt(D_FF))
        b2 = jnp.zeros((N_EXPERTS, D_MODEL), dtype=jnp.float32)
        return {'x': x, 'router_W': router_W, 'router_b': router_b, 'W1': W1, 'b1': b1, 'W2': W2, 'b2': b2}
    _L1_ffn_all = _L1_ffn_setup()
    _L1_ffn_in = {k: v for k, v in _L1_ffn_all.items() if k in ('router_W', 'router_b', 'W1', 'b1', 'W2', 'b2')}
    del _L1_ffn_all
    return {'x': x, 'ctx_1024': ctx_1024, 'mask_BxS2_bf1': mask_BxS2_bf1, 'L0_attn_q_w': _L0_attn_in['q_w'], 'L0_attn_q_b': _L0_attn_in['q_b'], 'L0_attn_k_w': _L0_attn_in['k_w'], 'L0_attn_k_b': _L0_attn_in['k_b'], 'L0_attn_v_w': _L0_attn_in['v_w'], 'L0_attn_v_b': _L0_attn_in['v_b'], 'L0_attn_pk_w': _L0_attn_in['pk_w'], 'L0_attn_pk_b': _L0_attn_in['pk_b'], 'L0_attn_pv_w': _L0_attn_in['pv_w'], 'L0_attn_pv_b': _L0_attn_in['pv_b'], 'L0_xattn_W_q': _L0_xattn_in['W_q'], 'L0_xattn_W_kv': _L0_xattn_in['W_kv'], 'L0_xattn_W_c': _L0_xattn_in['W_c'], 'L0_ffn_w_gate': _L0_ffn_in['w_gate'], 'L0_ffn_w_up': _L0_ffn_in['w_up'], 'L0_ffn_w_down': _L0_ffn_in['w_down'], 'L1_attn_W_qkv': _L1_attn_in['W_qkv'], 'L1_attn_W_out': _L1_attn_in['W_out'], 'L1_xattn_Wq': _L1_xattn_in['Wq'], 'L1_xattn_bq': _L1_xattn_in['bq'], 'L1_xattn_Wk': _L1_xattn_in['Wk'], 'L1_xattn_bk': _L1_xattn_in['bk'], 'L1_xattn_Wv': _L1_xattn_in['Wv'], 'L1_xattn_bv': _L1_xattn_in['bv'], 'L1_xattn_Wo': _L1_xattn_in['Wo'], 'L1_xattn_bo': _L1_xattn_in['bo'], 'L1_ffn_router_W': _L1_ffn_in['router_W'], 'L1_ffn_router_b': _L1_ffn_in['router_b'], 'L1_ffn_W1': _L1_ffn_in['W1'], 'L1_ffn_b1': _L1_ffn_in['b1'], 'L1_ffn_W2': _L1_ffn_in['W2'], 'L1_ffn_b2': _L1_ffn_in['b2']}

def reference(x, ctx_1024, mask_BxS2_bf1, L0_attn_q_w, L0_attn_q_b, L0_attn_k_w, L0_attn_k_b, L0_attn_v_w, L0_attn_v_b, L0_attn_pk_w, L0_attn_pk_b, L0_attn_pv_w, L0_attn_pv_b, L0_xattn_W_q, L0_xattn_W_kv, L0_xattn_W_c, L0_ffn_w_gate, L0_ffn_w_up, L0_ffn_w_down, L1_attn_W_qkv, L1_attn_W_out, L1_xattn_Wq, L1_xattn_bq, L1_xattn_Wk, L1_xattn_bk, L1_xattn_Wv, L1_xattn_bv, L1_xattn_Wo, L1_xattn_bo, L1_ffn_router_W, L1_ffn_router_b, L1_ffn_W1, L1_ffn_b1, L1_ffn_W2, L1_ffn_b2):
    import jax
    import jax.numpy as jnp

    def _L0_attn_ref(h, q_w, q_b, k_w, k_b, v_w, v_b, pk_w, pk_b, pv_w, pv_b):
        import jax, jax.numpy as jnp
        import numpy as np
        B, S, D = (2, 1024, 256)
        LOOKBACK = 64
        TOPK = 16
        CHUNK = 32
        NEG = -1e+30

        def _phrase_states(h):
            b, seq, d = h.shape
            hc = h.reshape(b, seq // CHUNK, CHUNK, d)
            pref = jnp.cumsum(hc, axis=2)
            denom = jnp.arange(1, CHUNK + 1, dtype=h.dtype).reshape(1, 1, CHUNK, 1)
            return (pref / denom).reshape(b, seq, d)

        def _shift1(x):
            return jnp.pad(x, ((0, 0), (1, 0), (0, 0)))[:, :-1]
        b, seq, d = h.shape
        scale = 1.0 / np.sqrt(d)
        q = h @ q_w.T + q_b
        k = h @ k_w.T + k_b
        v = h @ v_w.T + v_b
        ph = _phrase_states(h)
        pk = ph @ pk_w.T + pk_b
        pv = ph @ pv_w.T + pv_b
        k_prev, v_prev = (_shift1(k), _shift1(v))
        pk_prev, pv_prev = (_shift1(pk), _shift1(pv))
        seq_score = jnp.einsum('bsd,bsd->bs', q, k_prev) * scale
        phr_score = jnp.einsum('bsd,bsd->bs', q, pk_prev) * scale
        k_pad = jnp.pad(k, ((0, 0), (LOOKBACK, 0), (0, 0)))
        t_idx = jnp.arange(seq)

        def step(_, l):
            kl = jax.lax.dynamic_slice_in_dim(k_pad, l, seq, axis=1)
            sc = jnp.einsum('bsd,bsd->bs', q, kl) * scale
            valid = t_idx + l >= LOOKBACK
            return (None, jnp.where(valid[None, :], sc, NEG))
        _, scores = jax.lax.scan(step, None, jnp.arange(LOOKBACK))
        scores = jnp.moveaxis(scores, 0, -1)
        top_sc, top_l = jax.lax.top_k(scores, TOPK)
        gidx = jnp.clip(t_idx[None, :, None] - LOOKBACK + top_l, 0, seq - 1)
        sem_v = jax.vmap(lambda vb, ib: vb[ib])(v, gidx)
        all_sc = jnp.concatenate([seq_score[..., None], top_sc, phr_score[..., None]], axis=-1)
        all_v = jnp.concatenate([v_prev[:, :, None, :], sem_v, pv_prev[:, :, None, :]], axis=2)
        w = jax.nn.softmax(all_sc, axis=-1)
        out = jnp.einsum('bsn,bsnd->bsd', w, all_v)
        return jnp.where(t_idx[None, :, None] > 0, out, jnp.zeros((), out.dtype))

    def _L0_xattn_ref(x_q, x_kv, q_tok_mask, kv_tok_mask, W_q, W_kv, W_c):
        import jax, jax.numpy as jnp
        import numpy as np
        THETA = 10000.0

        def _rope_tables(T, head_dim, dtype):
            exps = jnp.arange(1, head_dim + 1, 2, dtype=jnp.float32)[:head_dim // 2] / head_dim
            w = 1.0 / THETA ** exps
            t = jnp.arange(1, T + 1, dtype=jnp.float32)
            angles = t[:, None] * w[None, :]
            return (jnp.sin(angles).astype(dtype), jnp.cos(angles).astype(dtype))

        def _rotate(x, sin, cos):
            x1 = x[..., ::2]
            x2 = x[..., 1::2]
            x1p = x1 * cos - x2 * sin
            x2p = x1 * sin + x2 * cos
            return jnp.stack((x1p, x2p), axis=-1).reshape(x.shape)
        B, Tq, C = x_q.shape
        Tkv = x_kv.shape[1]
        H = 16
        D = C // H
        q = (x_q @ W_q).reshape(B, Tq, H, D).transpose(0, 2, 1, 3)
        kv = x_kv @ W_kv
        k, v = (kv[..., :C], kv[..., C:])
        k = k.reshape(B, Tkv, H, D).transpose(0, 2, 1, 3)
        v = v.reshape(B, Tkv, H, D).transpose(0, 2, 1, 3)
        sin_q, cos_q = _rope_tables(Tq, D, x_q.dtype)
        sin_k, cos_k = _rope_tables(Tkv, D, x_q.dtype)
        q = _rotate(q, sin_q, cos_q)
        k = _rotate(k, sin_k, cos_k)
        att = jnp.einsum('bhqd,bhkd->bhqk', q, k) / jnp.sqrt(jnp.asarray(D, x_q.dtype))
        mask = (q_tok_mask[:, :, None] & kv_tok_mask[:, None, :])[:, None, :, :]
        att = jnp.where(mask, att, jnp.asarray(-1000000000.0, att.dtype))
        att = jax.nn.softmax(att, axis=-1)
        y = jnp.einsum('bhqk,bhkd->bhqd', att, v)
        y = y.transpose(0, 2, 1, 3).reshape(B, Tq, C)
        return y @ W_c

    def _L0_ffn_ref(x, w_gate, w_up, w_down):
        import jax, jax.numpy as jnp
        import numpy as np
        HIDDEN = 256
        INNER = 1024

        def _weight_quant(w):
            scale = 1.0 / jnp.clip(jnp.mean(jnp.abs(w)), 1e-05)
            wq = jnp.clip(jnp.round(w * scale), -1.0, 1.0) / scale
            return w + jax.lax.stop_gradient(wq - w)

        def _act_quant(x):
            scale = 127.0 / jnp.clip(jnp.max(jnp.abs(x), axis=-1, keepdims=True), 1e-05)
            xq = jnp.clip(jnp.round(x * scale), -128.0, 127.0) / scale
            return x + jax.lax.stop_gradient(xq - x)

        def _bitlinear(x, w):
            return jnp.einsum('bsi,oi->bso', _act_quant(x), _weight_quant(w))
        gate = jax.nn.silu(_bitlinear(x, w_gate))
        up = _bitlinear(x, w_up)
        return _bitlinear(gate * up, w_down)

    def _L1_attn_ref(X, W_qkv, W_out):
        import jax, jax.numpy as jnp
        import numpy as np
        D_MODEL, D_QKV, N_HEADS = (256, 64, 16)
        b, s, _ = X.shape
        h, d = (N_HEADS, D_QKV)
        scale = d ** 0.5
        qkv = X @ W_qkv
        qkv = qkv.reshape(b, s, h, d, 3)
        q, k, v = (qkv[..., 0], qkv[..., 1], qkv[..., 2])
        scores = jnp.einsum('bqhd,bkhd->bhqk', q, k) / scale
        weights = jax.nn.softmax(scores, axis=-1)
        attn = jnp.einsum('bhqk,bkhd->bqhd', weights, v)
        return attn.reshape(b, s, h * d) @ W_out

    def _L1_xattn_ref(query, key, value, Wq, bq, Wk, bk, Wv, bv, Wo, bo):
        import jax, jax.numpy as jnp
        import numpy as np
        EMBED_DIM = 256
        NUM_HEADS = 16
        HEAD_DIM = EMBED_DIM // NUM_HEADS
        WINDOW = 128
        B, S_Q, S_K = (2, 512, 512)

        def apply_rope(x):
            Dh = x.shape[-1]
            half = Dh // 2
            pos = jnp.arange(x.shape[2], dtype=jnp.float32)
            inv_freq = 1.0 / 10000.0 ** (jnp.arange(0, half, dtype=jnp.float32) / half)
            ang = pos[:, None] * inv_freq[None, :]
            cos = jnp.cos(ang)[None, None, :, :].astype(x.dtype)
            sin = jnp.sin(ang)[None, None, :, :].astype(x.dtype)
            x1, x2 = (x[..., :half], x[..., half:])
            return jnp.concatenate([x1 * cos - x2 * sin, x1 * sin + x2 * cos], axis=-1)
        Bq, Sq, D = query.shape
        Sk = key.shape[1]
        H, Dh = (NUM_HEADS, HEAD_DIM)

        def proj(x, W, b):
            return (x @ W.T + b).reshape(x.shape[0], x.shape[1], H, Dh).transpose(0, 2, 1, 3)
        q = apply_rope(proj(query, Wq, bq))
        k = apply_rope(proj(key, Wk, bk))
        v = proj(value, Wv, bv)
        q = q * Dh ** (-0.5)
        scores = jnp.einsum('bhqd,bhkd->bhqk', q, k)
        q_idx = jnp.arange(Sq)[:, None]
        kv_idx = jnp.arange(Sk)[None, :]
        rel = kv_idx - q_idx
        mask = (rel > 0) | (rel < -WINDOW)
        mask4 = mask[None, None, :, :]
        neg = jnp.finfo(scores.dtype).min
        scores = jnp.where(mask4, neg, scores)
        probs = jax.nn.softmax(scores, axis=-1)
        all_masked = jnp.all(mask4, axis=-1, keepdims=True)
        probs = jnp.where(all_masked, jnp.zeros((), probs.dtype), probs)
        out = jnp.einsum('bhqk,bhkd->bhqd', probs, v)
        out = out.transpose(0, 2, 1, 3).reshape(Bq, Sq, D)
        return out @ Wo.T + bo

    def _L1_ffn_ref(x, router_W, router_b, W1, b1, W2, b2):
        import jax, jax.numpy as jnp
        import numpy as np
        D_MODEL = 256
        D_FF = 1024
        N_EXPERTS = 8
        INIT_SCALE = 0.1

        def _trunc_normal(key, shape, std):
            return std * jax.random.truncated_normal(key, -2.0, 2.0, shape, dtype=jnp.float32)
        logits = jnp.einsum('bsd,de->bse', x.astype(jnp.float32), router_W) + router_b
        probs = jax.nn.softmax(logits, axis=-1)
        top1 = jnp.argmax(probs, axis=-1)
        mask = jax.nn.one_hot(top1, N_EXPERTS, dtype=x.dtype)
        gates = mask * probs.astype(x.dtype)
        h = jax.nn.relu(jnp.einsum('bsd,edf->besf', x, W1) + b1[:, None, :])
        y = jnp.einsum('besf,efd->besd', h, W2) + b2[:, None, :]
        out = jnp.einsum('bse,besd->bsd', gates, y)
        return out
    x = x + _L0_attn_ref(_layernorm(x, axis=-1), L0_attn_q_w, L0_attn_q_b, L0_attn_k_w, L0_attn_k_b, L0_attn_v_w, L0_attn_v_b, L0_attn_pk_w, L0_attn_pk_b, L0_attn_pv_w, L0_attn_pv_b)
    x = x + _L0_xattn_ref(_layernorm(x, axis=-1), ctx_1024, mask_BxS2_bf1, mask_BxS2_bf1, L0_xattn_W_q, L0_xattn_W_kv, L0_xattn_W_c)
    x = x + _L0_ffn_ref(_layernorm(x, axis=-1), L0_ffn_w_gate, L0_ffn_w_up, L0_ffn_w_down)
    x = x + _L1_attn_ref(_layernorm(x, axis=-1), L1_attn_W_qkv, L1_attn_W_out)
    x = x + _L1_xattn_ref(_layernorm(x, axis=-1), ctx_1024, ctx_1024, L1_xattn_Wq, L1_xattn_bq, L1_xattn_Wk, L1_xattn_bk, L1_xattn_Wv, L1_xattn_bv, L1_xattn_Wo, L1_xattn_bo)
    x = x + _L1_ffn_ref(_layernorm(x, axis=-1), L1_ffn_router_W, L1_ffn_router_b, L1_ffn_W1, L1_ffn_b1, L1_ffn_W2, L1_ffn_b2)
    return x

_drawn_inputs = setup_inputs


def setup_inputs(seed=0):
    import zlib

    import numpy as np

    out = dict(_drawn_inputs(seed))
    spreads = {'L1_xattn_bq': (0.0, 0.502),
     'L1_xattn_bk': (0.0, 0.8),
     'L1_xattn_bv': (0.0, 0.1),
     'L1_xattn_bo': (0.0, 0.1),
     'L1_ffn_router_b': (0.0, 0.605),
     'L1_ffn_b1': (0.0, 0.8),
     'L1_ffn_b2': (0.0, 0.718)}
    factors = {'L0_attn_q_b': 4.732,
     'L0_attn_k_b': 64.0,
     'L0_attn_v_b': 3.064,
     'L0_attn_pk_w': 8.0,
     'L0_attn_pk_b': 54.676,
     'L0_attn_pv_w': 7.783,
     'L0_attn_pv_b': 30.383,
     'L1_ffn_router_W': 6.831,
     'L1_ffn_W1': 8.0,
     'L1_ffn_W2': 8.0}
    for name, (base, spread) in spreads.items():
        noise = np.random.default_rng([zlib.crc32(name.encode()), seed]).standard_normal(out[name].shape)
        drawn = base * np.exp(spread * noise) if base else spread * noise
        out[name] = jnp.asarray(drawn.astype(out[name].dtype))
    for name, factor in factors.items():
        out[name] = (out[name] * factor).astype(out[name].dtype)
    return out
```

```python
from contextlib import ExitStack

import numpy as np

import concourse.bass as bass
from concourse import mybir

F32 = mybir.dt.float32
BF16 = mybir.dt.bfloat16
I32 = mybir.dt.int32
U32 = mybir.dt.uint32
U8 = mybir.dt.uint8
ALU = mybir.AluOpType
ACT = mybir.ActivationFunctionType
AX = mybir.AxisListType

P = 128
B, T, C = 8, 512, 256
NT = T // P
KC = C // P
NX = B * NT
H = 16
EPS = 1e-5
MASKED = -1e9
NEG = -1e30


class Loop:

    def __init__(self, sem, per, before=0):
        self.sem, self.per, self.before = sem, per, before

    def credit(self, eng):
        if self.before:
            eng.wait_ge(self.sem, self.before)
        if self.per > self.before:
            eng.sem_inc(self.sem, self.per - self.before)

    def wait(self, eng, it, k):
        if it is not None:
            eng.wait_ge(self.sem, it * self.per + (self.per + k))
        elif k > 0:
            eng.wait_ge(self.sem, k)


class Space:

    def __init__(self, nc, ctx, name):
        self.nc, self.ctx, self.name, self.sems = nc, ctx, name, []

    def sb(self, name, shape, dt=F32):
        return self.ctx.enter_context(self.nc.sbuf_tensor(f"{self.name}_{name}", shape, dt))

    def ps(self, name, shape, dt=F32):
        return self.ctx.enter_context(self.nc.psum_tensor(f"{self.name}_{name}", shape, dt))

    def sem(self, name):
        self.sems.append(self.ctx.enter_context(self.nc.semaphore(f"{self.name}_{name}")))
        return self.sems[-1]

    def clear(self):
        with self.nc.Block() as block:
            @block.sync
            def _(sp):
                for sem in self.sems:
                    sp.sem_clear(sem)


def first_norm(nc, name, x_all, ident, h_tok, hT, tr):
    with ExitStack() as ctx:
        s = Space(nc, ctx, name + "_first")
        stats, mv, rstd = s.sb("stats", [P, NT, 6]), s.sb("mv", [P, NT, 2]), s.sb("rstd", [P, NT])
        half = s.sb("half", [P, NT])
        s_stats, s_mv, s_pool, s_h, s_tr, s_ev = (s.sem(n) for n in ("stats", "mv", "pool", "h", "tr", "ev"))
        with nc.Block() as block:
            @block.vector
            def _(dve):
                for i in range(NT):
                    dve.bn_stats(stats[:, i, :], x_all[:, i, :]).then_inc(s_stats, 1)
                dve.wait_ge(s_stats, NT)
                for i in range(NT):
                    dve.bn_aggr(mv[:, i, :], stats[:, i, :]).then_inc(s_mv, 1)
                dve.wait_ge(s_tr, 2)
                dve.tensor_copy(hT[:, 1, :], tr[:, 1, :]).then_inc(s_ev, 1)

            @block.gpsimd
            def _(pool):
                pool.memset(half[:, :], -0.5).then_inc(s_pool, 1)
                pool.wait_ge(s_mv, NT)
                pool.tensor_scalar(rstd[:, :], mv[:, :, 1], EPS, None, ALU.add).then_inc(s_pool, 1)
                pool.wait_ge(s_pool, 2)
                pool.tensor_tensor(rstd[:, :], rstd[:, :], half[:, :], ALU.pow).then_inc(s_pool, 1)
                pool.wait_ge(s_pool, 3)
                for i in range(NT):
                    pool.tensor_scalar(h_tok[:, i, :], x_all[:, i, :], mv[:, i, 0:1], rstd[:, i:i + 1],
                                       ALU.subtract, ALU.mult).then_inc(s_h, 1)

            @block.tensor
            def _(pe):
                pe.wait_ge(s_h, NT)
                for c in range(KC):
                    for i in range(NT):
                        t = pe.transpose(tr[:, c, i * P:(i + 1) * P], h_tok[:, i, c * P:(c + 1) * P], ident)
                    t.then_inc(s_tr, 1)

            @block.scalar
            def _(act):
                act.wait_ge(s_tr, 1)
                act.copy(hT[:, 0, :], tr[:, 0, :]).then_inc(s_ev, 1)
        s.clear()


def attention(nc, name, x_mem, consts, D, wq_d, wk_d, wv_d, wo_d, ctx_d=None, rope=None, bias_d=None,
              mask_d=None, window=False):
    G = P // D
    NC = H * D // P
    DP = max(D, 32)
    HG = P // DP
    NG = H // HG
    NU = H * NT
    ident, ident_bf = consts["ident"], consts["ident_bf"]
    scale = float(D) ** -0.5
    VW = min(512, H * D)
    VH = H * D // VW

    def keys(i):
        return (max(i - 1, 0) * P, P if i == 0 else 2 * P) if window else (0, T)

    T_LAG, PV_LAG, TURN_LAG = (3, 5, 11) if rope else (2, 4, 10)
    LAST_VALUE = NU + PV_LAG + NT - 2
    NV = NT * VH
    late = ctx_d is not None
    prep = {2: [("stat", 0)], 6: [("mask", 0), ("htok", 0)] if mask_d is not None else [("htok", 0)],
            13: [("norm", c) for c in range(KC)]}
    for n in range(2 * NC):
        if rope:
            prep.setdefault(16 + 2 * n, []).append(("qk", n))
            prep.setdefault(20 + 2 * n, []).append(("rot", n))
        else:
            prep.setdefault(max(14, NU // NC * (n // 2 + 1)) + 1 + 2 * (n % 2), []).append(("qk", n))
    if not late:
        for n in range(NV // 2):
            prep.setdefault(LAST_VALUE + 1 + n * (TURN_LAG + NU - LAST_VALUE - 1) // NV * 2, []).append(("v", n))

    def plan(which):
        steps = []
        for slot in range(NU + TURN_LAG):
            if which != "first":
                if slot < NU:
                    steps.append(("score", slot))
                if 0 <= slot - T_LAG < NU:
                    steps.append(("flip", slot - T_LAG))
                u = slot - PV_LAG - NT * HG + 1
                if 0 <= u < NU and u % (NT * HG) < NT:
                    steps.append(("value", u // (NT * HG) * NT + u % (NT * HG)))
                if late and 3 <= slot < 3 + NV:
                    steps.append(("v", slot - 3))
                if late and 3 + NV <= slot < 3 + NV + NC:
                    steps.append(("back", slot - 3 - NV))
                if late and 5 + NV + NC <= slot < 5 + NV + NC + NT:
                    steps.append(("out", slot - 5 - NV - NC))
            if which != "last":
                steps += prep.get(slot, [])
            u = slot - TURN_LAG + 1
            if which != "first" and 0 <= u < NU and u % (NT * HG) == NT * HG - 1:
                steps.append(("turn", u // (NT * HG)))
        own = not late and which != "first" or which == "last"
        if not late and which != "last":
            steps += [("v", n) for n in range(NV // 2, NV * 3 // 4)]
        steps += [("own_back", c) for c in range(NC)] if own else []
        if not late and which != "last":
            steps += [("v", n) for n in range(NV * 3 // 4, NV)]
        return steps + ([("own_out", i) for i in range(NT)] if own else [])

    SR, WR, OPR = 3, 4, 1
    PR = 4 if rope else 3

    def drained_by(kind, n):
        if kind == "qk":
            return "act" if rope or n % 2 == 0 else "dve"
        if kind in ("rot", "turn", "out", "own_out") or (kind == "v" and bias_d):
            return "dve"
        return "dve" if n % 2 else "act"

    def numbered(steps):
        ring = [st for st in steps if st[0] not in ("score", "value", "stat", "htok", "mask")]
        order = {e: [st for st in ring if drained_by(*st) == e] for e in ("act", "dve")}
        return {st: n for n, st in enumerate(ring)}, order, {st: order[e].index(st) + 1 for e in order for st in order[e]}

    class Plan:

        def __init__(self, which, prev=None):
            self.steps = plan(which)
            self.place, self.order, self.nth = numbered(self.steps)
            self.ring = sorted(self.place, key=self.place.get)
            self.prev = prev or self

    whole = Plan("loop")
    first, last = Plan("first", whole), Plan("last", whole)

    with ExitStack() as ctx:
        s = Space(nc, ctx, name)
        h_tok, hT = s.sb("h_tok", [P, NT, C]), s.sb("hT", [P, KC, T])
        wq, wk, wv = (s.sb(n, [P, KC, H * D]) for n in ("wq", "wk", "wv"))
        wo = s.sb("wo", [P, NC, C])
        if rope:
            qs, ks = s.sb("qs", [P, H, T], BF16), s.sb("ks", [P, H, T], BF16)
            parts = s.sb("parts", [P, 2 * NC, 3, T], BF16)
            parts_d = nc.dram_tensor(f"{name}_parts_dram", (2 * NC, 3, P, T), BF16, kind="Internal").ap()
        else:
            qm = s.sb("qm", [P, H, T])
            kT = s.sb("kT", [P, NC, T])
        V = s.sb("V", [P, NT, H, DP])
        Pr = s.sb("Pr", [P, PR, T])
        PTN = HG + (1 if rope else 2)
        PT = s.sb("PT", [P, PTN, NT * (2 * P if window else T)])
        nmax, sums, rinv = s.sb("nmax", [P, NU]), s.sb("sums", [P, NU]), s.sb("rinv", [P, NU])
        Oraw = s.sb("Oraw", [P, 2, T])
        O = s.sb("O", [P, NT, H * D])
        if late:
            OT = s.sb("OT", [P, NC, T])
        else:
            OT = PT[:, :, :].rearrange("p n k -> p (n k)")[:, 0:NC * T].rearrange("p (c t) -> p c t", t=T)
        stats, mv, rstd, half, eps = s.sb("stats", [P, NT, 6]), s.sb("mv", [P, NT, 2]), s.sb("rstd", [P, NT]), s.sb("half", [P, NT]), s.sb("eps", [P, NT])
        if ctx_d is not None:
            cT = s.sb("cT", [P, KC, T])
        if rope:
            cos, sin, turnm = s.sb("cos", [P, T]), s.sb("sin", [P, T]), s.sb("turnm", [P, P])
            rows, rsin = s.sb("rows", [P, 2 * NC, T]), s.sb("rsin", [P, 2 * NC, T])
        if bias_d:
            bqk, bv, bo = s.sb("bqk", [P, 2 * NC]), s.sb("bv", [P, C]), s.sb("bo", [P, C])
            bqs = s.sb("bqs", [P, NC])
            ysum = s.sb("ysum", [P, C])
        if mask_d is not None:
            m8, mrow, qrow, krow = s.sb("m8", [P, B, T], U8), s.sb("mrow", [P, T], BF16), s.sb("qrow", [1, T], BF16), s.sb("krow", [1, T], BF16)
        if window:
            band, band32 = s.sb("band", [P, 2 * P], BF16), s.sb("band32", [P, 2 * P])
        S = s.ps("S", [P, SR, 512])
        W = s.ps("W", [P, WR, 512])
        OP = s.ps("OP", [P, OPR, 512])

        s_load, s_set = s.sem("load"), s.sem("set")
        s_fix, s_cast, s_fence = s.sem("fix"), s.sem("cast"), s.sem("fence")
        s_fence_pool, s_fence_sp = s.sem("fence_pool"), s.sem("fence_sp")
        ring_full = Loop(s.sem("ring_full"), len(whole.place), len(first.place))
        drained = {e: Loop(s.sem("drained_" + e), len(whole.order[e]), len(first.order[e])) for e in ("act", "dve")}
        scored = Loop(s.sem("scored"), NU)
        maxed = Loop(s.sem("maxed"), NU)
        exped = Loop(s.sem("exped"), NU)
        valued = Loop(s.sem("valued"), NG)
        lifted = Loop(s.sem("lifted"), NG)
        inverted = Loop(s.sem("inverted"), NG)
        normed = Loop(s.sem("normed"), NT, NT)
        s_stat = Loop(s.sem("stat"), 2 * NT, 2 * NT)
        rooted = Loop(s.sem("rooted"), 2, 2)
        kv_read = Loop(s.sem("kv_read"), 2 if late else 1, 1)
        s_ctx = Loop(s.sem("ctx"), 16, 16)
        masked = Loop(s.sem("masked"), 3, 3)
        biased = Loop(s.sem("biased"), NT)
        if rope:
            pool_ops = [(n, o) for n in range(2 * NC) for o in ("cos", "add", "mask", "high", "rest", "middle", "low")
                        if o != "mask" or (mask_d is not None and n % 2 == 0)]
            nth_pool = {op: n + 1 for n, op in enumerate(pool_ops)}
            pooled = Loop(s.sem("pooled"), len(pool_ops), len(pool_ops))
            spilled = Loop(s.sem("spilled"), 16 * 2 * NC, 16 * 2 * NC)
            NL = 12 + (2 if mask_d is not None else 0)
            stacked = [Loop(s.sem(f"stacked{c}"), 16 * NL, 16 * NL) for c in range(NC)]
            KS = 6 * D + (1 if mask_d is not None else 0)

        with nc.Block() as block:
            @block.sync
            def _(sp):
                sp.dma_start(wq[:, :, :], wq_d.rearrange("(k p) n -> p k n", p=P)).then_inc(s_load, 16)
                sp.dma_start(wk[:, :, :], wk_d.rearrange("(k p) n -> p k n", p=P)).then_inc(s_load, 16)
                sp.dma_start(wv[:, :, :], wv_d.rearrange("(k p) n -> p k n", p=P)).then_inc(s_load, 16)
                sp.dma_start(wo[:, :, :], wo_d.rearrange("(k p) n -> p k n", p=P)).then_inc(s_load, 16)
                if rope:
                    for t, d in zip((cos, sin, turnm), rope):
                        sp.dma_start(t[:, :], d).then_inc(s_load, 16)
                if bias_d:
                    for n, d in enumerate(bias_d[:2]):
                        for c in range(NC):
                            sp.dma_start(bqk[:, n * NC + c:n * NC + c + 1], d[c * P:(c + 1) * P].unsqueeze(1)).then_inc(s_load, 16)
                    sp.dma_start(bv[:, :], bias_d[2].unsqueeze(0).partition_broadcast(P)).then_inc(s_load, 16)
                    sp.dma_start(bo[:, :], bias_d[3].unsqueeze(0).partition_broadcast(P)).then_inc(s_load, 16)
                if window:
                    sp.dma_start(band32[:, :], consts["band_d"]).then_inc(s_load, 16)
                total = 4 + (3 if rope else 0) + (2 * NC + 2 if bias_d else 0) + (1 if window else 0)
                sp.wait_ge(s_load, 16 * total)
                if mask_d is not None:
                    sp.dma_start(m8[:, 0:B, :], mask_d.unsqueeze(0).partition_broadcast(P)).then_inc(s_load, 16)
                    sp.wait_ge(s_load, 16 * (total + 1))

            @block.vector
            def _(dve):
                dve.memset(half[:, :], -0.5).then_inc(s_set, 1)
                dve.memset(eps[:, :], EPS).then_inc(s_set, 1)
                if late:
                    dve.memset(O[:, :, :], 0.0).then_inc(s_set, 1)
                if DP != D:
                    dve.memset(V[:, :, :, D:DP], 0.0).then_inc(s_set, 1)
                if not rope:
                    for h in range(H):
                        other = (1 - h % 2) * D
                        dve.memset(qm[other:other + D, h, :], 0.0).then_inc(s_set, 1)

        if window:
            with nc.Block() as block:
                @block.vector
                def _(dve):
                    dve.tensor_copy(band[:, :], band32[:, :]).then_inc(s_cast, 1)
                    dve.wait_ge(s_cast, 1)

        if bias_d:
            with nc.Block() as block:
                @block.vector
                def _(dve):
                    dve.tensor_scalar(bqs[:, :], bqk[:, 0:NC], scale, None, ALU.mult).then_inc(s_fix, 1)
                    dve.wait_ge(s_fix, 1)

        src = cT if ctx_d is not None else hT

        def flip_copy(copy, b, n, src_, eng):
            h, i = n // NT, n % NT
            valued.wait(eng, b, (h - PTN) // HG + 1)
            if window:
                _, kn = keys(i)
                a = 2 * P * i - (kn - P)
                return copy(PT[:, h % PTN, a:a + kn], src_[:, 0:kn])
            o = PT[:, h % PTN, :].rearrange("p (k q) -> p k q", q=T)[:, :, i * P:(i + 1) * P]
            return copy(o, src_.rearrange("p (k q) -> p k q", q=P))

        def next_x(b, i):
            if b is None:
                return x_mem[:, NT + i, :]
            return x_mem[:, bass.ds(b * NT + (2 * NT + i), 1), :].rearrange("p a c -> p (a c)")

        def tensor_steps(pe, b, plan):
            place, order, nth, prev = plan.place, plan.order, plan.nth, plan.prev

            def bank(st):
                n = place[st]
                if n >= WR:
                    before = plan.ring[n - WR]
                    e = drained_by(*before)
                    drained[e].wait(pe, b, nth[before])
                else:
                    before = [st for m, st in enumerate(prev.ring) if m % WR == n][-1]
                    e = drained_by(*before)
                    drained[e].wait(pe, b, prev.nth[before] - drained[e].per)
                return W[:, n % WR, :]

            for kind, n in plan.steps:
                if kind == "norm":
                    dst = bank((kind, n))
                    normed.wait(pe, b, NT)
                    for i in range(NT):
                        m = pe.transpose(dst[:, i * P:(i + 1) * P], h_tok[:, i, n * P:(n + 1) * P], ident)
                    m.then_inc(ring_full.sem, 1)
                elif kind == "qk":
                    which, c = n % 2, n // 2
                    if n == 0:
                        for k in range(KC):
                            drained[drained_by("norm", k)].wait(pe, b, nth[("norm", k)])
                    if n == 1 and ctx_d is not None:
                        s_ctx.wait(pe, b, 16)
                    w, rhs = (wq, hT) if which == 0 else (wk, src)
                    dst = bank((kind, n))
                    for kc in range(KC):
                        m = pe.matmul(dst, w[:, kc, c * P:(c + 1) * P], rhs[:, kc, :],
                                      start=(kc == 0), stop=(kc == KC - 1))
                    m.then_inc(ring_full.sem, 1)
                    if late and n == 2 * NC - 1:
                        pe.drain().then_inc(kv_read.sem, 1)
                elif kind == "v":
                    i, v = n // VH, n % VH
                    dst = bank((kind, n))
                    for kc in range(KC):
                        m = pe.matmul(dst[:, 0:VW], src[:, kc, i * P:(i + 1) * P], wv[:, kc, v * VW:(v + 1) * VW],
                                      start=(kc == 0), stop=(kc == KC - 1))
                    m.then_inc(ring_full.sem, 1)
                    if n == NV - 1:
                        pe.drain().then_inc(kv_read.sem, 1)
                elif kind == "rot":
                    dst = bank((kind, n))
                    drained["act"].wait(pe, b, nth[("qk", n)])
                    pe.matmul(dst, turnm[:, :], rows[:, n, :], start=True, stop=True).then_inc(ring_full.sem, 1)
                elif kind == "score":
                    h, i = n // NT, n % NT
                    c = h // G
                    k0, kn = keys(i)
                    if n == c * G * NT:
                        if rope:
                            stacked[c].wait(pe, b, 0)
                        else:
                            for st in (("qk", 2 * c), ("qk", 2 * c + 1)):
                                e = drained_by(*st)
                                drained[e].wait(pe, b, prev.nth[st] - drained[e].per)
                    exped.wait(pe, b, n + 1 - SR)
                    if rope:
                        m = pe.matmul(S[:, n % SR, 0:kn], qs[0:KS, h, i * P:(i + 1) * P], ks[0:KS, h, k0:k0 + kn],
                                      start=True, stop=not window)
                    else:
                        m = pe.matmul(S[:, n % SR, 0:kn], qm[:, h, i * P:(i + 1) * P], kT[:, c, k0:k0 + kn],
                                      start=True, stop=not window)
                    if window:
                        m = pe.matmul(S[:, n % SR, 0:kn], ident_bf, band[:, 2 * P - kn:2 * P], start=False, stop=True)
                    m.then_inc(scored.sem, 1)
                elif kind == "flip":
                    _, kn = keys(n % NT)
                    dst = bank((kind, n))
                    exped.wait(pe, b, n + 1)
                    for k in range(kn // P):
                        m = pe.transpose(dst[:, k * P:(k + 1) * P], Pr[:, n % PR, k * P:(k + 1) * P], ident)
                    m.then_inc(ring_full.sem, 1)
                elif kind == "value":
                    g, nk = n // NT, n % NT
                    k = (0, 2, 1, 3)[nk] if window else nk
                    if n == 0 and not late:
                        for e in order:
                            v_last = max(prev.nth[st] for st in prev.order[e] if st[0] == "v")
                            drained[e].wait(pe, b, v_last - drained[e].per)
                    if nk == 0:
                        last = NT * HG * (g + 1) - 1
                        for u in (last - 1, last):
                            e = drained_by("flip", u)
                            drained[e].wait(pe, b, nth[("flip", u)])
                        lifted.wait(pe, b, g + 1 - OPR)
                    q0, qn = (k * P, min(2 * P, T - k * P)) if window else (0, T)
                    p0 = k * (2 * P) if window else k * T
                    for j in range(HG):
                        h = g * HG + j
                        m = pe.matmul(OP[DP * j:DP * (j + 1), g % OPR, q0:q0 + qn], V[:, k, h, :],
                                      PT[:, h % PTN, p0:p0 + qn], start=(nk == 0), stop=(nk == NT - 1),
                                      skip_group_check=True)
                    if nk == NT - 1:
                        m.then_inc(valued.sem, 1)
                elif kind == "turn":
                    dst = bank((kind, n))
                    lifted.wait(pe, b, n + 1)
                    for i in range(NT):
                        m = pe.transpose(dst[:, i * P:(i + 1) * P], Oraw[:, n % 2, i * P:(i + 1) * P], ident)
                    m.then_inc(ring_full.sem, 1)
                elif kind in ("back", "own_back"):
                    dst = bank((kind, n))
                    if kind == "back":
                        drained["dve"].wait(pe, b, prev.nth[("turn", NG - 1)] - drained["dve"].per)
                    else:
                        drained["dve"].wait(pe, b, nth[("turn", NG - 1)])
                    for i in range(NT):
                        m = pe.transpose(dst[:, i * P:(i + 1) * P], O[:, i, n * P:(n + 1) * P], ident)
                    m.then_inc(ring_full.sem, 1)
                elif kind in ("out", "own_out"):
                    dst = bank((kind, n))
                    if n == 0:
                        for e in order:
                            backs = [nth[st] for st in order[e] if st[0] == kind.replace("out", "back")]
                            drained[e].wait(pe, b, max(backs))
                    for c in range(NC):
                        m = pe.matmul(dst[:, 0:C], OT[:, c, n * P:(n + 1) * P], wo[:, c, :],
                                      start=(c == 0), stop=(c == NC - 1))
                    m.then_inc(ring_full.sem, 1)

        def scalar_steps(act, b, plan):
            place, order, nth, prev = plan.place, plan.order, plan.nth, plan.prev
            for kind, n in plan.steps:
                st = (kind, n)
                if kind == "score":
                    _, kn = keys(n % NT)
                    maxed.wait(act, b, n + 1)
                    f = ("flip", n - PR if n >= PR else NU + n - PR)
                    ring_full.wait(act, b, place[f] + 1 if n >= PR else prev.place[f] + 1 - ring_full.per)
                    act.activation(Pr[:, n % PR, 0:kn], S[:, n % SR, 0:kn], ACT.Exp, bias=nmax[:, n:n + 1],
                                   accum_out=sums[:, n:n + 1]).then_inc(exped.sem, 1)
                    continue
                if kind == "value":
                    g = n // NT
                    if n % NT == NT - 1:
                        valued.wait(act, b, g + 1)
                        if g < 2:
                            ring_full.wait(act, b, prev.place[("turn", NG + g - 2)] + 1 - ring_full.per)
                        else:
                            ring_full.wait(act, b, place[("turn", g - 2)] + 1)
                        act.copy(Oraw[:, g % 2, :], OP[:, g % OPR, :]).then_inc(lifted.sem, 1)
                    continue
                if st not in place or drained_by(*st) != "act":
                    continue
                ring_full.wait(act, b, place[st] + 1)
                src_ = W[:, place[st] % WR, :]
                done = drained["act"].sem
                if kind == "qk" and rope:
                    which, c = n % 2, n // 2
                    if bias_d:
                        bias = bqs[:, c:c + 1] if which == 0 else bqk[:, NC + c:NC + c + 1]
                    else:
                        bias = 0.0
                    pooled.wait(act, b, nth_pool[(n, "low")] - pooled.per)
                    act.activation(rows[:, n, :], src_, ACT.Identity, bias=bias,
                                   scale=scale if which == 0 else 1.0).then_inc(done, 1)
                elif kind == "qk":
                    c = n // 2
                    act.activation(qm[0:D, 2 * c, :], src_[0:D, :], ACT.Identity, scale=scale)
                    act.activation(qm[D:P, 2 * c + 1, :], src_[D:P, :], ACT.Identity, scale=scale).then_inc(done, 1)
                elif kind == "v":
                    i, v = n // VH, n % VH
                    hs = VW // D
                    o = V[:, i, v * hs:(v + 1) * hs, 0:D]
                    act.copy(o, src_[:, 0:VW].rearrange("p (h d) -> p h d", d=D)).then_inc(done, 1)
                elif kind == "flip":
                    flip_copy(act.copy, b, n, src_, act).then_inc(done, 1)
                elif kind == "norm":
                    act.copy(hT[:, n, :], src_).then_inc(done, 1)
                elif kind in ("back", "own_back"):
                    act.copy(OT[:, n, :], src_).then_inc(done, 1)

        def vector_steps(dve, b, plan):
            place, order, nth, prev = plan.place, plan.order, plan.nth, plan.prev
            for kind, n in plan.steps:
                st = (kind, n)
                if kind == "score":
                    _, kn = keys(n % NT)
                    scored.wait(dve, b, n + 1)
                    dve.tensor_reduce(nmax[:, n:n + 1], S[:, n % SR, 0:kn], AX.X, ALU.max, negate=True).then_inc(maxed.sem, 1)
                elif kind == "stat":
                    for i in range(NT):
                        dve.bn_stats(stats[:, i, :], next_x(b, i)).then_inc(s_stat.sem, 1)
                    s_stat.wait(dve, b, NT)
                    dve.sem_inc(s_fence, 1)
                    for i in range(NT):
                        dve.bn_aggr(mv[:, i, :], stats[:, i, :]).then_inc(s_stat.sem, 1)
                elif kind == "mask":
                    pooled.wait(dve, b, nth_pool[(2 * NC - 2, "mask")] - pooled.per)
                    m = m8[:, 0, :] if b is None else m8[:, bass.ds(b + 1, 1), :].rearrange("p a t -> p (a t)")
                    dve.tensor_copy(mrow[:, :], m).then_inc(masked.sem, 1)
                    masked.wait(dve, b, 1)
                    for c in range(NC):
                        stacked[c].wait(dve, b, 0)
                    dve.tensor_copy(qrow[0:1, :], mrow[0:1, :]).then_inc(masked.sem, 1)
                    dve.tensor_scalar(krow[0:1, :], mrow[0:1, :], -MASKED, MASKED, ALU.mult, ALU.add).then_inc(masked.sem, 1)
                elif kind == "htok":
                    rooted.wait(dve, b, 2)
                    for c in range(KC):
                        ring_full.wait(dve, b, prev.place[("norm", c)] + 1 - ring_full.per)
                    for i in range(NT):
                        dve.tensor_scalar(h_tok[:, i, :], next_x(b, i), mv[:, i, 0:1], rstd[:, i:i + 1],
                                          ALU.subtract, ALU.mult).then_inc(normed.sem, 1)
                if st not in place or drained_by(*st) != "dve":
                    continue
                ring_full.wait(dve, b, place[st] + 1)
                src_ = W[:, place[st] % WR, :]
                done = drained["dve"].sem
                if kind == "qk":
                    dve.tensor_copy(kT[:, n // 2, :], src_).then_inc(done, 1)
                elif kind == "v":
                    i, v = n // VH, n % VH
                    hs = VW // D
                    o = V[:, i, v * hs:(v + 1) * hs, 0:D]
                    if bias_d:
                        dve.tensor_tensor(o, src_[:, 0:VW].rearrange("p (h d) -> p h d", d=D),
                                          bv[:, :].rearrange("p (h d) -> p h d", d=D), ALU.add).then_inc(done, 1)
                    else:
                        dve.tensor_copy(o, src_[:, 0:VW].rearrange("p (h d) -> p h d", d=D)).then_inc(done, 1)
                elif kind == "rot":
                    pooled.wait(dve, b, nth_pool[(n, "add")] - pooled.per)
                    dve.tensor_tensor(rsin[:, n, :], src_, sin[:, :], ALU.mult).then_inc(done, 1)
                elif kind == "flip":
                    flip_copy(dve.tensor_copy, b, n, src_, dve).then_inc(done, 1)
                elif kind == "turn":
                    u0, nu = n * HG * NT, HG * NT
                    exped.wait(dve, b, u0 + nu)
                    dve.reciprocal(rinv[:, u0:u0 + nu], sums[:, u0:u0 + nu]).then_inc(inverted.sem, 1)
                    inverted.wait(dve, b, n + 1)
                    r = rinv[:, u0:u0 + nu].rearrange("p (h i) -> p i h", i=NT)
                    for j in range(HG):
                        last = dve.tensor_tensor(
                            O[:, :, (n * HG + j) * D:(n * HG + j + 1) * D],
                            src_.rearrange("p (i h d) -> p i h d", i=NT, d=DP)[:, :, j, 0:D],
                            r[:, :, j:j + 1].to_broadcast([P, NT, D]), ALU.mult)
                    last.then_inc(done, 1)
                elif kind == "norm":
                    dve.tensor_copy(hT[:, n, :], src_).then_inc(done, 1)
                elif kind in ("back", "own_back"):
                    dve.tensor_copy(OT[:, n, :], src_).then_inc(done, 1)
                elif kind in ("out", "own_out"):
                    tile = b * NT + (n if kind == "out" else NT + n)
                    xt = x_mem[:, bass.ds(tile, 1), :].rearrange("p a c -> p (a c)")
                    if bias_d:
                        dve.tensor_tensor(ysum[:, :], src_[:, 0:C], bo[:, :], ALU.add).then_inc(biased.sem, 1)
                        biased.wait(dve, b, n + 1 + (NT if kind == "own_out" else 0))
                        dve.tensor_tensor(xt, ysum[:, :], xt, ALU.add).then_inc(done, 1)
                        drained["dve"].wait(dve, b, nth[st])
                    else:
                        dve.tensor_tensor(xt, src_[:, 0:C], xt, ALU.add).then_inc(done, 1)

        def gpsimd_steps(pool, b, plan):
            nth = plan.nth
            s_stat.wait(pool, b, 2 * NT)
            pool.tensor_tensor(rstd[:, :], mv[:, :, 1], eps[:, :], ALU.add).then_inc(rooted.sem, 1)
            rooted.wait(pool, b, 1)
            pool.tensor_tensor(rstd[:, :], rstd[:, :], half[:, :], ALU.pow).then_inc(rooted.sem, 1)
            for k, (n, o) in enumerate(pool_ops if rope else ()):
                high, middle, low = (parts[:, n, e, :] for e in range(3))
                row = rows[:, n, :]
                pooled.wait(pool, b, k)
                if o == "cos":
                    drained["dve"].wait(pool, b, nth[("rot", n)])
                    ins = pool.tensor_tensor(row, row, cos[:, :], ALU.mult)
                elif o == "add":
                    ins = pool.tensor_tensor(row, row, rsin[:, n, :], ALU.add)
                elif o == "mask":
                    masked.wait(pool, b, 1)
                    ins = pool.tensor_tensor(row, row, mrow[:, :], ALU.mult)
                elif o == "high":
                    spilled.wait(pool, b, 16 * (n + 1) - spilled.per)
                    pool.sem_inc(s_fence_pool, 1)
                    ins = pool.tensor_copy(high, row)
                elif o == "rest":
                    ins = pool.tensor_tensor(row, row, high, ALU.subtract)
                elif o == "middle":
                    pool.sem_inc(s_fence_pool, 1)
                    ins = pool.tensor_copy(middle, row)
                else:
                    ins = pool.tensor_tensor(low, row, middle, ALU.subtract)
                ins.then_inc(pooled.sem, 1)

        def sync_steps(sp, b):
            def wait(loop, k):
                loop.wait(sp, b, k)
                sp.sem_inc(s_fence_sp, 1)

            if b is not None:
                wait(kv_read, 1)
            sp.dma_start(cT[:, :, :], context(0 if b is None else b + 1)).then_inc(s_ctx.sem, 16)
            for c in range(NC):
                wait(stacked[c], 0)
                for n in (2 * c, 2 * c + 1):
                    wait(pooled, nth_pool[(n, "low")])
                    sp.dma_start(parts_d[n].rearrange("e p t -> p e t"), parts[:, n, :, :]).then_inc(spilled.sem, 16)
                wait(spilled, 32 * (c + 1))
                if b is not None:
                    wait(scored, (c + 1) * G * NT)
                heads = slice(c * G, (c + 1) * G)
                for which, (stack, terms) in enumerate(((qs, (0, 0, 0, 1, 1, 2)), (ks, (0, 1, 2, 0, 1, 0)))):
                    for j, e in enumerate(terms):
                        sp.dma_start(stack[j * D:(j + 1) * D, heads, :],
                                     parts_d[2 * c + which, e].rearrange("(h d) t -> d h t", d=D)).then_inc(stacked[c].sem, 16)
                if mask_d is not None:
                    wait(masked, 3)
                    for stack, row in ((qs, qrow), (ks, krow)):
                        sp.dma_start(stack[6 * D:6 * D + 1, heads, :],
                                     row[0:1, :].unsqueeze(1).to_broadcast([1, G, T])).then_inc(stacked[c].sem, 16)

        def context(b):
            return ctx_d[b].rearrange("(k p) t -> p k t", p=P) if isinstance(b, int) else \
                ctx_d[bass.ds(b, 1), :, :].rearrange("a (k p) t -> p (a k) t", p=P)

        with nc.Block() as block:
            @block.tensor
            def _(pe):
                tensor_steps(pe, None, first)
                for sem in (ring_full, kv_read, scored, valued):
                    sem.credit(pe)

            @block.scalar
            def _(act):
                scalar_steps(act, None, first)
                for sem in (drained["act"], exped, lifted):
                    sem.credit(act)

            @block.vector
            def _(dve):
                vector_steps(dve, None, first)
                for sem in (drained["dve"], s_stat, normed, maxed, inverted, biased) + ((masked,) if mask_d is not None else ()):
                    sem.credit(dve)

            @block.gpsimd
            def _(pool):
                gpsimd_steps(pool, None, first)
                for sem in (rooted,) + ((pooled,) if rope else ()):
                    sem.credit(pool)

            if rope:
                @block.sync
                def _(sp):
                    sync_steps(sp, None)
                    for sem in (s_ctx, spilled, *stacked):
                        sem.credit(sp)

        with nc.Block() as block:
            @block.tensor
            def _(pe):
                with pe.Fori(0, B - 1) as b:
                    tensor_steps(pe, b, whole)
                tensor_steps(pe, B - 1, last)

            @block.scalar
            def _(act):
                with act.Fori(0, B - 1) as b:
                    scalar_steps(act, b, whole)
                scalar_steps(act, B - 1, last)

            @block.vector
            def _(dve):
                with dve.Fori(0, B - 1) as b:
                    vector_steps(dve, b, whole)
                vector_steps(dve, B - 1, last)

            @block.gpsimd
            def _(pool):
                with pool.Fori(0, B - 1) as b:
                    gpsimd_steps(pool, b, whole)

            if rope:
                @block.sync
                def _(sp):
                    with sp.Fori(0, B - 1) as b:
                        sync_steps(sp, b)
        s.clear()




class Ring:

    def __init__(self, s, tensor, banks, steps, drained_by):
        self.tensor, self.banks, self.steps = tensor, banks, steps
        self.who = [drained_by(*st) for st in steps]
        self.place = {st: n for n, st in enumerate(steps)}
        self.engines = sorted(set(self.who))
        self.nth, seen = {}, {e: 0 for e in self.engines}
        for st, e in zip(steps, self.who):
            seen[e] += 1
            self.nth[st] = seen[e]
        self.full = Loop(s.sem("ring_full"), len(steps))
        self.drained = {e: Loop(s.sem("drained_" + e), seen[e]) for e in self.engines}

    def engine(self, st):
        return self.who[self.place[st]]

    def bank(self, st):
        return self.tensor[:, self.place[st] % self.banks, :]

    def free_bank(self, pe, it, st):
        n = self.place[st]
        if n >= self.banks:
            self.wait_drained(pe, it, self.steps[n - self.banks])
        else:
            last = max(m for m in range(len(self.steps)) if m % self.banks == n)
            self.wait_drained(pe, it, self.steps[last], -1)
        return self.bank(st)

    def wait_full(self, eng, it, st, iterations=0):
        self.full.wait(eng, it, self.place[st] + 1 + iterations * self.full.per)

    def wait_drained(self, eng, it, st, iterations=0):
        d = self.drained[self.engine(st)]
        d.wait(eng, it, self.nth[st] + iterations * d.per)


LOOKBACK, TOPK, PHRASE = 64, 16, 32
BAND = LOOKBACK + P
GONE = -3e38


def band_attention(nc, x_all, consts, a):
    ident = consts["ident"]
    scale = float(C) ** -0.5
    qkp = [("proj", n) for n in range(3 * KC)]
    order = qkp + [("score", i) for i in range(NT)] + [("v", i) for i in range(NT)]
    order += [("norm", c) for c in range(KC)]
    order += [st for i in range(NT) for st in (("flip", i), ("out", i))]
    ring_steps = [st for st in order if st[0] != "score"]

    def drained_by(kind, n):
        return "act" if kind in ("proj", "flip") or (kind == "norm" and n == 0) else "dve"

    with ExitStack() as ctx:
        s = Space(nc, ctx, "band")
        w3 = s.sb("w3", [P, KC, 3 * C])
        wvv = s.sb("wvv", [P, KC, 2 * C])
        b3, b3s, bvv = s.sb("b3", [P, 3 * KC]), s.sb("b3s", [P, KC]), s.sb("bvv", [P, 2 * C])
        h_tok, hT = s.sb("h_tok", [P, NT, C]), s.sb("hT", [P, KC, T])
        qT = s.sb("qT", [P, KC, T])
        kk = s.sb("kk", [P, KC, 2, LOOKBACK + T])
        vv = s.sb("vv", [P, NT, 2 * C])
        bias, shift, phrase = s.sb("bias", [P, 2, BAND]), s.sb("shift", [P, BAND]), s.sb("phrase", [P, BAND])
        phraseT = s.sb("phraseT", [P, 2, P])
        after_first = s.sb("after_first", [P, 1])
        junk = s.sb("junk", [P, 2, BAND])
        Sm, taken8, taken16 = s.sb("Sm", [P, NT, BAND]), s.sb("taken8", [P, BAND]), s.sb("taken16", [P, NT, BAND])
        best8, next8 = s.sb("best8", [P, NT, 8]), s.sb("next8", [P, NT, 8])
        pair, epair, nmax = s.sb("pair", [P, NT, 2]), s.sb("epair", [P, NT, 2]), s.sb("nmax", [P, NT])
        E = s.sb("E", [P, NT, BAND])
        Wt = s.sb("Wt", [P, NT, 2 * P])
        WT = s.sb("WT", [P, 2, 2 * P])
        sumb, total, rinv, wphr = s.sb("sumb", [P, NT]), s.sb("total", [P, NT]), s.sb("rinv", [P, NT]), s.sb("wphr", [P, NT])
        stats, mv, rstd = s.sb("stats", [P, NT, 6]), s.sb("mv", [P, NT, 2]), s.sb("rstd", [P, NT])
        half, eps = s.sb("half", [P, NT]), s.sb("eps", [P, NT])
        S = s.ps("S", [P, NT, 512])
        W = s.ps("W", [P, 4, 512])

        s_load, s_set, s_fence = s.sem("load"), s.sem("set"), s.sem("fence")
        ring = Ring(s, W, 4, ring_steps, drained_by)
        scored = Loop(s.sem("scored"), NT)
        ready = Loop(s.sem("ready"), NT)
        exped = Loop(s.sem("exped"), 2 * NT)
        weighted = Loop(s.sem("weighted"), NT)
        s_stat = Loop(s.sem("stat"), 2 * NT)
        rooted, normed = Loop(s.sem("rooted"), 2), Loop(s.sem("normed"), NT)
        stepped = Loop(s.sem("stepped"), NT * 13 + 1)

        with nc.Block() as block:
            @block.sync
            def _(sp):
                loads = [(w3[:, :, n * C:(n + 1) * C], a[f"L0_attn_{w}_wT"].rearrange("(k p) n -> p k n", p=P))
                         for n, w in enumerate(("q", "k", "pk"))]
                loads += [(wvv[:, :, n * C:(n + 1) * C], a[f"L0_attn_{w}_wT"].rearrange("(k p) n -> p k n", p=P))
                          for n, w in enumerate(("v", "pv"))]
                loads += [(b3[:, n * KC + c:n * KC + c + 1], a[f"L0_attn_{w}_b"][c * P:(c + 1) * P].unsqueeze(1))
                          for n, w in enumerate(("q", "k", "pk")) for c in range(KC)]
                loads += [(bvv[:, n * C:(n + 1) * C], a[f"L0_attn_{w}_b"].unsqueeze(0).partition_broadcast(P))
                          for n, w in enumerate(("v", "pv"))]
                loads += [(bias[:, :, :], a["band_bias"]), (shift[:, :], a["band_shift"]), (phrase[:, :], a["phrase"]),
                          (phraseT[:, :, :], a["phrase_T"]), (after_first[:, :], a["after_first"])]
                for dst, src in loads:
                    sp.dma_start(dst, src).then_inc(s_load, 16)
                sp.wait_ge(s_load, 16 * len(loads))

            @block.vector
            def _(dve):
                dve.memset(half[:, :], -0.5).then_inc(s_set, 1)
                dve.memset(eps[:, :], EPS).then_inc(s_set, 1)
                dve.memset(kk[:, :, :, 0:LOOKBACK], 0.0).then_inc(s_set, 1)
                dve.memset(Wt[:, :, 0:P - LOOKBACK], 0.0).then_inc(s_set, 1)

        with nc.Block() as block:
            @block.vector
            def _(dve):
                dve.tensor_scalar(b3s[:, :], b3[:, 0:KC], scale, None, ALU.mult).then_inc(s_set, 1)
                dve.wait_ge(s_set, 5)

        first_norm(nc, "band", x_all, ident, h_tok, hT, W)

        with nc.Block() as block:
            @block.tensor
            def _(pe):
                for sem in (ring.full, scored):
                    sem.credit(pe)
                with pe.Fori(0, B) as b:
                    for kind, n in order:
                        if kind == "proj":
                            if n == 0:
                                for c in range(KC):
                                    ring.wait_drained(pe, b, ("norm", c), -1)
                            dst = ring.free_bank(pe, b, (kind, n))
                            for c in range(KC):
                                m = pe.matmul(dst, w3[:, c, n * P:(n + 1) * P], hT[:, c, :], start=(c == 0), stop=(c == KC - 1))
                            m.then_inc(ring.full.sem, 1)
                        elif kind == "v":
                            dst = ring.free_bank(pe, b, (kind, n))
                            for c in range(KC):
                                m = pe.matmul(dst, hT[:, c, n * P:(n + 1) * P], wvv[:, c, :], start=(c == 0), stop=(c == KC - 1))
                            m.then_inc(ring.full.sem, 1)
                        elif kind == "score":
                            if n == 0:
                                ring.wait_drained(pe, b, qkp[-1])
                            ready.wait(pe, b, n + 1 - NT)
                            for c in range(KC):
                                m = pe.matmul(S[:, n, 0:2 * BAND].rearrange("p (t k) -> p t k", t=2), qT[:, c, n * P:(n + 1) * P],
                                              kk[:, c, :, n * P:n * P + BAND], start=(c == 0), stop=(c == KC - 1))
                            m.then_inc(scored.sem, 1)
                        elif kind == "norm":
                            dst = ring.free_bank(pe, b, (kind, n))
                            normed.wait(pe, b, NT)
                            for i in range(NT):
                                m = pe.transpose(dst[:, i * P:(i + 1) * P], h_tok[:, i, n * P:(n + 1) * P], ident)
                            m.then_inc(ring.full.sem, 1)
                        elif kind == "flip":
                            dst = ring.free_bank(pe, b, (kind, n))
                            weighted.wait(pe, b, n + 1)
                            for k in range(0 if n else 1, 2):
                                m = pe.transpose(dst[:, k * P:(k + 1) * P], Wt[:, n, k * P:(k + 1) * P], ident)
                            m.then_inc(ring.full.sem, 1)
                        elif kind == "out":
                            dst = ring.free_bank(pe, b, (kind, n))
                            ring.wait_drained(pe, b, ("flip", n))
                            if n == 0:
                                ring.wait_drained(pe, b, ("v", NT - 1))
                            first = 0 if n else 1
                            for k in range(first, 2):
                                pe.matmul(dst[:, 0:C], WT[:, n % 2, k * P:(k + 1) * P], vv[:, n - 1 + k, 0:C],
                                          start=(k == first), stop=(k == 1))
                            for k in range(first, 2):
                                m = pe.matmul(dst[:, C:2 * C], phraseT[:, k, :], vv[:, n - 1 + k, C:2 * C],
                                              start=(k == first), stop=(k == 1))
                            m.then_inc(ring.full.sem, 1)

            @block.scalar
            def _(act):
                for sem in (ring.drained["act"], exped):
                    sem.credit(act)
                with act.Fori(0, B) as b:
                    for st in order:
                        kind, n = st
                        if kind == "score" or ring.engine(st) != "act":
                            continue
                        if kind == "flip":
                            ready.wait(act, b, n + 1)
                            act.activation(E[:, n, :], Sm[:, n, :], ACT.Exp, bias=nmax[:, n:n + 1]).then_inc(exped.sem, 1)
                            act.activation(epair[:, n, :], pair[:, n, :], ACT.Exp, bias=nmax[:, n:n + 1]).then_inc(exped.sem, 1)
                        ring.wait_full(act, b, st)
                        src, done = ring.bank(st), ring.drained["act"].sem
                        if kind == "proj":
                            which, c = n // KC, n % KC
                            if which == 0:
                                act.activation(qT[:, c, :], src, ACT.Identity, bias=b3s[:, c:c + 1], scale=scale).then_inc(done, 1)
                            else:
                                act.activation(kk[:, c, which - 1, LOOKBACK:], src, ACT.Identity, bias=b3[:, n:n + 1]).then_inc(done, 1)
                        elif kind == "flip":
                            if n >= 2:
                                ring.wait_full(act, b, ("out", n - 2))
                            first = 0 if n else P
                            act.copy(WT[:, n % 2, first:], src[:, first:2 * P]).then_inc(done, 1)
                        elif kind == "norm":
                            act.copy(hT[:, n, :], src).then_inc(done, 1)

            @block.vector
            def _(dve):
                for sem in (ring.drained["dve"], ready, weighted, s_stat, normed, stepped):
                    sem.credit(dve)
                with dve.Fori(0, B) as b:
                    n_done = [0]

                    def step(ins):
                        n_done[0] += 1
                        ins.then_inc(stepped.sem, 1)

                    def stepped_through(before_search=False):
                        stepped.wait(dve, b, n_done[0])
                        if before_search:
                            dve.sem_inc(s_fence, 1)

                    def choose(i):
                        scored.wait(dve, b, i + 1)
                        step(dve.tensor_tensor(Sm[:, i, :], S[:, i, 0:BAND], bias[:, 0 if i == 0 else 1, :], ALU.add))
                        step(dve.tensor_tensor_reduce(junk[:, 0, :], S[:, i, 0:BAND], shift[:, :], 1.0, 0.0, ALU.mult, ALU.add, pair[:, i, 0:1]))
                        step(dve.tensor_tensor_reduce(junk[:, 1, :], S[:, i, BAND:2 * BAND], phrase[:, :], 1.0, 0.0, ALU.mult, ALU.add, pair[:, i, 1:2]))
                        stepped_through(True)
                        step(dve.max(out=best8[:, i, :], in_=Sm[:, i, :]))
                        stepped_through()
                        step(dve.tensor_scalar(nmax[:, i:i + 1], best8[:, i, 0:1], pair[:, i, 1:2], -1.0, ALU.max, ALU.mult))
                        stepped_through()
                        dve.sem_inc(ready.sem, 1)
                        step(dve.match_replace(out=taken8[:, :], in_to_replace=best8[:, i, :], in_values=Sm[:, i, :], imm_value=GONE))
                        stepped_through(True)
                        step(dve.max(out=next8[:, i, :], in_=taken8[:, :]))
                        stepped_through(True)
                        step(dve.match_replace(out=taken16[:, i, :], in_to_replace=next8[:, i, :], in_values=taken8[:, :], imm_value=GONE))
                        stepped_through()

                    def weigh(i):
                        exped.wait(dve, b, 2 * i + 2)
                        step(dve.scalar_tensor_tensor(out=E[:, i, :], in0=taken16[:, i, :], scalar=GONE * 0.5, in1=E[:, i, :],
                                                      op0=ALU.is_lt, op1=ALU.mult, accum_out=sumb[:, i:i + 1]))
                        stepped_through()
                        dve.scalar_tensor_tensor(out=Wt[:, i, P - LOOKBACK:], in0=shift[:, :], scalar=epair[:, i, 0:1], in1=E[:, i, :],
                                                 op0=ALU.mult, op1=ALU.add).then_inc(weighted.sem, 1)
                        step(dve.tensor_scalar(total[:, i:i + 1], sumb[:, i:i + 1], epair[:, i, 0:1], epair[:, i, 1:2], ALU.add, ALU.add))
                        stepped_through()
                        step(dve.reciprocal(rinv[:, i:i + 1], total[:, i:i + 1]))
                        stepped_through()
                        if i == 0:
                            step(dve.tensor_scalar(rinv[:, 0:1], rinv[:, 0:1], after_first[:, :], None, ALU.mult))
                            stepped_through()
                        step(dve.tensor_scalar(wphr[:, i:i + 1], epair[:, i, 1:2], rinv[:, i:i + 1], None, ALU.mult))
                        stepped_through()

                    for st in order:
                        kind, n = st
                        if kind == "score":
                            if n == NT - 1:
                                for i in range(NT):
                                    dve.bn_stats(stats[:, i, :], x_all[:, bass.ds(b * NT + (NT + i), 1), :].rearrange("p a c -> p (a c)")).then_inc(s_stat.sem, 1)
                                s_stat.wait(dve, b, NT)
                                dve.sem_inc(s_fence, 1)
                                for i in range(NT):
                                    dve.bn_aggr(mv[:, i, :], stats[:, i, :]).then_inc(s_stat.sem, 1)
                            continue
                        if kind == "flip":
                            weigh(n)
                            continue
                        if ring.engine(st) != "dve":
                            continue
                        if kind == "out":
                            ring.wait_full(dve, b, st)
                            src, done = ring.bank(st), ring.drained["dve"].sem
                            xt = x_all[:, bass.ds(b * NT + n, 1), :].rearrange("p a c -> p (a c)")
                            step(dve.scalar_tensor_tensor(out=xt, in0=src[:, 0:C], scalar=rinv[:, n:n + 1], in1=xt, op0=ALU.mult, op1=ALU.add))
                            stepped_through()
                            dve.scalar_tensor_tensor(out=xt, in0=src[:, C:2 * C], scalar=wphr[:, n:n + 1], in1=xt, op0=ALU.mult, op1=ALU.add).then_inc(done, 1)
                            continue
                        ring.wait_full(dve, b, st)
                        src, done = ring.bank(st), ring.drained["dve"].sem
                        if kind == "v":
                            dve.tensor_tensor(vv[:, n, :], src, bvv[:, :], ALU.add).then_inc(done, 1)
                            choose(n)
                            if n == 0:
                                rooted.wait(dve, b, 2)
                                for c in range(KC):
                                    ring.wait_full(dve, b, ("norm", c), -1)
                                for i in range(NT):
                                    dve.tensor_scalar(h_tok[:, i, :], x_all[:, bass.ds(b * NT + (NT + i), 1), :].rearrange("p a c -> p (a c)"),
                                                      mv[:, i, 0:1], rstd[:, i:i + 1], ALU.subtract, ALU.mult).then_inc(normed.sem, 1)
                        elif kind == "norm":
                            dve.tensor_copy(hT[:, n, :], src).then_inc(done, 1)
                    assert n_done[0] == stepped.per, n_done

            @block.gpsimd
            def _(pool):
                rooted.credit(pool)
                with pool.Fori(0, B) as b:
                    s_stat.wait(pool, b, 2 * NT)
                    pool.tensor_tensor(rstd[:, :], mv[:, :, 1], eps[:, :], ALU.add).then_inc(rooted.sem, 1)
                    rooted.wait(pool, b, 1)
                    pool.tensor_tensor(rstd[:, :], rstd[:, :], half[:, :], ALU.pow).then_inc(rooted.sem, 1)
        s.clear()


ROUND = 1.5 * 2.0 ** 23
INNER = 1024
FC = INNER // P


def ternary_ffn(nc, x_all, consts, a):
    ident, ident_bf = consts["ident"], consts["ident_bf"]
    HALVES = 2
    order = []
    for i in range(NT + 1):
        if i < NT:
            order += [("gate", HALVES * i + j) for j in range(HALVES)]
        else:
            order.append(("turn_x", 0))
        if i:
            order += [("turn_p", i - 1), ("down", i - 1)]
    ring_steps = [st for st in order if st[0] != "gate"]

    def drained_by(kind, n):
        return "dve" if kind == "down" else "act"

    with ExitStack() as ctx:
        s = Space(nc, ctx, "ffn")
        names = ("gate", "up", "down")
        w = {n: s.sb("w_" + n, [P, 2 * INNER]) for n in names}
        wq = {n: s.sb("wq_" + n, [P, 2 * INNER], BF16) for n in names}
        part, mean, winv = s.sb("part", [P, 3]), s.sb("mean", [P, 3]), s.sb("winv", [P, 3])
        ones = s.sb("ones", [P, P])
        h_tok = s.sb("h_tok", [P, NT, C])
        hq, hqT = s.sb("hq", [P, NT, C], BF16), s.sb("hqT", [P, KC, T], BF16)
        amax, sx, fx = s.sb("amax", [P, NT]), s.sb("sx", [P, NT]), s.sb("fx", [P, 2, NT])
        fg, fu = s.sb("fg", [P, 2, NT]), s.sb("fu", [P, 2, NT])
        g = s.sb("g", [P, 2, 512])
        p = s.sb("p", [P, 2, INNER])
        pr, pq = s.sb("pr", [P, 2, INNER]), s.sb("pq", [P, 2, INNER], BF16)
        pT = s.sb("pT", [P, 2, FC * P], BF16)
        pmax, sp_, fd = s.sb("pmax", [P, NT]), s.sb("sp", [P, NT]), s.sb("fd", [P, NT])
        magic = s.sb("magic", [P, 1])
        stats, mv, rstd = s.sb("stats", [P, NT, 6]), s.sb("mv", [P, NT, 2]), s.sb("rstd", [P, NT])
        half, eps = s.sb("half", [P, NT]), s.sb("eps", [P, NT])
        GU = s.ps("GU", [P, 2, 2, 512])
        W = s.ps("W", [P, 4, 512])

        s_load, s_set, s_fence = s.sem("load"), s.sem("set"), s.sem("fence")
        s_sum, s_tot, s_q = s.sem("sum"), s.sem("tot"), s.sem("q")
        ring = Ring(s, W, 4, ring_steps, drained_by)
        gated = Loop(s.sem("gated"), 2 * NT)
        silued = Loop(s.sem("silued"), 2 * NT)
        multiplied = Loop(s.sem("multiplied"), 2 * NT)
        scaled = Loop(s.sem("scaled"), NT)
        raised = Loop(s.sem("raised"), NT)
        quantised = Loop(s.sem("quantised"), NT)
        x_quantised = Loop(s.sem("x_quantised"), 1)
        s_stat = Loop(s.sem("stat"), 2 * NT)
        rooted = Loop(s.sem("rooted"), 2)
        stepped = Loop(s.sem("stepped"), 5 * NT + 7)

        with nc.Block() as block:
            @block.sync
            def _(sp):
                for n in names:
                    k = KC if n != "down" else FC
                    sp.dma_start(w[n][:, :].rearrange("p (k n) -> p k n", k=k),
                                 a[f"L0_ffn_w_{n}T"].rearrange("(k p) n -> p k n", p=P)).then_inc(s_load, 16)

            @block.vector
            def _(dve):
                dve.memset(half[:, :], -0.5).then_inc(s_set, 1)
                dve.memset(eps[:, :], EPS).then_inc(s_set, 1)
                dve.memset(magic[:, :], ROUND).then_inc(s_set, 1)
                dve.memset(ones[:, :], 1.0).then_inc(s_set, 1)
                dve.wait_ge(s_load, 48)
                for n, name in enumerate(names):
                    dve.tensor_reduce(part[:, n:n + 1], w[name][:, :], AX.X, ALU.add, apply_absolute_value=True).then_inc(s_sum, 1)
                dve.wait_ge(s_tot, 1)
                dve.tensor_scalar(mean[:, :], W[:, 0, 0:3], 1.0 / (C * INNER), EPS, ALU.mult, ALU.max).then_inc(s_q, 1)
                dve.wait_ge(s_q, 1)
                dve.reciprocal(winv[:, :], mean[:, :]).then_inc(s_q, 1)
                dve.wait_ge(s_q, 2)
                for n, name in enumerate(names):
                    dve.tensor_scalar(w[name][:, :], w[name][:, :], winv[:, n:n + 1], 1.0, ALU.mult, ALU.min).then_inc(s_q, 1)
                    dve.wait_ge(s_q, 3 * n + 3)
                    dve.tensor_scalar(w[name][:, :], w[name][:, :], -1.0, ROUND, ALU.max, ALU.add).then_inc(s_q, 1)
                    dve.wait_ge(s_q, 3 * n + 4)
                    dve.tensor_scalar(wq[name][:, :], w[name][:, :], ROUND, None, ALU.subtract).then_inc(s_q, 1)
                dve.wait_ge(s_q, 11)

            @block.tensor
            def _(pe):
                pe.wait_ge(s_set, 4)
                pe.wait_ge(s_sum, 3)
                pe.matmul(W[:, 0, 0:3], ones[:, :], part[:, :], start=True, stop=True).then_inc(s_tot, 1)

        def quantise_x(dve, tiles, step, through, done, slot):
            for i in range(NT):
                step(dve.tensor_scalar(h_tok[:, i, :], tiles(i), mv[:, i, 0:1], rstd[:, i:i + 1], ALU.subtract, ALU.mult))
            through()
            step(dve.tensor_reduce(amax[:, :], h_tok[:, :, :], AX.X, ALU.max, apply_absolute_value=True))
            through()
            step(dve.tensor_scalar(amax[:, :], amax[:, :], EPS, 1.0 / 127.0, ALU.max, ALU.mult))
            through()
            step(dve.reciprocal(sx[:, :], amax[:, :]))
            step(dve.tensor_scalar(fg[:, slot, :], amax[:, :], mean[:, 0:1], None, ALU.mult))
            step(dve.tensor_scalar(fu[:, slot, :], amax[:, :], mean[:, 1:2], None, ALU.mult))
            through()
            for i in range(NT):
                step(dve.tensor_scalar(h_tok[:, i, :], h_tok[:, i, :], sx[:, i:i + 1], ROUND, ALU.mult, ALU.add))
            through()
            dve.tensor_scalar(hq[:, :, :], h_tok[:, :, :], ROUND, 127.0, ALU.subtract, ALU.min).then_inc(done, 1)

        def turn_x(pe, done):
            out = W[:, ring.place[("turn_x", 0)] % 4, :].bitcast(BF16)
            for c in range(KC):
                for i in range(NT):
                    m = pe.transpose(out[:, (c * NT + i) * P:(c * NT + i + 1) * P], hq[:, i, c * P:(c + 1) * P], ident_bf)
            m.then_inc(done, 1)

        s_first, s_p1, s_p2, s_p3 = s.sem("first"), s.sem("first_root"), s.sem("first_q"), s.sem("first_turned")
        with nc.Block() as block:
            @block.vector
            def _(dve):
                count = [0]

                def step(ins):
                    count[0] += 1
                    ins.then_inc(s_first, 1)

                def through():
                    dve.wait_ge(s_first, count[0])

                for i in range(NT):
                    step(dve.bn_stats(stats[:, i, :], x_all[:, i, :]))
                through()
                for i in range(NT):
                    step(dve.bn_aggr(mv[:, i, :], stats[:, i, :]))
                dve.wait_ge(s_p1, 2)
                quantise_x(dve, lambda i: x_all[:, i, :], step, through, s_p2, 0)
                dve.wait_ge(s_p3, 1)
                dve.tensor_copy(hqT[:, :, :].rearrange("p c t -> p (c t)"), W[:, ring.place[("turn_x", 0)] % 4, :].bitcast(BF16)).then_inc(s_p3, 1)
                dve.wait_ge(s_p3, 2)

            @block.gpsimd
            def _(pool):
                pool.wait_ge(s_first, 2 * NT)
                pool.tensor_tensor(rstd[:, :], mv[:, :, 1], eps[:, :], ALU.add).then_inc(s_p1, 1)
                pool.wait_ge(s_p1, 1)
                pool.tensor_tensor(rstd[:, :], rstd[:, :], half[:, :], ALU.pow).then_inc(s_p1, 1)

            @block.tensor
            def _(pe):
                pe.wait_ge(s_p2, 1)
                turn_x(pe, s_p3)

        with nc.Block() as block:
            @block.tensor
            def _(pe):
                for sem in (ring.full, gated):
                    sem.credit(pe)
                with pe.Fori(0, B) as b:
                    for kind, n in order:
                        if kind == "gate":
                            i, j = n // HALVES, n % HALVES
                            if n == 0:
                                ring.wait_drained(pe, b, ("turn_x", 0), -1)
                            multiplied.wait(pe, b, n - 1)
                            for t, name in enumerate(("gate", "up")):
                                for c in range(KC):
                                    m = pe.matmul(GU[:, j, t, :], hqT[:, c, i * P:(i + 1) * P],
                                                  wq[name][:, c * INNER + j * 512:c * INNER + (j + 1) * 512],
                                                  start=(c == 0), stop=(c == KC - 1))
                            m.then_inc(gated.sem, 1)
                        elif kind == "turn_x":
                            ring.free_bank(pe, b, (kind, n))
                            x_quantised.wait(pe, b, 1)
                            turn_x(pe, ring.full.sem)
                        elif kind == "turn_p":
                            out = ring.free_bank(pe, b, (kind, n)).bitcast(BF16)
                            quantised.wait(pe, b, n + 1)
                            for f in range(FC):
                                m = pe.transpose(out[:, f * P:(f + 1) * P], pq[:, n % 2, f * P:(f + 1) * P], ident_bf)
                            m.then_inc(ring.full.sem, 1)
                        elif kind == "down":
                            dst = ring.free_bank(pe, b, (kind, n))
                            ring.wait_drained(pe, b, ("turn_p", n))
                            for f in range(FC):
                                m = pe.matmul(dst[:, 0:C], pT[:, n % 2, f * P:(f + 1) * P], wq["down"][:, f * C:(f + 1) * C],
                                              start=(f == 0), stop=(f == FC - 1))
                            m.then_inc(ring.full.sem, 1)

            @block.scalar
            def _(act):
                for sem in (ring.drained["act"], silued, raised):
                    sem.credit(act)
                with act.Fori(0, B) as b:
                    def raise_p(i):
                        scaled.wait(act, b, i + 1)
                        act.activation(pr[:, i % 2, :], p[:, i % 2, :], ACT.Identity, bias=magic[:, :], scale=sp_[:, i:i + 1]).then_inc(raised.sem, 1)

                    for st in order:
                        kind, n = st
                        if kind == "gate":
                            i, j = n // HALVES, n % HALVES
                            gated.wait(act, b, n + 1)
                            if n == 0:
                                stepped.wait(act, b, 0)
                            multiplied.wait(act, b, n - 1)
                            act.activation(g[:, j, :], GU[:, j, 0, :], ACT.Silu, scale=fg[:, 0, i:i + 1]).then_inc(silued.sem, 1)
                            continue
                        if kind == "turn_p":
                            raise_p(n)
                        if ring.engine(st) != "act":
                            continue
                        ring.wait_full(act, b, st)
                        src, done = ring.bank(st), ring.drained["act"].sem
                        if kind == "turn_p":
                            if n >= 2:
                                ring.wait_full(act, b, ("down", n - 2))
                            act.copy(pT[:, n % 2, :], src.bitcast(BF16)).then_inc(done, 1)
                        else:
                            gated.wait(act, b, 2 * NT)
                            act.copy(hqT[:, :, :].rearrange("p c t -> p (c t)"), src.bitcast(BF16)).then_inc(done, 1)

            @block.vector
            def _(dve):
                for sem in (ring.drained["dve"], multiplied, scaled, quantised, x_quantised, s_stat, stepped):
                    sem.credit(dve)
                with dve.Fori(0, B) as b:
                    count = [0]

                    def step(ins):
                        count[0] += 1
                        ins.then_inc(stepped.sem, 1)

                    def through():
                        stepped.wait(dve, b, count[0])

                    def next_tile(i):
                        return x_all[:, bass.ds(b * NT + (NT + i), 1), :].rearrange("p a c -> p (a c)")

                    for st in order:
                        kind, n = st
                        if kind == "gate":
                            i, j = n // HALVES, n % HALVES
                            silued.wait(dve, b, n + 1)
                            dve.scalar_tensor_tensor(out=p[:, i % 2, j * 512:(j + 1) * 512], in0=GU[:, j, 1, :], scalar=fu[:, 0, i:i + 1],
                                                     in1=g[:, j, :], op0=ALU.mult, op1=ALU.mult).then_inc(multiplied.sem, 1)
                            if j == HALVES - 1:
                                multiplied.wait(dve, b, n + 1)
                                step(dve.tensor_reduce(pmax[:, i:i + 1], p[:, i % 2, :], AX.X, ALU.max, apply_absolute_value=True))
                                through()
                                step(dve.tensor_scalar(pmax[:, i:i + 1], pmax[:, i:i + 1], EPS, 1.0 / 127.0, ALU.max, ALU.mult))
                                through()
                                step(dve.tensor_scalar(fd[:, i:i + 1], pmax[:, i:i + 1], mean[:, 2:3], None, ALU.mult))
                                dve.reciprocal(sp_[:, i:i + 1], pmax[:, i:i + 1]).then_inc(scaled.sem, 1)
                            if n == 1:
                                for t in range(NT):
                                    dve.bn_stats(stats[:, t, :], next_tile(t)).then_inc(s_stat.sem, 1)
                                s_stat.wait(dve, b, NT)
                                dve.sem_inc(s_fence, 1)
                                for t in range(NT):
                                    dve.bn_aggr(mv[:, t, :], stats[:, t, :]).then_inc(s_stat.sem, 1)
                            if n == 3:
                                rooted.wait(dve, b, 2)
                                quantise_x(dve, next_tile, step, through, x_quantised.sem, 1)
                            continue
                        if kind == "turn_p":
                            raised.wait(dve, b, n + 1)
                            dve.tensor_scalar(pq[:, n % 2, :], pr[:, n % 2, :], ROUND, 127.0, ALU.subtract, ALU.min).then_inc(quantised.sem, 1)
                            continue
                        if kind == "down":
                            ring.wait_full(dve, b, st)
                            xt = x_all[:, bass.ds(b * NT + n, 1), :].rearrange("p a c -> p (a c)")
                            dve.scalar_tensor_tensor(out=xt, in0=ring.bank(st)[:, 0:C], scalar=fd[:, n:n + 1], in1=xt,
                                                     op0=ALU.mult, op1=ALU.add).then_inc(ring.drained["dve"].sem, 1)
                    through()
                    step(dve.tensor_copy(fg[:, 0, :], fg[:, 1, :]))
                    step(dve.tensor_copy(fu[:, 0, :], fu[:, 1, :]))
                    through()
                    assert count[0] == stepped.per, count

            @block.gpsimd
            def _(pool):
                rooted.credit(pool)
                with pool.Fori(0, B) as b:
                    s_stat.wait(pool, b, 2 * NT)
                    pool.tensor_tensor(rstd[:, :], mv[:, :, 1], eps[:, :], ALU.add).then_inc(rooted.sem, 1)
                    rooted.wait(pool, b, 1)
                    pool.tensor_tensor(rstd[:, :], rstd[:, :], half[:, :], ALU.pow).then_inc(rooted.sem, 1)
        s.clear()


EXPERTS, D_FF = 8, 1024
FF = D_FF // P
SLOTS = NX + EXPERTS - 1
AHEAD = 3


def mixture(nc, x_all, consts, a, out):
    ident = consts["ident"]
    sorted_h = nc.dram_tensor("sorted_h", ((SLOTS + AHEAD) * P, C), F32, kind="Internal").ap()
    sorted_y = nc.dram_tensor("sorted_y", (SLOTS * P, C), F32, kind="Internal").ap()
    with ExitStack() as ctx:
        s = Space(nc, ctx, "moe")
        W1 = s.sb("W1", [P, EXPERTS * KC * D_FF])
        W2 = s.sb("W2", [P, EXPERTS * FF * C])
        position = s.sb("position", [P, NX], I32)
        gate = s.sb("gate", [P, NX])
        owner = s.sb("owner", [P, SLOTS + AHEAD], I32)
        s_w, s_zero, s_set = s.sem("w"), s.sem("zero"), s.sem("set")
        route(nc, x_all, consts, a, sorted_h, W1, W2, position, gate, owner, s_w, s_zero)
        with ExitStack() as inner:
            experts(nc, Space(nc, inner, "experts"), consts, a, sorted_h, sorted_y, W1, W2, owner, s_w)
        with ExitStack() as inner:
            combine(nc, Space(nc, inner, "combine"), x_all, position, gate, sorted_y, out)


def route(nc, x_all, consts, a, sorted_h, W1, W2, position, gate, owner, s_w, s_zero):
    ident = consts["ident"]
    E = EXPERTS
    with ExitStack() as ctx:
        s = Space(nc, ctx, "route")
        h_all = s.sb("h", [P, NX, C])
        hT = s.sb("hT", [P, 2, C])
        rw, rb = s.sb("rw", [P, KC, E]), s.sb("rb", [P, E])
        later32, later, ones = s.sb("later32", [P, P]), s.sb("later", [P, P], BF16), s.sb("ones", [P, P], BF16)
        rank, slot_no = s.sb("rank", [P, E]), s.sb("slot_no", [P, SLOTS + AHEAD])
        logits, t0, t1 = (consts["spare"][:, n * NX * E:(n + 1) * NX * E].rearrange("p (t e) -> p t e", e=E) for n in range(3))
        hot = s.sb("hot", [P, NX, E], BF16)
        row = s.sb("row", [P, NX])
        cnt, tiles, start, end = s.sb("cnt", [P, E]), s.sb("tiles", [P, E]), s.sb("start", [P, 2, E]), s.sb("end", [P, E])
        over, own = s.sb("over", [P, SLOTS + AHEAD, E]), s.sb("own", [P, SLOTS + AHEAD])
        stats, mv, rstd = s.sb("stats", [P, 2, 6]), s.sb("mv", [P, NX, 2]), s.sb("rstd", [P, NX])
        half = s.sb("half", [P, NX])
        tr = s.ps("tr", [P, 2, 512])
        lg = s.ps("lg", [P, 2, 512])
        pre = s.ps("pre", [P, 512])
        tot = s.ps("tot", [P, 512])
        s_load, s_set, s_stat, s_mv, s_root, s_h = (s.sem(n) for n in ("load", "set", "stat", "mv", "root", "h"))
        s_tr, s_hT, s_lg, s_lgd = (s.sem(n) for n in ("tr", "hT", "lg", "lgd"))
        s_d, s_exp, s_hot, s_cnt, s_pos, s_sc = (s.sem(n) for n in ("d", "exp", "hot", "cnt", "pos", "sc"))

        with nc.Block() as block:
            @block.sync
            def _(sp):
                loads = [(rw[:, :, :], a["L1_ffn_router_W"].rearrange("(k p) e -> p k e", p=P)),
                         (rb[:, :], a["L1_ffn_router_b"].unsqueeze(0).partition_broadcast(P)),
                         (later32[:, :], a["later"]), (rank[:, :], a["rank"]), (slot_no[:, :], a["slot_no"])]
                for dst, src in loads:
                    sp.dma_start(dst, src).then_inc(s_load, 16)
                sp.dma_start(sorted_h.rearrange("(g p) c -> p g c", p=P),
                             x_all[:, NX, :].unsqueeze(1).to_broadcast([P, SLOTS + AHEAD, C])).then_inc(s_zero, 16)
                for e in range(E):
                    sp.dma_start(W1[:, e * KC * D_FF:(e + 1) * KC * D_FF].rearrange("p (k n) -> p k n", k=KC),
                                 a["L1_ffn_W1"][e].rearrange("(k p) n -> p k n", p=P)).then_inc(s_w, 16)
                for e in range(E):
                    sp.dma_start(W2[:, e * FF * C:(e + 1) * FF * C].rearrange("p (k n) -> p k n", k=FF),
                                 a["L1_ffn_W2"][e].rearrange("(k p) n -> p k n", p=P)).then_inc(s_w, 16)

            @block.gpsimd
            def _(pool):
                pool.memset(half[:, :], -0.5).then_inc(s_root, 1)
                pool.wait_ge(s_mv, NX)
                pool.tensor_scalar(rstd[:, :], mv[:, :, 1], EPS, None, ALU.add).then_inc(s_root, 1)
                pool.wait_ge(s_root, 2)
                pool.tensor_tensor(rstd[:, :], rstd[:, :], half[:, :], ALU.pow).then_inc(s_root, 1)
                pool.wait_ge(s_zero, 16)
                pool.wait_ge(s_h, NX)
                pool.wait_ge(s_pos, 1)
                for t in range(NX):
                    pool.indirect_dma_start(out=sorted_h, out_offset=bass.IndirectOffsetOnAxis(ap=position[:, t:t + 1], axis=0),
                                            in_=h_all[:, t, :], in_offset=None).then_inc(s_sc, 16)
                pool.wait_ge(s_sc, 16 * NX)

            @block.vector
            def _(dve):
                for t in range(NX):
                    if t >= 2:
                        dve.wait_ge(s_mv, t - 1)
                    dve.bn_stats(stats[:, t % 2, :], x_all[:, t, :]).then_inc(s_stat, 1)
                    if t:
                        dve.wait_ge(s_stat, t)
                        dve.bn_aggr(mv[:, t - 1, :], stats[:, (t - 1) % 2, :]).then_inc(s_mv, 1)
                dve.wait_ge(s_stat, NX)
                dve.bn_aggr(mv[:, NX - 1, :], stats[:, (NX - 1) % 2, :]).then_inc(s_mv, 1)
                dve.wait_ge(s_root, 3)
                dve.memset(ones[:, :], 1.0).then_inc(s_set, 1)
                for t in range(NX):
                    dve.tensor_scalar(h_all[:, t, :], x_all[:, t, :], mv[:, t, 0:1], rstd[:, t:t + 1],
                                      ALU.subtract, ALU.mult).then_inc(s_h, 1)
                dve.wait_ge(s_load, 16 * 5)
                dve.tensor_copy(later[:, :], later32[:, :]).then_inc(s_set, 1)
                for t in range(NX):
                    dve.wait_ge(s_lg, t + 1)
                    dve.tensor_tensor(logits[:, t, :], lg[:, t % 2, 0:E], rb[:, :], ALU.add).then_inc(s_lgd, 1)
                dve.wait_ge(s_lgd, NX)

                count = [0]

                def step(ins):
                    count[0] += 1
                    ins.then_inc(s_d, 1)
                    dve.wait_ge(s_d, count[0])

                def per_token(v):
                    return v[:, :].unsqueeze(2).to_broadcast([P, NX, E])

                def per_expert(v, n=NX):
                    return v.unsqueeze(1).to_broadcast([P, n, E])

                step(dve.tensor_reduce(row[:, :], logits[:, :, :], AX.X, ALU.max))
                step(dve.tensor_tensor(t0[:, :, :], logits[:, :, :], per_token(row), ALU.subtract))
                dve.sem_inc(s_exp, 1)
                dve.wait_ge(s_exp, 2)
                step(dve.tensor_reduce(row[:, :], t1[:, :, :], AX.X, ALU.add))
                step(dve.reciprocal(gate[:, :], row[:, :]))
                step(dve.tensor_reduce(row[:, :], t1[:, :, :], AX.X, ALU.max))
                step(dve.tensor_tensor(gate[:, :], gate[:, :], row[:, :], ALU.mult))
                step(dve.tensor_tensor(t0[:, :, :], t1[:, :, :], per_token(row), ALU.is_ge))
                step(dve.tensor_tensor(t0[:, :, :], t0[:, :, :], per_expert(rank[:, :]), ALU.mult))
                step(dve.tensor_reduce(row[:, :], t0[:, :, :], AX.X, ALU.max))
                step(dve.tensor_tensor(hot[:, :, :], t0[:, :, :], per_token(row), ALU.is_equal))
                dve.sem_inc(s_hot, 1)
                dve.wait_ge(s_cnt, 2)
                step(dve.tensor_copy(t0[:, :, :], tot[:, 0:NX * E].rearrange("p (t e) -> p t e", e=E)))
                src, dst = t0, t1
                for d in (1, 2, 4, 8, 16):
                    step(dve.tensor_tensor(dst[:, d:, :], src[:, d:, :], src[:, 0:NX - d, :], ALU.add))
                    step(dve.tensor_copy(dst[:, 0:d, :], src[:, 0:d, :]))
                    src, dst = dst, src
                step(dve.tensor_scalar(cnt[:, :], src[:, NX - 1, :], float(P - 1), 1.0 / P, ALU.add, ALU.mult))
                step(dve.tensor_scalar(cnt[:, :], cnt[:, :], (P / 2 - 0.5) / P, ROUND, ALU.subtract, ALU.add))
                step(dve.tensor_scalar(tiles[:, :], cnt[:, :], ROUND, None, ALU.subtract))
                step(dve.tensor_copy(end[:, 0:1], tiles[:, 0:1]))
                for e in range(1, E):
                    step(dve.tensor_tensor(end[:, e:e + 1], end[:, e - 1:e], tiles[:, e:e + 1], ALU.add))
                step(dve.tensor_tensor(start[:, 0, :], end[:, :], tiles[:, :], ALU.subtract))
                step(dve.tensor_scalar(start[:, 1, :], start[:, 0, :], float(P), None, ALU.mult))
                step(dve.tensor_tensor(src[:, :, :], src[:, :, :], tot[:, 0:NX * E].rearrange("p (t e) -> p t e", e=E), ALU.subtract))
                step(dve.tensor_tensor(src[:, :, :], src[:, :, :], pre[:, 0:NX * E].rearrange("p (t e) -> p t e", e=E), ALU.add))
                step(dve.tensor_tensor(src[:, :, :], src[:, :, :], per_expert(start[:, 1, :]), ALU.add))
                step(dve.tensor_tensor(src[:, :, :], src[:, :, :], hot[:, :, :], ALU.mult))
                step(dve.tensor_reduce(row[:, :], src[:, :, :], AX.X, ALU.add))
                step(dve.tensor_copy(position[:, :], row[:, :]))
                dve.sem_inc(s_pos, 1)
                n = SLOTS + AHEAD
                step(dve.tensor_tensor(over[:, :, :], slot_no[:, :].unsqueeze(2).to_broadcast([P, n, E]), per_expert(end[:, :], n), ALU.is_ge))
                step(dve.tensor_reduce(own[:, :], over[:, :, :], AX.X, ALU.add))
                step(dve.tensor_scalar(own[:, :], own[:, :], float(E - 1), None, ALU.min))
                step(dve.tensor_copy(owner[:, :], own[:, :]))

            @block.tensor
            def _(pe):
                def logits_of(t):
                    pe.wait_ge(s_hT, t + 1)
                    if t >= 2:
                        pe.wait_ge(s_lgd, t - 1)
                    for c in range(KC):
                        m = pe.matmul(lg[:, t % 2, 0:E], hT[:, t % 2, c * P:(c + 1) * P], rw[:, c, :], start=(c == 0), stop=(c == KC - 1))
                    m.then_inc(s_lg, 1)

                pe.wait_ge(s_load, 16 * 5)
                for t in range(NX):
                    pe.wait_ge(s_h, t + 1)
                    if t >= 2:
                        pe.wait_ge(s_hT, t - 1)
                    for c in range(KC):
                        m = pe.transpose(tr[:, t % 2, c * P:(c + 1) * P], h_all[:, t, c * P:(c + 1) * P], ident)
                    m.then_inc(s_tr, 1)
                    if t:
                        logits_of(t - 1)
                logits_of(NX - 1)
                pe.wait_ge(s_hot, 1)
                pe.wait_ge(s_set, 2)
                flat = hot[:, :, :].rearrange("p t e -> p (t e)")
                pe.matmul(pre[:, 0:NX * E], later[:, :], flat, start=True, stop=True).then_inc(s_cnt, 1)
                pe.matmul(tot[:, 0:NX * E], ones[:, :], flat, start=True, stop=True).then_inc(s_cnt, 1)

            @block.scalar
            def _(act):
                for t in range(NX):
                    act.wait_ge(s_tr, t + 1)
                    if t >= 2:
                        act.wait_ge(s_lg, t - 1)
                    act.copy(hT[:, t % 2, :], tr[:, t % 2, 0:C]).then_inc(s_hT, 1)
                act.wait_ge(s_exp, 1)
                act.activation(t1[:, :, :], t0[:, :, :], ACT.Exp).then_inc(s_exp, 1)
        s.clear()



def experts(nc, s, consts, a, sorted_h, sorted_y, W1, W2, owner, s_w):
    ident = consts["ident"]
    xs, xT = s.sb("xs", [P, C]), s.sb("xT", [P, C])
    hid, hidT = s.sb("hid", [P, D_FF]), s.sb("hidT", [P, FF, P])
    y = s.sb("y", [P, C])
    b1T, b2B = s.sb("b1T", [P, EXPERTS * FF]), s.sb("b2B", [P, EXPERTS * C])
    A = s.ps("A", [P, 2, 512])
    AT = s.ps("AT", [P, 2, 512])
    XP, Y = s.ps("XP", [P, 512]), s.ps("Y", [P, 512])
    s_load, s_pro, s_half = s.sem("load"), s.sem("pro"), s.sem("half")
    loaded, stored = Loop(s.sem("loaded"), 16), Loop(s.sem("stored"), 16)
    x_turned, x_moved = Loop(s.sem("x_turned"), 1), Loop(s.sem("x_moved"), 1)
    first, hid_act, hid_dve = Loop(s.sem("first"), 1), Loop(s.sem("hid_act"), 1), Loop(s.sem("hid_dve"), 1)
    turned, turned_act, turned_dve = Loop(s.sem("turned"), 2), Loop(s.sem("turned_act"), 1), Loop(s.sem("turned_dve"), 1)
    second, y_ready = Loop(s.sem("second"), 1), Loop(s.sem("y_ready"), 1)
    tiles_h = sorted_h.rearrange("(g p) c -> g p c", p=P)
    tiles_y = sorted_y.rearrange("(g p) c -> g p c", p=P)

    def turn_x(pe):
        for c in range(KC):
            m = pe.transpose(XP[:, c * P:(c + 1) * P], xs[:, c * P:(c + 1) * P], ident)
        return m

    def first_product(pe, e):
        for j in range(2):
            for c in range(KC):
                m = pe.matmul(A[:, j, :], xT[:, c * P:(c + 1) * P], W1[:, bass.ds(e * (KC * D_FF) + (c * D_FF + j * 512), 512)],
                              start=(c == 0), stop=(c == KC - 1))
        return m

    def expert_of(eng, g):
        return eng.value_load(owner[0:1, bass.ds(g, 1)], min_val=0, max_val=EXPERTS - 1)

    with nc.Block() as block:
        @block.sync
        def _(sp):
            sp.dma_start(b1T[:, :].rearrange("p (e f) -> p e f", f=FF), a["L1_ffn_b1"].rearrange("e (f p) -> p e f", p=P),
                         allow_slow_non_contiguous=True).then_inc(s_load, 16)
            sp.dma_start(b2B[:, :], a["L1_ffn_b2"].rearrange("e c -> (e c)").unsqueeze(0).partition_broadcast(P)).then_inc(s_load, 16)
            sp.wait_ge(s_load, 32)
            for g in range(3):
                if g:
                    sp.wait_ge(s_pro, 3 * g - 2)
                sp.dma_start(xs[:, :], tiles_h[g]).then_inc(s_load, 16)
                sp.wait_ge(s_load, 16 * (3 + g))

        @block.tensor
        def _(pe):
            pe.wait_ge(s_load, 48)
            turn_x(pe).then_inc(s_pro, 1)
            pe.wait_ge(s_pro, 2)
            pe.wait_ge(s_w, 32 * EXPERTS)
            first_product(pe, expert_of(pe, 0)).then_inc(s_pro, 1)
            pe.wait_ge(s_load, 64)
            turn_x(pe).then_inc(s_pro, 1)

        @block.scalar
        def _(act):
            act.wait_ge(s_pro, 1)
            act.copy(xT[:, :], XP[:, 0:C]).then_inc(s_pro, 1)
            act.wait_ge(s_pro, 4)
            act.copy(xT[:, :], XP[:, 0:C]).then_inc(s_pro, 1)
            act.copy(hid[:, 0:512], A[:, 0, :]).then_inc(s_pro, 1)

        @block.vector
        def _(dve):
            dve.wait_ge(s_pro, 3)
            dve.tensor_copy(hid[:, 512:D_FF], A[:, 1, :]).then_inc(s_half, 1)

    with nc.Block() as block:
        @block.tensor
        def _(pe):
            for sem in (turned, first, x_turned, second):
                sem.credit(pe)
            with pe.Fori(0, SLOTS) as g:
                e_next, e = expert_of(pe, g + 1), expert_of(pe, g)
                for j, moved, freed in ((0, hid_act, turned_act), (1, hid_dve, turned_dve)):
                    moved.wait(pe, g, 0)
                    freed.wait(pe, g, 0)
                    for f in range(4):
                        m = pe.transpose(AT[:, j, f * P:(f + 1) * P], hid[:, (4 * j + f) * P:(4 * j + f + 1) * P], ident)
                    m.then_inc(turned.sem, 1)
                x_moved.wait(pe, g, 0)
                first_product(pe, e_next).then_inc(first.sem, 1)
                loaded.wait(pe, g, 0)
                turn_x(pe).then_inc(x_turned.sem, 1)
                turned_act.wait(pe, g, 1)
                turned_dve.wait(pe, g, 1)
                y_ready.wait(pe, g, 0)
                for f in range(FF):
                    m = pe.matmul(Y[:, 0:C], hidT[:, f, :], W2[:, bass.ds(e * (FF * C) + f * C, C)], start=(f == 0), stop=(f == FF - 1))
                m.then_inc(second.sem, 1)

        @block.scalar
        def _(act):
            for sem in (turned_act, hid_act, x_moved):
                sem.credit(act)
            with act.Fori(0, SLOTS) as g:
                e = expert_of(act, g)
                turned.wait(act, g, 1)
                second.wait(act, g, 0)
                for f in range(4):
                    m = act.activation(hidT[:, f, :], AT[:, 0, f * P:(f + 1) * P], ACT.Relu, bias=b1T[:, bass.ds(e * FF + f, 1)])
                m.then_inc(turned_act.sem, 1)
                first.wait(act, g, 1)
                act.copy(hid[:, 0:512], A[:, 0, :]).then_inc(hid_act.sem, 1)
                x_turned.wait(act, g, 1)
                act.copy(xT[:, :], XP[:, 0:C]).then_inc(x_moved.sem, 1)

        @block.vector
        def _(dve):
            for sem in (turned_dve, hid_dve, y_ready):
                sem.credit(dve)
            with dve.Fori(0, SLOTS) as g:
                e = expert_of(dve, g)
                turned.wait(dve, g, 2)
                second.wait(dve, g, 0)
                for f in range(4, FF):
                    m = dve.tensor_scalar(hidT[:, f, :], AT[:, 1, (f - 4) * P:(f - 3) * P], b1T[:, bass.ds(e * FF + f, 1)], 0.0, ALU.add, ALU.max)
                m.then_inc(turned_dve.sem, 1)
                first.wait(dve, g, 1)
                dve.tensor_copy(hid[:, 512:D_FF], A[:, 1, :]).then_inc(hid_dve.sem, 1)
                second.wait(dve, g, 1)
                stored.wait(dve, g, 0)
                dve.tensor_tensor(y[:, :], Y[:, 0:C], b2B[:, bass.ds(e * C, C)], ALU.add).then_inc(y_ready.sem, 1)

        @block.sync
        def _(sp):
            loaded.credit(sp)
            stored.credit(sp)
            with sp.Fori(0, SLOTS) as g:
                following = sp.snap(g + AHEAD)
                x_turned.wait(sp, g, 1)
                sp.dma_start(xs[:, :], tiles_h[bass.ds(following, 1), :, :].rearrange("a p c -> (a p) c")).then_inc(loaded.sem, 16)
                y_ready.wait(sp, g, 1)
                sp.dma_start(tiles_y[bass.ds(g, 1), :, :].rearrange("a p c -> (a p) c"), y[:, :]).then_inc(stored.sem, 16)
            sp.wait_ge(stored.sem, 16 * (SLOTS + 1))
            sp.wait_ge(loaded.sem, 16 * (SLOTS + 1))
    s.clear()



def combine(nc, s, x_all, position, gate, sorted_y, out):
    DEPTH = 8
    yg = s.sb("yg", [P, DEPTH, C])
    got = [s.sem(f"got{d}") for d in range(DEPTH)]
    s_done, s_out = s.sem("done"), s.sem("out")
    PART = 4
    with nc.Block() as block:
        @block.gpsimd
        def _(pool):
            for t in range(NX):
                if t >= DEPTH:
                    pool.wait_ge(s_done, t - DEPTH + 1)
                pool.indirect_dma_start(out=yg[:, t % DEPTH, :], out_offset=None, in_=sorted_y,
                                        in_offset=bass.IndirectOffsetOnAxis(ap=position[:, t:t + 1], axis=0)).then_inc(got[t % DEPTH], 16)

        @block.vector
        def _(dve):
            for t in range(NX):
                dve.wait_ge(got[t % DEPTH], 16 * (t // DEPTH + 1))
                dve.scalar_tensor_tensor(out=x_all[:, t, :], in0=yg[:, t % DEPTH, :], scalar=gate[:, t:t + 1], in1=x_all[:, t, :],
                                         op0=ALU.mult, op1=ALU.add).then_inc(s_done, 1)

        @block.sync
        def _(sp):
            for t in range(0, NX, PART):
                sp.wait_ge(s_done, t + PART)
                sp.dma_start(out[t * P:(t + PART) * P, :].rearrange("(n p) c -> p n c", p=P), x_all[:, t:t + PART, :]).then_inc(s_out, 16)
            sp.wait_ge(s_out, 16 * (NX // PART))
    s.clear()


def build(nc, a, outs, phases=("band", "cross0", "ffn", "self", "cross1", "moe")):
    with ExitStack() as ctx:
        s = Space(nc, ctx, "all")
        x_mem = s.sb("x", [P, NT + NX + NT, C])
        x_all = x_mem[:, NT:, :]
        ident, ident_bf = s.sb("ident", [P, P]), s.sb("ident_bf", [P, P], BF16)
        s_x, s_c = s.sem("x"), s.sem("c")
        consts = {"ident": ident[:, :], "ident_bf": ident_bf[:, :], "band_d": a["window_bias"],
                  "spare": x_mem[:, 0:NT, :].rearrange("p n c -> p (n c)")}
        with nc.Block() as block:
            @block.sync
            def _(sp):
                sp.dma_start(ident[:, :], a["ident"]).then_inc(s_x, 16)
                sp.dma_start(x_all[:, 0:NX, :], a["x"].rearrange("(n p) c -> p n c", p=P)).then_inc(s_x, 16)
                sp.wait_ge(s_x, 32)

            @block.vector
            def _(dve):
                dve.memset(x_mem[:, 0:NT, :], 0.0).then_inc(s_c, 1)
                dve.memset(x_mem[:, NT + NX:, :], 0.0).then_inc(s_c, 1)
                dve.wait_ge(s_x, 32)
                dve.tensor_copy(ident_bf[:, :], ident[:, :]).then_inc(s_c, 1)
                dve.wait_ge(s_c, 3)

        if "band" in phases:
            band_attention(nc, x_all, consts, a)
        if "cross0" in phases:
            attention(nc, "cross0", x_mem, consts, 16, a["L0_xattn_W_q"], a["L0_xattn_W_k"], a["L0_xattn_W_v"],
                      a["L0_xattn_W_c"], ctx_d=a["ctx_T"], mask_d=a["mask"],
                      rope=(a["cos0"], a["sin0"], a["turn0"]))
        if "ffn" in phases:
            ternary_ffn(nc, x_all, consts, a)
        if "self" in phases:
            attention(nc, "self1", x_mem, consts, 64, a["L1_attn_W_q"], a["L1_attn_W_k"], a["L1_attn_W_v"], a["L1_attn_W_out"])
        if "cross1" in phases:
            attention(nc, "cross1", x_mem, consts, 16, a["L1_xattn_WqT"], a["L1_xattn_WkT"], a["L1_xattn_WvT"],
                      a["L1_xattn_WoT"], ctx_d=a["ctx_T"], window=True,
                      rope=(a["cos1"], a["sin1"], a["turn1"]),
                      bias_d=(a["L1_xattn_bq"], a["L1_xattn_bk"], a["L1_xattn_bv"], a["L1_xattn_bo"]))
        if "moe" in phases:
            mixture(nc, x_all, consts, a, outs)
        else:
            with nc.Block() as block:
                @block.sync
                def _(sp):
                    sp.dma_start(outs.rearrange("(n p) c -> p n c", p=P), x_all[:, 0:NX, :]).then_inc(s_x, 16)
                    sp.wait_ge(s_x, 48)


def rotation_tables():
    D = C // H
    f = np.float32
    d = np.arange(P) % D
    w = f(1.0) / f(10000.0) ** (np.arange(1, D + 1, 2, dtype=f) / f(D))
    ang = np.arange(1, T + 1, dtype=f)[None, :] * w[(d // 2)][:, None]
    sign0 = np.where(d % 2 == 0, -1.0, 1.0)[:, None]
    cos0, sin0 = np.cos(ang).astype(f), (np.sin(ang) * sign0).astype(f)
    turn0 = np.zeros((P, P), f)
    turn0[np.arange(P) ^ 1, np.arange(P)] = 1
    half = D // 2
    w = f(1.0) / f(10000.0) ** (np.arange(half, dtype=f) / f(half))
    ang = np.arange(T, dtype=f)[None, :] * w[d % half][:, None]
    sign1 = np.where(d < half, -1.0, 1.0)[:, None]
    cos1, sin1 = np.cos(ang).astype(f), (np.sin(ang) * sign1).astype(f)
    turn1 = np.zeros((P, P), f)
    turn1[np.arange(P) ^ half, np.arange(P)] = 1
    return cos0, sin0, turn0, cos1, sin1, turn1


def shape_constants():
    f = np.float32
    c = {"ident": np.eye(P, dtype=f)}
    c["cos0"], c["sin0"], c["turn0"], c["cos1"], c["sin1"], c["turn1"] = rotation_tables()
    p, k = np.arange(P)[:, None], np.arange(P)[None, :]
    c["window_bias"] = np.where(np.concatenate([k >= p, k <= p], 1), 0.0, NEG).astype(f)
    j = np.arange(BAND)[None, :]
    inside = (j >= p) & (j < p + LOOKBACK)
    c["band_bias"] = np.stack([np.where(inside & (j >= LOOKBACK), 0.0, NEG), np.where(inside, 0.0, NEG)], 1).astype(f)
    c["band_shift"] = (j == p + LOOKBACK - 1).astype(f)
    def mean_weights(tok):
        last = p - 1
        start = last // PHRASE * PHRASE
        return np.where((tok >= start) & (tok <= last), 1.0 / (last - start + 1), 0.0).astype(f)
    c["phrase"] = mean_weights(j - LOOKBACK)
    c["phrase_T"] = np.stack([mean_weights(k - P).T, mean_weights(k).T], 1)
    c["after_first"] = (p > 0).astype(f)
    c["later"] = (p < k).astype(f)
    c["rank"] = np.broadcast_to(np.arange(EXPERTS, 0, -1, dtype=f), (P, EXPERTS)).copy()
    c["slot_no"] = np.broadcast_to(np.arange(SLOTS + AHEAD, dtype=f), (P, SLOTS + AHEAD)).copy()
    return c


def laid_out(inputs):
    a = {k: np.asarray(v) for k, v in inputs.items()}
    m = shape_constants()
    m["x"] = a["x"].reshape(B * T, C)
    m["ctx_T"] = a["ctx_1024"].transpose(0, 2, 1)
    m["mask"] = a["mask_BxS2_bf1"].view(np.uint8)
    for n in ("q", "k", "v", "pk", "pv"):
        m[f"L0_attn_{n}_wT"] = a[f"L0_attn_{n}_w"].T
        m[f"L0_attn_{n}_b"] = a[f"L0_attn_{n}_b"]
    m["L0_xattn_W_q"], m["L0_xattn_W_c"] = a["L0_xattn_W_q"], a["L0_xattn_W_c"]
    m["L0_xattn_W_k"], m["L0_xattn_W_v"] = a["L0_xattn_W_kv"][:, :C], a["L0_xattn_W_kv"][:, C:]
    for n in ("gate", "up", "down"):
        m[f"L0_ffn_w_{n}T"] = a[f"L0_ffn_w_{n}"].T
    qkv = a["L1_attn_W_qkv"].reshape(C, -1, 3)
    for n, name in enumerate("qkv"):
        m[f"L1_attn_W_{name}"] = qkv[:, :, n]
    m["L1_attn_W_out"] = a["L1_attn_W_out"]
    for n in "qkvo":
        m[f"L1_xattn_W{n}T"] = a[f"L1_xattn_W{n}"].T
        m[f"L1_xattn_b{n}"] = a[f"L1_xattn_b{n}"]
    for n in ("router_W", "router_b", "W1", "b1", "W2", "b2"):
        m[f"L1_ffn_{n}"] = a[f"L1_ffn_{n}"]
    return {k: np.ascontiguousarray(v) for k, v in m.items()}


def program(nc, arrays, phases=None):
    a = {k: nc.dram_tensor(f"in_{k}", v.shape, mybir.dt.from_np(v.dtype), kind="ExternalInput").ap() for k, v in arrays.items()}
    out = nc.dram_tensor("out_x", (B * T, C), F32, kind="ExternalOutput").ap()
    build(nc, a, out, *([phases] if phases else []))


def kernel(**inputs):
    import concourse.bacc as bacc
    from concourse.bass_utils import run_bass_kernel_spmd

    arrays = laid_out(inputs)
    nc = bacc.Bacc("TRN2", target_bir_lowering=False, num_devices=1)
    program(nc, arrays)
    r = run_bass_kernel_spmd(nc, [{f"in_{k}": v for k, v in arrays.items()}], core_ids=[0])
    return r.results[0]["out_x"].reshape(B, T, C)
```

```python
from contextlib import ExitStack

import numpy as np

import concourse.bass as bass
from concourse import mybir

F32 = mybir.dt.float32
BF16 = mybir.dt.bfloat16
F32R = mybir.dt.float32r
I32 = mybir.dt.int32
U32 = mybir.dt.uint32
U8 = mybir.dt.uint8
ALU = mybir.AluOpType
ACT = mybir.ActivationFunctionType
AX = mybir.AxisListType

P = 128
B, T, C = 8, 512, 256
NT = T // P
KC = C // P
NX = B * NT
H = 16
EPS = 1e-5
MASKED = -1e9
NEG = -1e30


class Loop:

    def __init__(self, sem, per, before=0):
        self.sem, self.per, self.before = sem, per, before

    def credit(self, eng):
        if self.before:
            eng.wait_ge(self.sem, self.before)
        if self.per > self.before:
            eng.sem_inc(self.sem, self.per - self.before)

    def wait(self, eng, it, k):
        if it is not None:
            assert self.per + k > 0
            eng.wait_ge(self.sem, it * self.per + (self.per + k))
        elif k > 0:
            eng.wait_ge(self.sem, k)


class Space:

    def __init__(self, nc, ctx, name):
        self.nc, self.ctx, self.name, self.sems = nc, ctx, name, []

    def sb(self, name, shape, dt=F32):
        return self.ctx.enter_context(self.nc.sbuf_tensor(f"{self.name}_{name}", shape, dt))

    def ps(self, name, shape, dt=F32):
        return self.ctx.enter_context(self.nc.psum_tensor(f"{self.name}_{name}", shape, dt))

    def sem(self, name):
        self.sems.append(self.ctx.enter_context(self.nc.semaphore(f"{self.name}_{name}")))
        return self.sems[-1]

    def clear(self):
        with self.nc.Block() as block:
            @block.sync
            def _(sp):
                for sem in self.sems:
                    sp.sem_clear(sem)


def first_norm(nc, name, x_all, ident, h_tok, hT, tr):
    with ExitStack() as ctx:
        s = Space(nc, ctx, name + "_first")
        stats, mv, rstd = s.sb("stats", [P, NT, 6]), s.sb("mv", [P, NT, 2]), s.sb("rstd", [P, NT])
        half = s.sb("half", [P, NT])
        s_stats, s_mv, s_pool, s_h, s_tr, s_ev = (s.sem(n) for n in ("stats", "mv", "pool", "h", "tr", "ev"))
        with nc.Block() as block:
            @block.vector
            def _(dve):
                for i in range(NT):
                    dve.bn_stats(stats[:, i, :], x_all[:, i, :]).then_inc(s_stats, 1)
                dve.wait_ge(s_stats, NT)
                for i in range(NT):
                    dve.bn_aggr(mv[:, i, :], stats[:, i, :]).then_inc(s_mv, 1)
                dve.wait_ge(s_tr, 2)
                dve.tensor_copy(hT[:, 1, :], tr[:, 1, :]).then_inc(s_ev, 1)

            @block.gpsimd
            def _(pool):
                pool.memset(half[:, :], -0.5).then_inc(s_pool, 1)
                pool.wait_ge(s_mv, NT)
                pool.tensor_scalar(rstd[:, :], mv[:, :, 1], EPS, None, ALU.add).then_inc(s_pool, 1)
                pool.wait_ge(s_pool, 2)
                pool.tensor_tensor(rstd[:, :], rstd[:, :], half[:, :], ALU.pow).then_inc(s_pool, 1)
                pool.wait_ge(s_pool, 3)
                for i in range(NT):
                    pool.tensor_scalar(h_tok[:, i, :], x_all[:, i, :], mv[:, i, 0:1], rstd[:, i:i + 1],
                                       ALU.subtract, ALU.mult).then_inc(s_h, 1)

            @block.tensor
            def _(pe):
                pe.wait_ge(s_h, NT)
                for c in range(KC):
                    for i in range(NT):
                        t = pe.transpose(tr[:, c, i * P:(i + 1) * P], h_tok[:, i, c * P:(c + 1) * P], ident)
                    t.then_inc(s_tr, 1)

            @block.scalar
            def _(act):
                act.wait_ge(s_tr, 1)
                act.copy(hT[:, 0, :], tr[:, 0, :]).then_inc(s_ev, 1)
        s.clear()


def attention(nc, name, x_mem, consts, D, wq_d, wk_d, wv_d, wo_d, ctx_d=None, rope=None, bias_d=None,
              mask_d=None, window=False):
    G = P // D
    NC = H * D // P
    DP = max(D, 32)
    HG = P // DP
    NG = H // HG
    NU = H * NT
    ident, ident_bf = consts["ident"], consts["ident_bf"]
    scale = float(D) ** -0.5
    VW = min(512, H * D)
    VH = H * D // VW

    def keys(i):
        return (max(i - 1, 0) * P, P if i == 0 else 2 * P) if window else (0, T)

    T_LAG, PV_LAG, TURN_LAG = (3, 5, 12) if rope else (3, 4, 10)
    LAST_VALUE = NU + PV_LAG + NT - 2
    NV = NT * VH
    late = ctx_d is not None
    norm_at = 13 if late else NU - 12
    prep = {2: [("stat", 0)], 6: [("htok", 0)], norm_at: [("norm", c) for c in range(KC)]}
    if mask_d is not None:
        prep[norm_at + 1] = [("mask", 0)]
    same = {}
    for n in range(2 * NC) if rope else range(2 * NC - 1, -1, -1):
        if rope:
            prep.setdefault(16 + 4 * n, []).append(("qk", n))
            prep.setdefault(20 + 4 * n, []).append(("rot", n))
        else:
            to, slot = (prep, NU) if n < 2 else (same, NU // NC * (n // 2))
            to.setdefault(slot - NU // NC + 2 * (1 - n % 2), []).append(("qk", n))
    if not late:
        for n in range(NV // 2):
            prep.setdefault(LAST_VALUE + 1 + n * (TURN_LAG + NU - LAST_VALUE - 1) // NV * 2, []).append(("v", n))

    def plan(which):
        steps = []
        for slot in range(NU + TURN_LAG):
            if which != "first":
                if slot < NU:
                    steps.append(("score", slot))
                if 0 <= slot - T_LAG < NU:
                    steps.append(("flip", slot - T_LAG))
                u = slot - PV_LAG - NT * HG + 1
                if 0 <= u < NU and u % (NT * HG) < NT:
                    steps.append(("value", u // (NT * HG) * NT + u % (NT * HG)))
                if late and 3 <= slot < 3 + NV:
                    steps.append(("v", slot - 3))
                if late and 3 + NV <= slot < 3 + NV + NC:
                    steps.append(("back", slot - 3 - NV))
                if late and 5 + NV + NC <= slot < 5 + NV + NC + NT:
                    steps.append(("out", slot - 5 - NV - NC))
            if which != "first":
                steps += same.get(slot, [])
            if which != "last":
                steps += prep.get(slot, [])
            u = slot - TURN_LAG + 1
            if which != "first" and 0 <= u < NU and u % (NT * HG) == NT * HG - 1:
                steps.append(("turn", u // (NT * HG)))
        own = not late and which != "first" or which == "last"
        if not late and which != "last":
            steps += [("v", n) for n in range(NV // 2, NV * 3 // 4)]
        steps += [("own_back", c) for c in range(NC)] if own else []
        if not late and which != "last":
            steps += [("v", n) for n in range(NV * 3 // 4, NV)]
        return steps + ([("own_out", i) for i in range(NT)] if own else [])

    SR, WR, OPR = 3, 4, 1
    PR = 4

    def drained_by(kind, n):
        if kind == "qk":
            return "act" if rope else "dve"
        if kind in ("rot", "turn", "out", "own_out") or (kind == "norm" and not rope) or (kind == "v" and bias_d):
            return "dve"
        return "dve" if n % 2 else "act"

    def numbered(steps):
        ring = [st for st in steps if st[0] not in ("score", "value", "stat", "htok", "mask")]
        order = {e: [st for st in ring if drained_by(*st) == e] for e in ("act", "dve")}
        return {st: n for n, st in enumerate(ring)}, order, {st: order[e].index(st) + 1 for e in order for st in order[e]}

    class Plan:

        def __init__(self, which, prev=None):
            self.steps = plan(which)
            self.place, self.order, self.nth = numbered(self.steps)
            self.ring = sorted(self.place, key=self.place.get)
            self.highs = [st for st in self.steps if st[0] in ("qk", "norm")]
            self.prev = prev or self

    whole = Plan("loop")
    first, last = Plan("first", whole), Plan("last", whole)

    with ExitStack() as ctx:
        s = Space(nc, ctx, name)
        h_tok = s.sb("h_tok", [P, NT, C]) if late else x_mem[:, 0:NT, :]
        hT = s.sb("hT", [P, KC, T]) if rope else None
        wq, wk, wv = (s.sb(n, [P, KC, H * D], F32 if rope else F32R) for n in ("wq", "wk", "wv"))
        wo = s.sb("wo", [P, NC, C])
        if rope:
            qs, ks = s.sb("qs", [P, H, T], BF16), s.sb("ks", [P, H, T], BF16)
            parts = s.sb("parts", [P, 2 * NC, 3, T], BF16)
            parts_d = nc.dram_tensor(f"{name}_parts_dram", (2 * NC, 3, P, T), BF16, kind="Internal").ap()
        else:
            wq_lo, wk_lo, wv_lo = (s.sb(n + "_lo", [P, KC, H * D], F32R) for n in ("wq", "wk", "wv"))
            hT_hi, hT_lo = s.sb("hT_hi", [P, KC, T], F32R), s.sb("hT_lo", [P, KC, T], F32R)
            qp, kp = s.sb("qp", [P, 4, T], F32R), s.sb("kp", [P, 4, 2, T], F32R)
        V = s.sb("V", [P, NT, H, DP])
        Pr = s.sb("Pr", [P, PR, T])
        PTN = HG + (1 if rope else 2)
        PT = s.sb("PT", [P, PTN, NT * (2 * P if window else T)])
        nmax, sums, rinv = s.sb("nmax", [P, NU]), s.sb("sums", [P, NU]), s.sb("rinv", [P, NU])
        Oraw = s.sb("Oraw", [P, 2, T])
        O = s.sb("O", [P, NT, H * D])
        if late:
            OT = s.sb("OT", [P, NC, T])
        else:
            OT = PT[:, :, :].rearrange("p n k -> p (n k)")[:, 0:NC * T].rearrange("p (c t) -> p c t", t=T)
        stats, mv, rstd, half, eps = s.sb("stats", [P, NT, 6]), s.sb("mv", [P, NT, 2]), s.sb("rstd", [P, NT]), s.sb("half", [P, NT]), s.sb("eps", [P, NT])
        if ctx_d is not None:
            cT = s.sb("cT", [P, KC, T])
        if rope:
            cos, sin, turnm = s.sb("cos", [P, T]), s.sb("sin", [P, T]), s.sb("turnm", [P, P])
            rows, rsin = s.sb("rows", [P, 2 * NC, T]), s.sb("rsin", [P, 2 * NC, T])
        if bias_d:
            bqk, bv, bo = s.sb("bqk", [P, 2 * NC]), s.sb("bv", [P, C]), s.sb("bo", [P, C])
            bqs = s.sb("bqs", [P, NC])
            ysum = s.sb("ysum", [P, C])
        if mask_d is not None:
            m8, mrow, qrow, krow = s.sb("m8", [P, B, T], U8), s.sb("mrow", [P, T], BF16), s.sb("qrow", [1, T], BF16), s.sb("krow", [1, T], BF16)
        if window:
            band, band32 = s.sb("band", [P, 2 * P], BF16), s.sb("band32", [P, 2 * P])
        S = s.ps("S", [P, SR, 512])
        W = s.ps("W", [P, WR, 512])
        OP = s.ps("OP", [P, OPR, 512])

        s_load, s_set = s.sem("load"), s.sem("set")
        s_fix, s_cast, s_fence = s.sem("fix"), s.sem("cast"), s.sem("fence")
        s_weight, s_low = [s.sem(f"weight{n}") for n in range(0 if rope else 3)], s.sem("low")
        s_fence_pool, s_fence_sp = s.sem("fence_pool"), s.sem("fence_sp")
        ring_full = Loop(s.sem("ring_full"), len(whole.place), len(first.place))
        drained = {e: Loop(s.sem("drained_" + e), len(whole.order[e]), len(first.order[e])) for e in ("act", "dve")}
        scored = Loop(s.sem("scored"), NU)
        maxed = Loop(s.sem("maxed"), NU)
        exped = Loop(s.sem("exped"), NU)
        valued = Loop(s.sem("valued"), NG)
        lifted = Loop(s.sem("lifted"), NG)
        inverted = Loop(s.sem("inverted"), NG)
        normed = Loop(s.sem("normed"), NT, NT)
        s_stat = Loop(s.sem("stat"), 2 * NT, 2 * NT)
        rooted = Loop(s.sem("rooted"), 2, 2)
        split_high = Loop(s.sem("split_high"), 2 * NC + KC, 2 + KC)
        doubled = Loop(s.sem("doubled"), 2 * NC, 2)
        kv_read = Loop(s.sem("kv_read"), 2 if late else 1, 1)
        s_ctx = Loop(s.sem("ctx"), 16, 16)
        masked = Loop(s.sem("masked"), 3, 3)
        biased = Loop(s.sem("biased"), NT)
        if rope:
            pool_ops = [(n, o) for n in range(2 * NC) for o in ("cos", "add", "mask", "high", "rest", "middle", "low")
                        if o != "mask" or (mask_d is not None and n % 2 == 0)]
            nth_pool = {op: n + 1 for n, op in enumerate(pool_ops)}
            pooled = Loop(s.sem("pooled"), len(pool_ops), len(pool_ops))
            spilled = Loop(s.sem("spilled"), 16 * 2 * NC, 16 * 2 * NC)
            NL = 12 + (2 if mask_d is not None else 0)
            stacked = [Loop(s.sem(f"stacked{c}"), 16 * NL, 16 * NL) for c in range(NC)]
            KS = 6 * D + (1 if mask_d is not None else 0)

        loads = 16 * ((4 if rope else 1) + (3 if rope else 0) + (2 * NC + 2 if bias_d else 0) + (1 if window else 0) + (1 if mask_d is not None else 0))
        if rope:
            weights = [w[:, :, :] for w in (wq, wk, wv)]
        else:
            room = PT[:, :, :].rearrange("p n k -> p (n k)")
            weights = [room[:, n * KC * H * D:(n + 1) * KC * H * D].rearrange("p (k n) -> p k n", k=KC) for n in range(3)]
        with nc.Block() as block:
            @block.sync
            def _(sp):
                for n, (t, d) in enumerate(zip(weights, (wq_d, wk_d, wv_d))):
                    sp.dma_start(t, d.rearrange("(k p) n -> p k n", p=P)).then_inc(s_load if rope else s_weight[n], 16)
                sp.dma_start(wo[:, :, :], wo_d.rearrange("(k p) n -> p k n", p=P)).then_inc(s_load, 16)
                if rope:
                    for t, d in zip((cos, sin, turnm), rope):
                        sp.dma_start(t[:, :], d).then_inc(s_load, 16)
                if bias_d:
                    for n, d in enumerate(bias_d[:2]):
                        for c in range(NC):
                            sp.dma_start(bqk[:, n * NC + c:n * NC + c + 1], d[c * P:(c + 1) * P].unsqueeze(1)).then_inc(s_load, 16)
                    sp.dma_start(bv[:, :], bias_d[2].unsqueeze(0).partition_broadcast(P)).then_inc(s_load, 16)
                    sp.dma_start(bo[:, :], bias_d[3].unsqueeze(0).partition_broadcast(P)).then_inc(s_load, 16)
                if window:
                    sp.dma_start(band32[:, :], consts["band_d"]).then_inc(s_load, 16)
                if mask_d is not None:
                    sp.dma_start(m8[:, 0:B, :], mask_d.unsqueeze(0).partition_broadcast(P)).then_inc(s_load, 16)

            @block.vector
            def _(dve):
                dve.memset(half[:, :], -0.5).then_inc(s_set, 1)
                dve.memset(eps[:, :], EPS).then_inc(s_set, 1)
                if late:
                    dve.memset(O[:, :, :], 0.0).then_inc(s_set, 1)
                if DP != D:
                    dve.memset(V[:, :, :, D:DP], 0.0).then_inc(s_set, 1)

        src = cT if ctx_d is not None else hT

        def projection(pe, dst, pairs):
            ops = [op for lhs, rhs in pairs for op in
                   ([(lhs[0], rhs[0])] if len(lhs) == 1 else [(lhs[0], rhs[0]), (lhs[0], rhs[1]), (lhs[1], rhs[0])])]
            for n, (lhs, rhs) in enumerate(ops):
                m = pe.matmul(dst, lhs, rhs, start=(n == 0), stop=(n == len(ops) - 1))
            return m

        def flip_copy(copy, b, n, src_, eng):
            h, i = n // NT, n % NT
            valued.wait(eng, b, (h - PTN) // HG + 1)
            if window:
                _, kn = keys(i)
                a = 2 * P * i - (kn - P)
                return copy(PT[:, h % PTN, a:a + kn], src_[:, 0:kn])
            o = PT[:, h % PTN, :].rearrange("p (k q) -> p k q", q=T)[:, :, i * P:(i + 1) * P]
            return copy(o, src_.rearrange("p (k q) -> p k q", q=P))

        def next_x(b, i):
            if b is None:
                return x_mem[:, NT + i, :]
            return x_mem[:, bass.ds(b * NT + (2 * NT + i), 1), :].rearrange("p a c -> p (a c)")

        def tensor_steps(pe, b, plan):
            place, order, nth, prev = plan.place, plan.order, plan.nth, plan.prev

            def bank(st):
                n = place[st]
                if n >= WR:
                    before = plan.ring[n - WR]
                    e = drained_by(*before)
                    drained[e].wait(pe, b, nth[before])
                else:
                    before = [st for m, st in enumerate(prev.ring) if m % WR == n][-1]
                    e = drained_by(*before)
                    drained[e].wait(pe, b, prev.nth[before] - drained[e].per)
                return W[:, n % WR, :]

            for kind, n in plan.steps:
                if kind == "norm":
                    dst = bank((kind, n))
                    normed.wait(pe, b, NT)
                    for i in range(NT):
                        m = pe.transpose(dst[:, i * P:(i + 1) * P], h_tok[:, i, n * P:(n + 1) * P], ident)
                    m.then_inc(ring_full.sem, 1)
                elif kind == "qk":
                    which, c = n % 2, n // 2
                    if b is None and n == 0:
                        pe.wait_ge(s_load, loads)
                    if b is None and n == 1 and not rope:
                        pe.wait_ge(s_load, loads)
                        pe.wait_ge(s_low, 3)
                    if c == 0 and which == (0 if rope else 1):
                        for k in range(KC):
                            drained[drained_by("norm", k)].wait(pe, b, nth[("norm", k)])
                    if n == 1 and ctx_d is not None:
                        s_ctx.wait(pe, b, 16)
                    if rope:
                        w, rhs = ((wq,), (hT,)) if which == 0 else ((wk,), (src,))
                    else:
                        w, rhs = ((wq, wq_lo), (wk, wk_lo))[which], (hT_hi, hT_lo)
                    dst = bank((kind, n))
                    m = projection(pe, dst, [([t[:, kc, c * P:(c + 1) * P] for t in w], [t[:, kc, :] for t in rhs])
                                             for kc in range(KC)])
                    m.then_inc(ring_full.sem, 1)
                    if late and n == 2 * NC - 1:
                        pe.drain().then_inc(kv_read.sem, 1)
                elif kind == "v":
                    i, v = n // VH, n % VH
                    dst = bank((kind, n))
                    lhs, rhs = ((src,), (wv,)) if rope else ((hT_hi, hT_lo), (wv, wv_lo))
                    m = projection(pe, dst[:, 0:VW], [([t[:, kc, i * P:(i + 1) * P] for t in lhs],
                                                       [t[:, kc, v * VW:(v + 1) * VW] for t in rhs]) for kc in range(KC)])
                    m.then_inc(ring_full.sem, 1)
                    if n == NV - 1:
                        pe.drain().then_inc(kv_read.sem, 1)
                elif kind == "rot":
                    dst = bank((kind, n))
                    drained["act"].wait(pe, b, nth[("qk", n)])
                    pe.matmul(dst, turnm[:, :], rows[:, n, :], start=True, stop=True).then_inc(ring_full.sem, 1)
                elif kind == "score":
                    h, i = n // NT, n % NT
                    c = h // G
                    k0, kn = keys(i)
                    if n == c * G * NT:
                        if rope:
                            stacked[c].wait(pe, b, 0)
                        else:
                            doubled.wait(pe, b, 2 * c)
                            st = ("qk", 2 * c)
                            drained["dve"].wait(pe, b, nth[st] if c else prev.nth[st] - drained["dve"].per)
                    exped.wait(pe, b, n + 1 - SR)
                    if rope:
                        m = pe.matmul(S[:, n % SR, 0:kn], qs[0:KS, h, i * P:(i + 1) * P], ks[0:KS, h, k0:k0 + kn],
                                      start=True, stop=not window)
                    else:
                        for part in range(2):
                            m = pe.matmul(S[:, n % SR, :], qp[:, h % 4, i * P:(i + 1) * P], kp[:, h % 4, part, :],
                                          start=(part == 0), stop=(part == 1))
                    if window:
                        m = pe.matmul(S[:, n % SR, 0:kn], ident_bf, band[:, 2 * P - kn:2 * P], start=False, stop=True)
                    m.then_inc(scored.sem, 1)
                elif kind == "flip":
                    _, kn = keys(n % NT)
                    dst = bank((kind, n))
                    exped.wait(pe, b, n + 1)
                    for k in range(kn // P):
                        m = pe.transpose(dst[:, k * P:(k + 1) * P], Pr[:, n % PR, k * P:(k + 1) * P], ident)
                    m.then_inc(ring_full.sem, 1)
                elif kind == "value":
                    g, nk = n // NT, n % NT
                    k = (0, 2, 1, 3)[nk] if window else nk
                    if n == 0 and not late:
                        for e in order:
                            v_last = max(prev.nth[st] for st in prev.order[e] if st[0] == "v")
                            drained[e].wait(pe, b, v_last - drained[e].per)
                    if nk == 0:
                        last = NT * HG * (g + 1) - 1
                        for u in (last - 1, last):
                            e = drained_by("flip", u)
                            drained[e].wait(pe, b, nth[("flip", u)])
                        lifted.wait(pe, b, g + 1 - OPR)
                    q0, qn = (k * P, min(2 * P, T - k * P)) if window else (0, T)
                    p0 = k * (2 * P) if window else k * T
                    for j in range(HG):
                        h = g * HG + j
                        m = pe.matmul(OP[DP * j:DP * (j + 1), g % OPR, q0:q0 + qn], V[:, k, h, :],
                                      PT[:, h % PTN, p0:p0 + qn], start=(nk == 0), stop=(nk == NT - 1),
                                      skip_group_check=True)
                    if nk == NT - 1:
                        m.then_inc(valued.sem, 1)
                elif kind == "turn":
                    dst = bank((kind, n))
                    lifted.wait(pe, b, n + 1)
                    for i in range(NT):
                        m = pe.transpose(dst[:, i * P:(i + 1) * P], Oraw[:, n % 2, i * P:(i + 1) * P], ident)
                    m.then_inc(ring_full.sem, 1)
                elif kind in ("back", "own_back"):
                    dst = bank((kind, n))
                    if kind == "back":
                        drained["dve"].wait(pe, b, prev.nth[("turn", NG - 1)] - drained["dve"].per)
                    else:
                        drained["dve"].wait(pe, b, nth[("turn", NG - 1)])
                    for i in range(NT):
                        m = pe.transpose(dst[:, i * P:(i + 1) * P], O[:, i, n * P:(n + 1) * P], ident)
                    m.then_inc(ring_full.sem, 1)
                elif kind in ("out", "own_out"):
                    dst = bank((kind, n))
                    if n == 0:
                        for e in order:
                            backs = [nth[st] for st in order[e] if st[0] == kind.replace("out", "back")]
                            drained[e].wait(pe, b, max(backs))
                    for c in range(NC):
                        m = pe.matmul(dst[:, 0:C], OT[:, c, n * P:(n + 1) * P], wo[:, c, :],
                                      start=(c == 0), stop=(c == NC - 1))
                    m.then_inc(ring_full.sem, 1)

        def scalar_steps(act, b, plan):
            place, order, nth, prev = plan.place, plan.order, plan.nth, plan.prev
            for kind, n in plan.steps:
                st = (kind, n)
                if kind == "score":
                    _, kn = keys(n % NT)
                    maxed.wait(act, b, n + 1)
                    f = ("flip", n - PR if n >= PR else NU + n - PR)
                    ring_full.wait(act, b, place[f] + 1 if n >= PR else prev.place[f] + 1 - ring_full.per)
                    act.activation(Pr[:, n % PR, 0:kn], S[:, n % SR, 0:kn], ACT.Exp, bias=nmax[:, n:n + 1],
                                   accum_out=sums[:, n:n + 1]).then_inc(exped.sem, 1)
                    continue
                if kind == "value":
                    g = n // NT
                    if n % NT == NT - 1:
                        valued.wait(act, b, g + 1)
                        if g < 2:
                            ring_full.wait(act, b, prev.place[("turn", NG + g - 2)] + 1 - ring_full.per)
                        else:
                            ring_full.wait(act, b, place[("turn", g - 2)] + 1)
                        act.copy(Oraw[:, g % 2, :], OP[:, g % OPR, :]).then_inc(lifted.sem, 1)
                    continue
                if kind == "qk" and not rope:
                    ring_full.wait(act, b, place[st] + 1)
                    part = W[:, place[st] % WR, :]
                    for r in range(2):
                        at, h4 = slice(r * D, (r + 1) * D), (n // 2 * 2 + r) % 4
                        if n % 2 == 0:
                            m = act.activation(qp[at, h4, :], part[at, :], ACT.Identity, scale=scale)
                        else:
                            m = act.copy(kp[at, h4, 0, :], part[at, :])
                    m.then_inc(split_high.sem, 1)
                    continue
                if b is None and st == ("norm", 0) and not rope:
                    for w, hi, loaded in zip(weights, (wq, wk, wv), s_weight):
                        act.wait_ge(loaded, 16)
                        act.copy(hi[:, :, :], w).then_inc(s_cast, 1)
                if kind == "norm" and not rope:
                    ring_full.wait(act, b, place[st] + 1)
                    act.copy(hT_hi[:, n, :], W[:, place[st] % WR, :]).then_inc(split_high.sem, 1)
                    continue
                if st not in place or drained_by(*st) != "act":
                    continue
                ring_full.wait(act, b, place[st] + 1)
                src_ = W[:, place[st] % WR, :]
                done = drained["act"].sem
                if kind == "qk" and rope:
                    which, c = n % 2, n // 2
                    if b is None and n == 0 and bias_d:
                        act.wait_ge(s_load, loads)
                        act.activation(bqs[:, :], bqk[:, 0:NC], ACT.Identity, scale=scale).then_inc(s_fix, 1)
                        act.wait_ge(s_fix, 1)
                    if bias_d:
                        bias = bqs[:, c:c + 1] if which == 0 else bqk[:, NC + c:NC + c + 1]
                    else:
                        bias = 0.0
                    pooled.wait(act, b, nth_pool[(n, "low")] - pooled.per)
                    act.activation(rows[:, n, :], src_, ACT.Identity, bias=bias,
                                   scale=scale if which == 0 else 1.0).then_inc(done, 1)
                elif kind == "v":
                    i, v = n // VH, n % VH
                    hs = VW // D
                    o = V[:, i, v * hs:(v + 1) * hs, 0:D]
                    act.copy(o, src_[:, 0:VW].rearrange("p (h d) -> p h d", d=D)).then_inc(done, 1)
                elif kind == "flip":
                    flip_copy(act.copy, b, n, src_, act).then_inc(done, 1)
                elif kind == "norm":
                    act.copy(hT[:, n, :], src_).then_inc(done, 1)
                elif kind in ("back", "own_back"):
                    act.copy(OT[:, n, :], src_).then_inc(done, 1)

        def vector_steps(dve, b, plan):
            place, order, nth, prev = plan.place, plan.order, plan.nth, plan.prev
            for kind, n in plan.steps:
                st = (kind, n)
                if kind == "score":
                    _, kn = keys(n % NT)
                    scored.wait(dve, b, n + 1)
                    dve.tensor_reduce(nmax[:, n:n + 1], S[:, n % SR, 0:kn], AX.X, ALU.max, negate=True).then_inc(maxed.sem, 1)
                elif kind == "stat":
                    for i in range(NT):
                        dve.bn_stats(stats[:, i, :], next_x(b, i)).then_inc(s_stat.sem, 1)
                    s_stat.wait(dve, b, NT)
                    dve.sem_inc(s_fence, 1)
                    for i in range(NT):
                        dve.bn_aggr(mv[:, i, :], stats[:, i, :]).then_inc(s_stat.sem, 1)
                elif kind == "mask":
                    if b is None:
                        dve.wait_ge(s_load, loads)
                    pooled.wait(dve, b, nth_pool[(2 * NC - 2, "mask")] - pooled.per)
                    m = m8[:, 0, :] if b is None else m8[:, bass.ds(b + 1, 1), :].rearrange("p a t -> p (a t)")
                    dve.tensor_copy(mrow[:, :], m).then_inc(masked.sem, 1)
                    masked.wait(dve, b, 1)
                    for c in range(NC):
                        stacked[c].wait(dve, b, 0)
                    dve.tensor_copy(qrow[0:1, :], mrow[0:1, :]).then_inc(masked.sem, 1)
                    dve.tensor_scalar(krow[0:1, :], mrow[0:1, :], -MASKED, MASKED, ALU.mult, ALU.add).then_inc(masked.sem, 1)
                elif kind == "htok":
                    rooted.wait(dve, b, 2)
                    for c in range(KC):
                        ring_full.wait(dve, b, prev.place[("norm", c)] + 1 - ring_full.per)
                    for i in range(NT):
                        dve.tensor_scalar(h_tok[:, i, :], next_x(b, i), mv[:, i, 0:1], rstd[:, i:i + 1],
                                          ALU.subtract, ALU.mult).then_inc(normed.sem, 1)
                    if b is None and not rope:
                        for n, (w, lo, hi) in enumerate(zip(weights, (wq_lo, wk_lo, wv_lo), (wq, wk, wv))):
                            dve.wait_ge(s_cast, n + 1)
                            dve.tensor_tensor(lo[:, :, :], w, hi[:, :, :].bitcast(F32), ALU.subtract).then_inc(s_low, 1)
                if st not in place or drained_by(*st) != "dve":
                    continue
                ring_full.wait(dve, b, place[st] + 1)
                src_ = W[:, place[st] % WR, :]
                done = drained["dve"].sem
                if kind == "qk":
                    split_high.wait(dve, b, plan.highs.index(st) + 1)
                    for r in range(2):
                        at, other, h4 = slice(r * D, (r + 1) * D), slice((1 - r) * D, (2 - r) * D), (n // 2 * 2 + r) % 4
                        if n % 2 == 0:
                            m = dve.scalar_tensor_tensor(out=qp[other, h4, :], in0=src_[at, :], scalar=scale,
                                                         in1=qp[at, h4, :].bitcast(F32), op0=ALU.mult, op1=ALU.subtract)
                        else:
                            m = dve.tensor_tensor(kp[at, h4, 1, :], src_[at, :], kp[at, h4, 0, :].bitcast(F32), ALU.subtract)
                    m.then_inc(done, 1)
                elif kind == "v":
                    i, v = n // VH, n % VH
                    hs = VW // D
                    o = V[:, i, v * hs:(v + 1) * hs, 0:D]
                    if bias_d:
                        dve.tensor_tensor(o, src_[:, 0:VW].rearrange("p (h d) -> p h d", d=D),
                                          bv[:, :].rearrange("p (h d) -> p h d", d=D), ALU.add).then_inc(done, 1)
                    else:
                        dve.tensor_copy(o, src_[:, 0:VW].rearrange("p (h d) -> p h d", d=D)).then_inc(done, 1)
                elif kind == "rot":
                    if b is None and n == 0:
                        dve.wait_ge(s_load, loads)
                        if window:
                            dve.tensor_copy(band[:, :], band32[:, :]).then_inc(s_cast, 1)
                    pooled.wait(dve, b, nth_pool[(n, "add")] - pooled.per)
                    dve.tensor_tensor(rsin[:, n, :], src_, sin[:, :], ALU.mult).then_inc(done, 1)
                elif kind == "flip":
                    flip_copy(dve.tensor_copy, b, n, src_, dve).then_inc(done, 1)
                elif kind == "turn":
                    u0, nu = n * HG * NT, HG * NT
                    exped.wait(dve, b, u0 + nu)
                    dve.reciprocal(rinv[:, u0:u0 + nu], sums[:, u0:u0 + nu]).then_inc(inverted.sem, 1)
                    inverted.wait(dve, b, n + 1)
                    r = rinv[:, u0:u0 + nu].rearrange("p (h i) -> p i h", i=NT)
                    for j in range(HG):
                        last = dve.tensor_tensor(
                            O[:, :, (n * HG + j) * D:(n * HG + j + 1) * D],
                            src_.rearrange("p (i h d) -> p i h d", i=NT, d=DP)[:, :, j, 0:D],
                            r[:, :, j:j + 1].to_broadcast([P, NT, D]), ALU.mult)
                    last.then_inc(done, 1)
                elif kind == "norm" and not rope:
                    split_high.wait(dve, b, plan.highs.index(st) + 1)
                    dve.tensor_tensor(hT_lo[:, n, :], src_, hT_hi[:, n, :].bitcast(F32), ALU.subtract).then_inc(done, 1)
                elif kind == "norm":
                    dve.tensor_copy(hT[:, n, :], src_).then_inc(done, 1)
                elif kind in ("back", "own_back"):
                    dve.tensor_copy(OT[:, n, :], src_).then_inc(done, 1)
                elif kind in ("out", "own_out"):
                    tile = b * NT + (n if kind == "out" else NT + n)
                    xt = x_mem[:, bass.ds(tile, 1), :].rearrange("p a c -> p (a c)")
                    if bias_d:
                        dve.tensor_tensor(ysum[:, :], src_[:, 0:C], bo[:, :], ALU.add).then_inc(biased.sem, 1)
                        biased.wait(dve, b, n + 1 + (NT if kind == "own_out" else 0))
                        dve.tensor_tensor(xt, ysum[:, :], xt, ALU.add).then_inc(done, 1)
                        drained["dve"].wait(dve, b, nth[st])
                    else:
                        dve.tensor_tensor(xt, src_[:, 0:C], xt, ALU.add).then_inc(done, 1)

        def gpsimd_steps(pool, b, plan):
            nth = plan.nth
            if plan is not last:
                s_stat.wait(pool, b, 2 * NT)
                if not rope:
                    doubled.wait(pool, b, 0)
                pool.tensor_tensor(rstd[:, :], mv[:, :, 1], eps[:, :], ALU.add).then_inc(rooted.sem, 1)
                rooted.wait(pool, b, 1)
                pool.tensor_tensor(rstd[:, :], rstd[:, :], half[:, :], ALU.pow).then_inc(rooted.sem, 1)
                if not rope:
                    rooted.wait(pool, b, 2)
            chunks = [] if rope else [st[1] // 2 for st in plan.steps if st[0] == "qk" and st[1] % 2]
            for n, c in enumerate(chunks):
                drained["dve"].wait(pool, b, nth[("qk", 2 * c + 1)])
                for r in range(2):
                    at, other = slice(r * D, (r + 1) * D), slice((1 - r) * D, (2 - r) * D)
                    doubled.wait(pool, b, 2 * n + r)
                    pool.sem_inc(s_fence_pool, 1)
                    pool.tensor_copy(kp[other, (2 * c + r) % 4, :, :], kp[at, (2 * c + r) % 4, :, :]).then_inc(doubled.sem, 1)
            if rope and b is None:
                pool.wait_ge(s_load, loads)
            for k, (n, o) in enumerate(pool_ops if rope else ()):
                high, middle, low = (parts[:, n, e, :] for e in range(3))
                row = rows[:, n, :]
                pooled.wait(pool, b, k)
                if o == "cos":
                    drained["dve"].wait(pool, b, nth[("rot", n)])
                    ins = pool.tensor_tensor(row, row, cos[:, :], ALU.mult)
                elif o == "add":
                    ins = pool.tensor_tensor(row, row, rsin[:, n, :], ALU.add)
                elif o == "mask":
                    masked.wait(pool, b, 1)
                    ins = pool.tensor_tensor(row, row, mrow[:, :], ALU.mult)
                elif o == "high":
                    spilled.wait(pool, b, 16 * (n + 1) - spilled.per)
                    pool.sem_inc(s_fence_pool, 1)
                    ins = pool.tensor_copy(high, row)
                elif o == "rest":
                    ins = pool.tensor_tensor(row, row, high, ALU.subtract)
                elif o == "middle":
                    pool.sem_inc(s_fence_pool, 1)
                    ins = pool.tensor_copy(middle, row)
                else:
                    ins = pool.tensor_tensor(low, row, middle, ALU.subtract)
                ins.then_inc(pooled.sem, 1)

        def sync_steps(sp, b):
            def wait(loop, k):
                loop.wait(sp, b, k)
                sp.sem_inc(s_fence_sp, 1)

            if b is not None:
                wait(kv_read, 1)
            sp.dma_start(cT[:, :, :], context(0 if b is None else b + 1)).then_inc(s_ctx.sem, 16)
            for c in range(NC):
                wait(stacked[c], 0)
                for n in (2 * c, 2 * c + 1):
                    wait(pooled, nth_pool[(n, "low")])
                    sp.dma_start(parts_d[n].rearrange("e p t -> p e t"), parts[:, n, :, :]).then_inc(spilled.sem, 16)
                wait(spilled, 32 * (c + 1))
                if b is not None:
                    wait(scored, (c + 1) * G * NT)
                heads = slice(c * G, (c + 1) * G)
                for which, (stack, terms) in enumerate(((qs, (0, 0, 0, 1, 1, 2)), (ks, (0, 1, 2, 0, 1, 0)))):
                    for j, e in enumerate(terms):
                        sp.dma_start(stack[j * D:(j + 1) * D, heads, :],
                                     parts_d[2 * c + which, e].rearrange("(h d) t -> d h t", d=D)).then_inc(stacked[c].sem, 16)
                if mask_d is not None:
                    wait(masked, 3)
                    for stack, row in ((qs, qrow), (ks, krow)):
                        sp.dma_start(stack[6 * D:6 * D + 1, heads, :],
                                     row[0:1, :].unsqueeze(1).to_broadcast([1, G, T])).then_inc(stacked[c].sem, 16)

        def context(b):
            return ctx_d[b].rearrange("(k p) t -> p k t", p=P) if isinstance(b, int) else \
                ctx_d[bass.ds(b, 1), :, :].rearrange("a (k p) t -> p (a k) t", p=P)

        with nc.Block() as block:
            @block.tensor
            def _(pe):
                tensor_steps(pe, None, first)
                if window:
                    pe.wait_ge(s_cast, 1)
                for sem in (ring_full, kv_read, scored, valued):
                    sem.credit(pe)
                with pe.Fori(0, B - 1) as b:
                    tensor_steps(pe, b, whole)
                tensor_steps(pe, B - 1, last)

            @block.scalar
            def _(act):
                scalar_steps(act, None, first)
                for sem in (drained["act"], exped, lifted) + (() if rope else (split_high,)):
                    sem.credit(act)
                with act.Fori(0, B - 1) as b:
                    scalar_steps(act, b, whole)
                scalar_steps(act, B - 1, last)

            @block.vector
            def _(dve):
                vector_steps(dve, None, first)
                for sem in (drained["dve"], s_stat, normed, maxed, inverted, biased) + ((masked,) if mask_d is not None else ()):
                    sem.credit(dve)
                with dve.Fori(0, B - 1) as b:
                    vector_steps(dve, b, whole)
                vector_steps(dve, B - 1, last)

            @block.gpsimd
            def _(pool):
                gpsimd_steps(pool, None, first)
                for sem in (rooted, pooled if rope else doubled):
                    sem.credit(pool)
                with pool.Fori(0, B - 1) as b:
                    gpsimd_steps(pool, b, whole)
                if not rope:
                    gpsimd_steps(pool, B - 1, last)

            if rope:
                @block.sync
                def _(sp):
                    sync_steps(sp, None)
                    with sp.Fori(0, B - 1) as b:
                        sync_steps(sp, b)
        s.clear()




class Ring:

    def __init__(self, s, tensor, banks, steps, drained_by, before=None):
        self.tensor, self.banks, self.steps = tensor, banks, steps
        self.before = before or self
        self.who = [drained_by(*st) for st in steps]
        self.place = {st: n for n, st in enumerate(steps)}
        self.engines = sorted(set(self.who))
        self.nth, seen = {}, {e: 0 for e in self.engines}
        for st, e in zip(steps, self.who):
            seen[e] += 1
            self.nth[st] = seen[e]
        self.full = before.full if before else Loop(s.sem("ring_full"), len(steps))
        self.drained = before.drained if before else {e: Loop(s.sem("drained_" + e), seen[e]) for e in self.engines}

    def engine(self, st):
        return self.who[self.place[st]]

    def bank(self, st):
        return self.tensor[:, self.place[st] % self.banks, :]

    def free_bank(self, pe, it, st):
        n = self.place[st]
        if n >= self.banks:
            self.wait_drained(pe, it, self.steps[n - self.banks])
        else:
            last = max(m for m in range(len(self.before.steps)) if m % self.banks == n)
            self.before.wait_drained(pe, it, self.before.steps[last], -1)
        return self.bank(st)

    def wait_full(self, eng, it, st, iterations=0):
        self.full.wait(eng, it, self.place[st] + 1 + iterations * self.full.per)

    def wait_drained(self, eng, it, st, iterations=0):
        d = self.drained[self.engine(st)]
        d.wait(eng, it, self.nth[st] + iterations * d.per)


LOOKBACK, TOPK, PHRASE = 64, 16, 32
BAND = LOOKBACK + P
GONE = -3e38


def band_attention(nc, x_mem, consts, a):
    ident = consts["ident"]
    scale = float(C) ** -0.5
    def attending(h):
        two = (2 * h, 2 * h + 1)
        return ([("exp", n) for n in two] + [("weigh", h)], [("flip", n) for n in two], [("out", n) for n in two])

    (weigh0, flip0, out0), (weigh1, flip1, out1) = attending(0), attending(1)
    proj = [("proj", n) for n in range(3 * KC)]
    order = proj[:2] + weigh0 + [("stat", 0)] + proj[2:4] + flip0 + proj[4:5] + out0 + weigh1 + [("htok", 0)]
    order += flip1 + proj[5:] + out1 + [("score", i) for i in range(NT)]
    order += [("v", 0), ("choose", 0)] + [("v", i) for i in range(1, NT)] + [("choose", 1)]
    order += [("norm", c) for c in range(KC)]
    ending = weigh0 + flip0 + out0 + weigh1 + flip1 + out1

    def in_ring(steps):
        return [st for st in steps if st[0] in ("proj", "flip", "out", "v", "norm")]

    def drained_by(kind, n):
        return "act" if kind in ("proj", "flip", "norm") else "dve"

    with ExitStack() as ctx:
        s = Space(nc, ctx, "band")
        w3 = s.sb("w3", [P, KC, 3 * C])
        wvv = s.sb("wvv", [P, KC, 2 * C])
        b3, b3s, bvv = s.sb("b3", [P, 3 * KC]), s.sb("b3s", [P, KC]), s.sb("bvv", [P, 2 * C])
        h_tok, hT = s.sb("h_tok", [P, NT, C]), s.sb("hT", [P, KC, T])
        qT = s.sb("qT", [P, KC, T])
        kk = s.sb("kk", [P, KC, 2, LOOKBACK + T])
        vv = s.sb("vv", [P, NT, 2 * C])
        bias, shift, phrase = s.sb("bias", [P, 2, BAND]), s.sb("shift", [P, BAND]), s.sb("phrase", [P, BAND])
        phraseT = s.sb("phraseT", [P, 2, P])
        after_first = s.sb("after_first", [P, 1])
        junk = s.sb("junk", [P, 4, BAND])
        Sm, taken8, taken16 = s.sb("Sm", [P, NT, BAND]), s.sb("taken8", [P, 2, BAND]), s.sb("taken16", [P, NT, BAND])
        best8, next8 = s.sb("best8", [P, NT, 8]), s.sb("next8", [P, NT, 8])
        pair, epair, nmax = s.sb("pair", [P, NT, 2]), s.sb("epair", [P, NT, 2]), s.sb("nmax", [P, NT])
        E = s.sb("E", [P, NT, BAND])
        Wt = s.sb("Wt", [P, NT, 2 * P])
        WT = s.sb("WT", [P, 2, 2 * P])
        sumb, total, rinv, wphr = s.sb("sumb", [P, NT]), s.sb("total", [P, NT]), s.sb("rinv", [P, NT]), s.sb("wphr", [P, NT])
        stats, mv, rstd = s.sb("stats", [P, NT, 6]), s.sb("mv", [P, NT, 2]), s.sb("rstd", [P, NT])
        half, eps = s.sb("half", [P, NT]), s.sb("eps", [P, NT])
        S = s.ps("S", [P, NT, 512])
        W = s.ps("W", [P, 4, 512])

        s_load, s_set, s_fence, s_b3s = s.sem("load"), s.sem("set"), s.sem("fence"), s.sem("b3s")
        ring = Ring(s, W, 4, in_ring(order), drained_by)
        last_ring = Ring(s, W, 4, in_ring(ending), drained_by, ring)
        scored = Loop(s.sem("scored"), NT)
        ready = Loop(s.sem("ready"), NT)
        exped = Loop(s.sem("exped"), 2 * NT)
        weighted = Loop(s.sem("weighted"), NT)
        s_stat = Loop(s.sem("stat"), 2 * NT)
        rooted, normed = Loop(s.sem("rooted"), 2), Loop(s.sem("normed"), NT)
        stepped = Loop(s.sem("stepped"), NT * 12 + NT // 2 + 1)

        N_LOADS = 18
        with nc.Block() as block:
            @block.sync
            def _(sp):
                loads = [(w3[:, :, n * C:(n + 1) * C], a[f"L0_attn_{w}_wT"].rearrange("(k p) n -> p k n", p=P))
                         for n, w in enumerate(("q", "k", "pk"))]
                loads += [(wvv[:, :, n * C:(n + 1) * C], a[f"L0_attn_{w}_wT"].rearrange("(k p) n -> p k n", p=P))
                          for n, w in enumerate(("v", "pv"))]
                loads += [(b3[:, n * KC + c:n * KC + c + 1], a[f"L0_attn_{w}_b"][c * P:(c + 1) * P].unsqueeze(1))
                          for n, w in enumerate(("q", "k", "pk")) for c in range(KC)]
                loads += [(bvv[:, n * C:(n + 1) * C], a[f"L0_attn_{w}_b"].unsqueeze(0).partition_broadcast(P))
                          for n, w in enumerate(("v", "pv"))]
                loads += [(bias[:, :, :], a["band_bias"]), (shift[:, :], a["band_shift"]), (phrase[:, :], a["phrase"]),
                          (phraseT[:, :, :], a["phrase_T"]), (after_first[:, :], a["after_first"])]
                assert len(loads) == N_LOADS, len(loads)
                for dst, src in loads:
                    sp.dma_start(dst, src).then_inc(s_load, 16)

            @block.vector
            def _(dve):
                dve.memset(half[:, :], -0.5).then_inc(s_set, 1)
                dve.memset(eps[:, :], EPS).then_inc(s_set, 1)
                dve.memset(kk[:, :, :, 0:LOOKBACK], 0.0).then_inc(s_set, 1)
                dve.memset(Wt[:, :, 0:P - LOOKBACK], 0.0).then_inc(s_set, 1)
                for t in (Sm, taken16, pair, vv):
                    dve.memset(t[:, :, :], 0.0).then_inc(s_set, 1)
                dve.memset(nmax[:, :], 0.0).then_inc(s_set, 1)

        first_norm(nc, "band", x_mem[:, NT:, :], ident, h_tok, hT, W)

        def tensor_steps(pe, b, order, ring):
            for kind, n in order:
                if kind == "proj":
                    if n == 0:
                        ring.wait_drained(pe, b, ("norm", KC - 1), -1)
                    dst = ring.free_bank(pe, b, (kind, n))
                    for c in range(KC):
                        m = pe.matmul(dst, w3[:, c, n * P:(n + 1) * P], hT[:, c, :], start=(c == 0), stop=(c == KC - 1))
                    m.then_inc(ring.full.sem, 1)
                elif kind == "v":
                    dst = ring.free_bank(pe, b, (kind, n))
                    for c in range(KC):
                        m = pe.matmul(dst, hT[:, c, n * P:(n + 1) * P], wvv[:, c, :], start=(c == 0), stop=(c == KC - 1))
                    m.then_inc(ring.full.sem, 1)
                elif kind == "score":
                    if n == 0:
                        ring.wait_drained(pe, b, proj[-1])
                    ready.wait(pe, b, n + 1 - NT)
                    for c in range(KC):
                        m = pe.matmul(S[:, n, 0:2 * BAND].rearrange("p (t k) -> p t k", t=2), qT[:, c, n * P:(n + 1) * P],
                                      kk[:, c, :, n * P:n * P + BAND], start=(c == 0), stop=(c == KC - 1))
                    m.then_inc(scored.sem, 1)
                elif kind == "norm":
                    dst = ring.free_bank(pe, b, (kind, n))
                    normed.wait(pe, b, NT)
                    for i in range(NT):
                        m = pe.transpose(dst[:, i * P:(i + 1) * P], h_tok[:, i, n * P:(n + 1) * P], ident)
                    m.then_inc(ring.full.sem, 1)
                elif kind == "flip":
                    dst = ring.free_bank(pe, b, (kind, n))
                    weighted.wait(pe, b, n + 1)
                    for k in range(0 if n else 1, 2):
                        m = pe.transpose(dst[:, k * P:(k + 1) * P], Wt[:, n, k * P:(k + 1) * P], ident)
                    m.then_inc(ring.full.sem, 1)
                elif kind == "out":
                    dst = ring.free_bank(pe, b, (kind, n))
                    ring.wait_drained(pe, b, ("flip", n))
                    first = 0 if n else 1
                    for k in range(first, 2):
                        pe.matmul(dst[:, 0:C], WT[:, n % 2, k * P:(k + 1) * P], vv[:, n - 1 + k, 0:C],
                                  start=(k == first), stop=(k == 1))
                    for k in range(first, 2):
                        m = pe.matmul(dst[:, C:2 * C], phraseT[:, k, :], vv[:, n - 1 + k, C:2 * C],
                                      start=(k == first), stop=(k == 1))
                    m.then_inc(ring.full.sem, 1)

        def scalar_steps(act, b, order, ring):
            for st in order:
                kind, n = st
                if kind == "exp":
                    ready.wait(act, b, n + 1 - NT)
                    act.activation(E[:, n, :], Sm[:, n, :], ACT.Exp, bias=nmax[:, n:n + 1]).then_inc(exped.sem, 1)
                    act.activation(epair[:, n, :], pair[:, n, :], ACT.Exp, bias=nmax[:, n:n + 1]).then_inc(exped.sem, 1)
                if st not in ring.place or ring.engine(st) != "act":
                    continue
                ring.wait_full(act, b, st)
                src, done = ring.bank(st), ring.drained["act"].sem
                if kind == "proj":
                    which, c = n // KC, n % KC
                    if which == 0:
                        act.activation(qT[:, c, :], src, ACT.Identity, bias=b3s[:, c:c + 1], scale=scale).then_inc(done, 1)
                    else:
                        act.activation(kk[:, c, which - 1, LOOKBACK:], src, ACT.Identity, bias=b3[:, n:n + 1]).then_inc(done, 1)
                elif kind == "flip":
                    first = 0 if n else P
                    act.copy(WT[:, n % 2, first:], src[:, first:2 * P]).then_inc(done, 1)
                elif kind == "norm":
                    act.copy(hT[:, n, :], src).then_inc(done, 1)

        def vector_steps(dve, b, order, ring):
            n_done = [0]

            def step(ins):
                n_done[0] += 1
                ins.then_inc(stepped.sem, 1)

            def stepped_through(before_search=False):
                stepped.wait(dve, b, n_done[0])
                if before_search:
                    dve.sem_inc(s_fence, 1)

            def next_tile(i):
                return x_mem[:, bass.ds(b * NT + (2 * NT + i), 1), :].rearrange("p a c -> p (a c)")

            def choose(two):
                for i in two:
                    scored.wait(dve, b, i + 1)
                    step(dve.tensor_tensor(Sm[:, i, :], S[:, i, 0:BAND], bias[:, 0 if i == 0 else 1, :], ALU.add))
                    for t, at in enumerate((shift, phrase)):
                        step(dve.tensor_tensor_reduce(junk[:, 2 * (i % 2) + t, :], S[:, i, t * BAND:(t + 1) * BAND], at[:, :], 1.0, 0.0,
                                                      ALU.mult, ALU.add, pair[:, i, t:t + 1]))
                stepped_through(True)
                for i in two:
                    step(dve.max(out=best8[:, i, :], in_=Sm[:, i, :]))
                stepped_through(True)
                for i in two:
                    step(dve.tensor_scalar(nmax[:, i:i + 1], best8[:, i, 0:1], pair[:, i, 1:2], -1.0, ALU.max, ALU.mult))
                for i in two:
                    step(dve.match_replace(out=taken8[:, i % 2, :], in_to_replace=best8[:, i, :], in_values=Sm[:, i, :], imm_value=GONE))
                stepped_through(True)
                dve.sem_inc(ready.sem, len(two))
                for i in two:
                    step(dve.max(out=next8[:, i, :], in_=taken8[:, i % 2, :]))
                stepped_through(True)
                for i in two:
                    step(dve.match_replace(out=taken16[:, i, :], in_to_replace=next8[:, i, :], in_values=taken8[:, i % 2, :], imm_value=GONE))
                stepped_through()

            def weigh(two):
                exped.wait(dve, b, 2 * two[-1] + 2)
                for i in two:
                    step(dve.scalar_tensor_tensor(out=E[:, i, :], in0=taken16[:, i, :], scalar=GONE * 0.5, in1=E[:, i, :],
                                                  op0=ALU.is_lt, op1=ALU.mult, accum_out=sumb[:, i:i + 1]))
                stepped_through()
                for i in two:
                    dve.scalar_tensor_tensor(out=Wt[:, i, P - LOOKBACK:], in0=shift[:, :], scalar=epair[:, i, 0:1], in1=E[:, i, :],
                                             op0=ALU.mult, op1=ALU.add).then_inc(weighted.sem, 1)
                for i in two:
                    step(dve.tensor_scalar(total[:, i:i + 1], sumb[:, i:i + 1], epair[:, i, 0:1], epair[:, i, 1:2], ALU.add, ALU.add))
                stepped_through()
                step(dve.reciprocal(rinv[:, two[0]:two[-1] + 1], total[:, two[0]:two[-1] + 1]))
                stepped_through()
                if two[0] == 0:
                    step(dve.tensor_scalar(rinv[:, 0:1], rinv[:, 0:1], after_first[:, :], None, ALU.mult))
                    stepped_through()
                for i in two:
                    step(dve.tensor_scalar(wphr[:, i:i + 1], epair[:, i, 1:2], rinv[:, i:i + 1], None, ALU.mult))
                stepped_through()

            for st in order:
                kind, n = st
                if kind == "stat":
                    for i in range(NT):
                        dve.bn_stats(stats[:, i, :], next_tile(i)).then_inc(s_stat.sem, 1)
                    s_stat.wait(dve, b, NT)
                    dve.sem_inc(s_fence, 1)
                    for i in range(NT):
                        dve.bn_aggr(mv[:, i, :], stats[:, i, :]).then_inc(s_stat.sem, 1)
                elif kind == "htok":
                    rooted.wait(dve, b, 2)
                    ring.wait_full(dve, b, ("norm", KC - 1), -1)
                    for i in range(NT):
                        dve.tensor_scalar(h_tok[:, i, :], next_tile(i), mv[:, i, 0:1], rstd[:, i:i + 1],
                                          ALU.subtract, ALU.mult).then_inc(normed.sem, 1)
                elif kind == "choose":
                    choose((2 * n, 2 * n + 1))
                elif kind == "weigh":
                    weigh((2 * n, 2 * n + 1))
                elif kind == "out":
                    ring.wait_full(dve, b, st)
                    src, done = ring.bank(st), ring.drained["dve"].sem
                    xt = x_mem[:, bass.ds(b * NT + n, 1), :].rearrange("p a c -> p (a c)")
                    step(dve.scalar_tensor_tensor(out=xt, in0=src[:, 0:C], scalar=rinv[:, n:n + 1], in1=xt, op0=ALU.mult, op1=ALU.add))
                    stepped_through()
                    dve.scalar_tensor_tensor(out=xt, in0=src[:, C:2 * C], scalar=wphr[:, n:n + 1], in1=xt, op0=ALU.mult, op1=ALU.add).then_inc(done, 1)
                elif kind == "v":
                    ring.wait_full(dve, b, st)
                    dve.tensor_tensor(vv[:, n, :], ring.bank(st), bvv[:, :], ALU.add).then_inc(ring.drained["dve"].sem, 1)
            assert order is ending or n_done[0] == stepped.per, n_done

        with nc.Block() as block:
            @block.tensor
            def _(pe):
                for sem in (ring.full, scored):
                    sem.credit(pe)
                pe.wait_ge(s_load, 16 * N_LOADS)
                with pe.Fori(0, B) as b:
                    tensor_steps(pe, b, order, ring)
                tensor_steps(pe, B, ending, last_ring)

            @block.scalar
            def _(act):
                for sem in (ring.drained["act"], exped):
                    sem.credit(act)
                act.wait_ge(s_load, 16 * N_LOADS)
                act.activation(b3s[:, :], b3[:, 0:KC], ACT.Identity, scale=scale).then_inc(s_b3s, 1)
                act.wait_ge(s_b3s, 1)
                with act.Fori(0, B) as b:
                    scalar_steps(act, b, order, ring)
                scalar_steps(act, B, ending, last_ring)

            @block.vector
            def _(dve):
                for sem in (ring.drained["dve"], ready, weighted, s_stat, normed, stepped):
                    sem.credit(dve)
                dve.wait_ge(s_load, 16 * N_LOADS)
                dve.wait_ge(consts["x_loaded"], 32)
                with dve.Fori(0, B) as b:
                    vector_steps(dve, b, order, ring)
                vector_steps(dve, B, ending, last_ring)

            @block.gpsimd
            def _(pool):
                rooted.credit(pool)
                with pool.Fori(0, B) as b:
                    s_stat.wait(pool, b, 2 * NT)
                    pool.tensor_tensor(rstd[:, :], mv[:, :, 1], eps[:, :], ALU.add).then_inc(rooted.sem, 1)
                    rooted.wait(pool, b, 1)
                    pool.tensor_tensor(rstd[:, :], rstd[:, :], half[:, :], ALU.pow).then_inc(rooted.sem, 1)
        s.clear()




ROUND = 1.5 * 2.0 ** 23
INNER = 1024
FC = INNER // P


def ternary_ffn(nc, x_mem, consts, a):
    ident_bf = consts["ident_bf"]
    HALVES = 2
    order = []
    for i in range(NT):
        order.append(("raise", (i - 1) % NT))
        order += [("gate", HALVES * i + j) for j in range(HALVES)]
        order.append(("turn_p", (i - 2) % NT))
        if i == NT - 1:
            order.append(("turn_x", 0))
        order += [("quant", (i - 1) % NT), ("down", (i - 2) % NT)]
    ending = [("raise", NT - 1), ("turn_p", NT - 2), ("quant", NT - 1), ("down", NT - 2), ("turn_p", NT - 1), ("down", NT - 1)]

    ring_steps = [st for st in order if st[0] in ("turn_x", "turn_p", "down")]

    def drained_by(kind, n):
        return "dve" if kind == "down" else "act"

    with ExitStack() as ctx:
        s = Space(nc, ctx, "ffn")
        names = ("gate", "up", "down")
        w = {n: s.sb("w_" + n, [P, 2 * INNER]) for n in names}
        wq = {n: s.sb("wq_" + n, [P, 2 * INNER], BF16) for n in names}
        part, mean, winv = s.sb("part", [P, 3]), s.sb("mean", [P, 3]), s.sb("winv", [P, 3])
        ones = s.sb("ones", [P, P])
        h_tok = s.sb("h_tok", [P, NT, C])
        hq, hqT = s.sb("hq", [P, NT, C], BF16), s.sb("hqT", [P, KC, T], BF16)
        amax, sx = s.sb("amax", [P, NT]), s.sb("sx", [P, NT])
        fg, fu = s.sb("fg", [P, 2, NT]), s.sb("fu", [P, 2, NT])
        g = s.sb("g", [P, 2, 512])
        p = s.sb("p", [P, NT, INNER])
        pr, pq = s.sb("pr", [P, NT, INNER]), s.sb("pq", [P, NT, INNER], BF16)
        pT = s.sb("pT", [P, NT, FC * P], BF16)
        pmax, sp_, fd = s.sb("pmax", [P, NT]), s.sb("sp", [P, NT]), s.sb("fd", [P, NT])
        magic = s.sb("magic", [P, 1])
        stats, mv, rstd = s.sb("stats", [P, NT, 6]), s.sb("mv", [P, NT, 2]), s.sb("rstd", [P, NT])
        half, eps = s.sb("half", [P, NT]), s.sb("eps", [P, NT])
        GU = s.ps("GU", [P, 2, 2, 512])
        W = s.ps("W", [P, 4, 512])

        s_load, s_set, s_fence = s.sem("load"), s.sem("set"), s.sem("fence")
        s_sum, s_tot, s_q = s.sem("sum"), s.sem("tot"), s.sem("q")
        ring = Ring(s, W, 4, ring_steps, drained_by)
        gated = Loop(s.sem("gated"), 2 * NT)
        silued = Loop(s.sem("silued"), 2 * NT)
        multiplied = Loop(s.sem("multiplied"), 2 * NT)
        scaled = Loop(s.sem("scaled"), NT)
        raised = Loop(s.sem("raised"), NT)
        quantised = Loop(s.sem("quantised"), NT)
        x_quantised = Loop(s.sem("x_quantised"), 1)
        s_stat = Loop(s.sem("stat"), 2 * NT)
        rooted = Loop(s.sem("rooted"), 2)
        stepped = Loop(s.sem("stepped"), 5 * NT + 5)
        refreshed = Loop(s.sem("refreshed"), 2)

        def scales_of_products(dve, step, slot):
            step(dve.tensor_scalar(fg[:, slot, :], amax[:, :], mean[:, 0:1], None, ALU.mult))
            step(dve.tensor_scalar(fu[:, slot, :], amax[:, :], mean[:, 1:2], None, ALU.mult))

        def quantise_x(dve, tiles, step, through, done, slot):
            for i in range(NT):
                step(dve.tensor_scalar(h_tok[:, i, :], tiles(i), mv[:, i, 0:1], rstd[:, i:i + 1], ALU.subtract, ALU.mult))
            through()
            step(dve.tensor_reduce(amax[:, :], h_tok[:, :, :], AX.X, ALU.max, apply_absolute_value=True))
            through()
            step(dve.tensor_scalar(amax[:, :], amax[:, :], EPS, 1.0 / 127.0, ALU.max, ALU.mult))
            through()
            step(dve.reciprocal(sx[:, :], amax[:, :]))
            if slot:
                scales_of_products(dve, step, slot)
            through()
            for i in range(NT):
                step(dve.tensor_scalar(h_tok[:, i, :], h_tok[:, i, :], sx[:, i:i + 1], ROUND, ALU.mult, ALU.add))
            through()
            dve.tensor_scalar(hq[:, :, :], h_tok[:, :, :], ROUND, 127.0, ALU.subtract, ALU.min).then_inc(done, 1)

        def turn_x(pe, done):
            out = W[:, ring.place[("turn_x", 0)] % 4, :].bitcast(BF16)
            for c in range(KC):
                for i in range(NT):
                    m = pe.transpose(out[:, (c * NT + i) * P:(c * NT + i + 1) * P], hq[:, i, c * P:(c + 1) * P], ident_bf)
            m.then_inc(done, 1)

        s_first, s_p1, s_p2, s_p3 = s.sem("first"), s.sem("first_root"), s.sem("first_q"), s.sem("first_turned")
        with nc.Block() as block:
            @block.sync
            def _(sp):
                for n in names:
                    k = KC if n != "down" else FC
                    sp.dma_start(w[n][:, :].rearrange("p (k n) -> p k n", k=k),
                                 a[f"L0_ffn_w_{n}T"].rearrange("(k p) n -> p k n", p=P)).then_inc(s_load, 16)

            @block.vector
            def _(dve):
                count = [0]

                def step(ins):
                    count[0] += 1
                    ins.then_inc(s_first, 1)

                def through():
                    dve.wait_ge(s_first, count[0])

                dve.memset(half[:, :], -0.5).then_inc(s_set, 1)
                dve.memset(eps[:, :], EPS).then_inc(s_set, 1)
                dve.memset(magic[:, :], ROUND).then_inc(s_set, 1)
                dve.memset(ones[:, :], 1.0).then_inc(s_set, 1)
                for t in (p[:, NT - 1, :], pq[:, NT - 2, :], sp_[:, :], pmax[:, :]):
                    dve.memset(t, 0.0).then_inc(s_set, 1)
                for i in range(NT):
                    step(dve.bn_stats(stats[:, i, :], x_mem[:, NT + i, :]))
                through()
                for i in range(NT):
                    step(dve.bn_aggr(mv[:, i, :], stats[:, i, :]))
                dve.wait_ge(s_p1, 2)
                quantise_x(dve, lambda i: x_mem[:, NT + i, :], step, through, s_p2, 0)
                dve.wait_ge(s_load, 48)
                for n, name in enumerate(names):
                    dve.tensor_reduce(part[:, n:n + 1], w[name][:, :], AX.X, ALU.add, apply_absolute_value=True).then_inc(s_sum, 1)
                dve.wait_ge(s_tot, 1)
                dve.tensor_scalar(mean[:, :], W[:, 0, 0:3], 1.0 / (C * INNER), EPS, ALU.mult, ALU.max).then_inc(s_q, 1)
                dve.wait_ge(s_q, 1)
                dve.reciprocal(winv[:, :], mean[:, :]).then_inc(s_q, 1)
                scales_of_products(dve, step, 0)
                dve.wait_ge(s_q, 2)
                for n, name in enumerate(names):
                    dve.tensor_scalar(w[name][:, :], w[name][:, :], winv[:, n:n + 1], 1.0, ALU.mult, ALU.min).then_inc(s_q, 1)
                    dve.wait_ge(s_q, 3 * n + 3)
                    dve.tensor_scalar(w[name][:, :], w[name][:, :], -1.0, ROUND, ALU.max, ALU.add).then_inc(s_q, 1)
                    dve.wait_ge(s_q, 3 * n + 4)
                    dve.tensor_scalar(wq[name][:, :], w[name][:, :], ROUND, None, ALU.subtract).then_inc(s_q, 1)
                dve.wait_ge(s_q, 11)
                through()

            @block.gpsimd
            def _(pool):
                pool.wait_ge(s_set, 2)
                pool.wait_ge(s_first, 2 * NT)
                pool.tensor_tensor(rstd[:, :], mv[:, :, 1], eps[:, :], ALU.add).then_inc(s_p1, 1)
                pool.wait_ge(s_p1, 1)
                pool.tensor_tensor(rstd[:, :], rstd[:, :], half[:, :], ALU.pow).then_inc(s_p1, 1)

            @block.tensor
            def _(pe):
                pe.wait_ge(s_p2, 1)
                turn_x(pe, s_p3)
                pe.wait_ge(s_set, 4)
                pe.wait_ge(s_sum, 3)
                pe.matmul(W[:, 0, 0:3], ones[:, :], part[:, :], start=True, stop=True).then_inc(s_tot, 1)

            @block.scalar
            def _(act):
                act.wait_ge(s_p3, 1)
                act.copy(hqT[:, :, :].rearrange("p c t -> p (c t)"), W[:, ring.place[("turn_x", 0)] % 4, :].bitcast(BF16)).then_inc(s_p3, 1)

        def tensor_steps(pe, b, order):
            for kind, n in order:
                if kind == "gate":
                    i, j = n // HALVES, n % HALVES
                    if n == 0:
                        ring.wait_drained(pe, b, ("turn_x", 0), -1)
                    multiplied.wait(pe, b, n - 1)
                    for t, name in enumerate(("gate", "up")):
                        for c in range(KC):
                            m = pe.matmul(GU[:, j, t, :], hqT[:, c, i * P:(i + 1) * P],
                                          wq[name][:, c * INNER + j * 512:c * INNER + (j + 1) * 512],
                                          start=(c == 0), stop=(c == KC - 1))
                    m.then_inc(gated.sem, 1)
                elif kind == "turn_x":
                    ring.free_bank(pe, b, (kind, n))
                    x_quantised.wait(pe, b, 1)
                    turn_x(pe, ring.full.sem)
                elif kind == "turn_p":
                    out = ring.free_bank(pe, b, (kind, n)).bitcast(BF16)
                    quantised.wait(pe, b, (n + 2) % NT)
                    for f in range(FC):
                        m = pe.transpose(out[:, f * P:(f + 1) * P], pq[:, n, f * P:(f + 1) * P], ident_bf)
                    m.then_inc(ring.full.sem, 1)
                elif kind == "down":
                    dst = ring.free_bank(pe, b, (kind, n))
                    ring.wait_drained(pe, b, ("turn_p", n))
                    for f in range(FC):
                        m = pe.matmul(dst[:, 0:C], pT[:, n, f * P:(f + 1) * P], wq["down"][:, f * C:(f + 1) * C],
                                      start=(f == 0), stop=(f == FC - 1))
                    m.then_inc(ring.full.sem, 1)

        def scalar_steps(act, b, order):
            for st in order:
                kind, n = st
                if kind == "gate":
                    i, j = n // HALVES, n % HALVES
                    gated.wait(act, b, n + 1)
                    if n == 0:
                        refreshed.wait(act, b, 0)
                    multiplied.wait(act, b, n - 1)
                    act.activation(g[:, j, :], GU[:, j, 0, :], ACT.Silu, scale=fg[:, 0, i:i + 1]).then_inc(silued.sem, 1)
                    continue
                if kind == "raise":
                    scaled.wait(act, b, (n + 1) % NT)
                    act.activation(pr[:, n, :], p[:, n, :], ACT.Identity, bias=magic[:, :], scale=sp_[:, n:n + 1]).then_inc(raised.sem, 1)
                if st not in ring.place or ring.engine(st) != "act":
                    continue
                ring.wait_full(act, b, st)
                src, done = ring.bank(st), ring.drained["act"].sem
                if kind == "turn_p":
                    act.copy(pT[:, n, :], src.bitcast(BF16)).then_inc(done, 1)
                else:
                    gated.wait(act, b, 2 * NT)
                    act.copy(hqT[:, :, :].rearrange("p c t -> p (c t)"), src.bitcast(BF16)).then_inc(done, 1)

        def vector_steps(dve, b, order):
            count = [0]

            def step(ins):
                count[0] += 1
                ins.then_inc(stepped.sem, 1)

            def through():
                stepped.wait(dve, b, count[0])

            def next_tile(i):
                return x_mem[:, bass.ds(b * NT + (2 * NT + i), 1), :].rearrange("p a c -> p (a c)")

            for st in order:
                kind, n = st
                if kind == "gate":
                    i, j = n // HALVES, n % HALVES
                    silued.wait(dve, b, n + 1)
                    if n == 0:
                        refreshed.wait(dve, b, 0)
                    dve.scalar_tensor_tensor(out=p[:, i, j * 512:(j + 1) * 512], in0=GU[:, j, 1, :], scalar=fu[:, 0, i:i + 1],
                                             in1=g[:, j, :], op0=ALU.mult, op1=ALU.mult).then_inc(multiplied.sem, 1)
                    if n == HALVES * NT - 1:
                        multiplied.wait(dve, b, n + 1)
                        dve.tensor_copy(fg[:, 0, :], fg[:, 1, :]).then_inc(refreshed.sem, 1)
                        dve.tensor_copy(fu[:, 0, :], fu[:, 1, :]).then_inc(refreshed.sem, 1)
                    if j == HALVES - 1:
                        multiplied.wait(dve, b, n + 1)
                        step(dve.tensor_reduce(pmax[:, i:i + 1], p[:, i, :], AX.X, ALU.max, apply_absolute_value=True))
                        through()
                        step(dve.tensor_scalar(pmax[:, i:i + 1], pmax[:, i:i + 1], EPS, 1.0 / 127.0, ALU.max, ALU.mult))
                        through()
                        dve.reciprocal(sp_[:, i:i + 1], pmax[:, i:i + 1]).then_inc(scaled.sem, 1)
                elif kind == "quant":
                    raised.wait(dve, b, (n + 1) % NT + 1)
                    dve.tensor_scalar(pq[:, n, :], pr[:, n, :], ROUND, 127.0, ALU.subtract, ALU.min).then_inc(quantised.sem, 1)
                    if n == NT - 1 and order is not ending:
                        for t in range(NT):
                            dve.bn_stats(stats[:, t, :], next_tile(t)).then_inc(s_stat.sem, 1)
                        s_stat.wait(dve, b, NT)
                        dve.sem_inc(s_fence, 1)
                        for t in range(NT):
                            dve.bn_aggr(mv[:, t, :], stats[:, t, :]).then_inc(s_stat.sem, 1)
                    if n == 0:
                        rooted.wait(dve, b, 2)
                        quantise_x(dve, next_tile, step, through, x_quantised.sem, 1)
                elif kind == "down":
                    ring.wait_full(dve, b, st)
                    tile = b * NT + (n if n >= NT - 2 else NT + n)
                    xt = x_mem[:, bass.ds(tile, 1), :].rearrange("p a c -> p (a c)")
                    step(dve.tensor_scalar(fd[:, n:n + 1], pmax[:, n:n + 1], mean[:, 2:3], None, ALU.mult))
                    through()
                    dve.scalar_tensor_tensor(out=xt, in0=ring.bank(st)[:, 0:C], scalar=fd[:, n:n + 1], in1=xt,
                                             op0=ALU.mult, op1=ALU.add).then_inc(ring.drained["dve"].sem, 1)
            if order is ending:
                return
            through()
            assert count[0] == stepped.per, count

        with nc.Block() as block:
            @block.tensor
            def _(pe):
                for sem in (ring.full, gated):
                    sem.credit(pe)
                with pe.Fori(0, B) as b:
                    tensor_steps(pe, b, order)
                tensor_steps(pe, B, ending)

            @block.scalar
            def _(act):
                for sem in (ring.drained["act"], silued, raised):
                    sem.credit(act)
                with act.Fori(0, B) as b:
                    scalar_steps(act, b, order)
                scalar_steps(act, B, ending)

            @block.vector
            def _(dve):
                for sem in (ring.drained["dve"], multiplied, scaled, quantised, x_quantised, s_stat, stepped, refreshed):
                    sem.credit(dve)
                with dve.Fori(0, B) as b:
                    vector_steps(dve, b, order)
                vector_steps(dve, B, ending)

            @block.gpsimd
            def _(pool):
                rooted.credit(pool)
                with pool.Fori(0, B) as b:
                    s_stat.wait(pool, b, 2 * NT)
                    pool.tensor_tensor(rstd[:, :], mv[:, :, 1], eps[:, :], ALU.add).then_inc(rooted.sem, 1)
                    rooted.wait(pool, b, 1)
                    pool.tensor_tensor(rstd[:, :], rstd[:, :], half[:, :], ALU.pow).then_inc(rooted.sem, 1)
        s.clear()




EXPERTS, D_FF = 8, 1024
FF = D_FF // P
SLOTS = NX + EXPERTS - 1
AHEAD = 3


def mixture(nc, x_all, consts, a, out):
    sorted_h = nc.dram_tensor("sorted_h", ((SLOTS + AHEAD) * P, C), F32, kind="Internal").ap()
    sorted_y = nc.dram_tensor("sorted_y", (SLOTS * P, C), F32, kind="Internal").ap()
    with ExitStack() as ctx:
        s = Space(nc, ctx, "moe")
        W1 = s.sb("W1", [P, EXPERTS * KC * D_FF])
        W2 = s.sb("W2", [P, EXPERTS * FF * C])
        position = s.sb("position", [P, NX], I32)
        gate = s.sb("gate", [P, NX])
        owner = s.sb("owner", [P, SLOTS + AHEAD], I32)
        s_w, s_zero = s.sem("w"), s.sem("zero")
        route(nc, x_all, consts, a, sorted_h, W1, W2, position, gate, owner, s_w, s_zero)
        with ExitStack() as inner:
            experts(nc, Space(nc, inner, "experts"), consts, a, sorted_h, sorted_y, W1, W2, owner, s_w)
        with ExitStack() as inner:
            combine(nc, Space(nc, inner, "combine"), x_all, position, gate, sorted_y, out)


def route(nc, x_all, consts, a, sorted_h, W1, W2, position, gate, owner, s_w, s_zero):
    ident = consts["ident"]
    E = EXPERTS
    with ExitStack() as ctx:
        s = Space(nc, ctx, "route")
        h_all = s.sb("h", [P, NX, C])
        hT = s.sb("hT", [P, 2, C])
        rw, rb = s.sb("rw", [P, KC, E]), s.sb("rb", [P, E])
        later32, later, ones = s.sb("later32", [P, P]), s.sb("later", [P, P], BF16), s.sb("ones", [P, P], BF16)
        rank, slot_no = s.sb("rank", [P, E]), s.sb("slot_no", [P, SLOTS + AHEAD])
        logits, t0, t1 = (consts["spare"][:, n * NX * E:(n + 1) * NX * E].rearrange("p (t e) -> p t e", e=E) for n in range(3))
        hot = s.sb("hot", [P, NX, E], BF16)
        row = s.sb("row", [P, NX])
        cnt, tiles, start, end = s.sb("cnt", [P, E]), s.sb("tiles", [P, E]), s.sb("start", [P, 2, E]), s.sb("end", [P, E])
        over, own = s.sb("over", [P, SLOTS + AHEAD, E]), s.sb("own", [P, SLOTS + AHEAD])
        stats = consts["spare"][:, 3 * NX * E:3 * NX * E + NX * 6].rearrange("p (t s) -> p t s", s=6)
        mv, rstd = s.sb("mv", [P, NX, 2]), s.sb("rstd", [P, NX])
        half = s.sb("half", [P, NX])
        tr = s.ps("tr", [P, 2, 512])
        lg = s.ps("lg", [P, 2, 512])
        pre = s.ps("pre", [P, 512])
        tot = s.ps("tot", [P, 512])
        s_load, s_set, s_stat, s_mv, s_root, s_h = (s.sem(n) for n in ("load", "set", "stat", "mv", "root", "h"))
        s_tr, s_hT, s_lg, s_lgd = (s.sem(n) for n in ("tr", "hT", "lg", "lgd"))
        s_d, s_exp, s_hot, s_cnt, s_pos, s_sc = (s.sem(n) for n in ("d", "exp", "hot", "cnt", "pos", "sc"))

        with nc.Block() as block:
            @block.sync
            def _(sp):
                loads = [(rw[:, :, :], a["L1_ffn_router_W"].rearrange("(k p) e -> p k e", p=P)),
                         (rb[:, :], a["L1_ffn_router_b"].unsqueeze(0).partition_broadcast(P)),
                         (later32[:, :], a["later"]), (rank[:, :], a["rank"]), (slot_no[:, :], a["slot_no"])]
                for dst, src in loads:
                    sp.dma_start(dst, src).then_inc(s_load, 16)
                sp.dma_start(sorted_h.rearrange("(g p) c -> p g c", p=P),
                             x_all[:, NX, :].unsqueeze(1).to_broadcast([P, SLOTS + AHEAD, C])).then_inc(s_zero, 16)
                for e in range(E):
                    sp.dma_start(W1[:, e * KC * D_FF:(e + 1) * KC * D_FF].rearrange("p (k n) -> p k n", k=KC),
                                 a["L1_ffn_W1"][e].rearrange("(k p) n -> p k n", p=P)).then_inc(s_w, 16)
                for e in range(E):
                    sp.dma_start(W2[:, e * FF * C:(e + 1) * FF * C].rearrange("p (k n) -> p k n", k=FF),
                                 a["L1_ffn_W2"][e].rearrange("(k p) n -> p k n", p=P)).then_inc(s_w, 16)

            @block.gpsimd
            def _(pool):
                pool.memset(half[:, :], -0.5).then_inc(s_root, 1)
                pool.wait_ge(s_mv, NX)
                pool.tensor_scalar(rstd[:, :], mv[:, :, 1], EPS, None, ALU.add).then_inc(s_root, 1)
                pool.wait_ge(s_root, 2)
                pool.tensor_tensor(rstd[:, :], rstd[:, :], half[:, :], ALU.pow).then_inc(s_root, 1)
                pool.wait_ge(s_zero, 16)
                pool.wait_ge(s_h, NX)
                pool.wait_ge(s_pos, 1)
                for t in range(NX):
                    pool.indirect_dma_start(out=sorted_h, out_offset=bass.IndirectOffsetOnAxis(ap=position[:, t:t + 1], axis=0),
                                            in_=h_all[:, t, :], in_offset=None).then_inc(s_sc, 16)
                pool.wait_ge(s_sc, 16 * NX)

            @block.vector
            def _(dve):
                for t in range(NX):
                    dve.bn_stats(stats[:, t, :], x_all[:, t, :]).then_inc(s_stat, 1)
                dve.wait_ge(s_stat, NX)
                for t in range(NX):
                    dve.bn_aggr(mv[:, t, :], stats[:, t, :]).then_inc(s_mv, 1)
                dve.wait_ge(s_root, 3)
                dve.memset(ones[:, :], 1.0).then_inc(s_set, 1)
                for t in range(NX):
                    dve.tensor_scalar(h_all[:, t, :], x_all[:, t, :], mv[:, t, 0:1], rstd[:, t:t + 1],
                                      ALU.subtract, ALU.mult).then_inc(s_h, 1)
                dve.wait_ge(s_load, 16 * 5)
                dve.tensor_copy(later[:, :], later32[:, :]).then_inc(s_set, 1)
                for t in range(NX):
                    dve.wait_ge(s_lg, t + 1)
                    dve.tensor_tensor(logits[:, t, :], lg[:, t % 2, 0:E], rb[:, :], ALU.add).then_inc(s_lgd, 1)
                dve.wait_ge(s_lgd, NX)

                count = [0]

                def step(ins):
                    count[0] += 1
                    ins.then_inc(s_d, 1)
                    dve.wait_ge(s_d, count[0])

                def per_token(v):
                    return v[:, :].unsqueeze(2).to_broadcast([P, NX, E])

                def per_expert(v, n=NX):
                    return v.unsqueeze(1).to_broadcast([P, n, E])

                step(dve.tensor_reduce(row[:, :], logits[:, :, :], AX.X, ALU.max))
                step(dve.tensor_tensor(t0[:, :, :], logits[:, :, :], per_token(row), ALU.subtract))
                dve.sem_inc(s_exp, 1)
                dve.wait_ge(s_exp, 2)
                step(dve.tensor_reduce(row[:, :], t1[:, :, :], AX.X, ALU.add))
                step(dve.reciprocal(gate[:, :], row[:, :]))
                step(dve.tensor_reduce(row[:, :], t1[:, :, :], AX.X, ALU.max))
                step(dve.tensor_tensor(gate[:, :], gate[:, :], row[:, :], ALU.mult))
                step(dve.tensor_tensor(t0[:, :, :], t1[:, :, :], per_token(row), ALU.is_ge))
                step(dve.tensor_tensor(t0[:, :, :], t0[:, :, :], per_expert(rank[:, :]), ALU.mult))
                step(dve.tensor_reduce(row[:, :], t0[:, :, :], AX.X, ALU.max))
                step(dve.tensor_tensor(hot[:, :, :], t0[:, :, :], per_token(row), ALU.is_equal))
                dve.sem_inc(s_hot, 1)
                dve.wait_ge(s_cnt, 2)
                step(dve.tensor_copy(t0[:, :, :], tot[:, 0:NX * E].rearrange("p (t e) -> p t e", e=E)))
                src, dst = t0, t1
                for d in (1, 2, 4, 8, 16):
                    step(dve.tensor_tensor(dst[:, d:, :], src[:, d:, :], src[:, 0:NX - d, :], ALU.add))
                    step(dve.tensor_copy(dst[:, 0:d, :], src[:, 0:d, :]))
                    src, dst = dst, src
                step(dve.tensor_scalar(cnt[:, :], src[:, NX - 1, :], float(P - 1), 1.0 / P, ALU.add, ALU.mult))
                step(dve.tensor_scalar(cnt[:, :], cnt[:, :], (P / 2 - 0.5) / P, ROUND, ALU.subtract, ALU.add))
                step(dve.tensor_scalar(tiles[:, :], cnt[:, :], ROUND, None, ALU.subtract))
                step(dve.tensor_copy(end[:, 0:1], tiles[:, 0:1]))
                for e in range(1, E):
                    step(dve.tensor_tensor(end[:, e:e + 1], end[:, e - 1:e], tiles[:, e:e + 1], ALU.add))
                step(dve.tensor_tensor(start[:, 0, :], end[:, :], tiles[:, :], ALU.subtract))
                step(dve.tensor_scalar(start[:, 1, :], start[:, 0, :], float(P), None, ALU.mult))
                step(dve.tensor_tensor(src[:, :, :], src[:, :, :], tot[:, 0:NX * E].rearrange("p (t e) -> p t e", e=E), ALU.subtract))
                step(dve.tensor_tensor(src[:, :, :], src[:, :, :], pre[:, 0:NX * E].rearrange("p (t e) -> p t e", e=E), ALU.add))
                step(dve.tensor_tensor(src[:, :, :], src[:, :, :], per_expert(start[:, 1, :]), ALU.add))
                step(dve.tensor_tensor(src[:, :, :], src[:, :, :], hot[:, :, :], ALU.mult))
                step(dve.tensor_reduce(row[:, :], src[:, :, :], AX.X, ALU.add))
                step(dve.tensor_copy(position[:, :], row[:, :]))
                dve.sem_inc(s_pos, 1)
                n = SLOTS + AHEAD
                step(dve.tensor_tensor(over[:, :, :], slot_no[:, :].unsqueeze(2).to_broadcast([P, n, E]), per_expert(end[:, :], n), ALU.is_ge))
                step(dve.tensor_reduce(own[:, :], over[:, :, :], AX.X, ALU.add))
                step(dve.tensor_scalar(own[:, :], own[:, :], float(E - 1), None, ALU.min))
                step(dve.tensor_copy(owner[:, :], own[:, :]))

            @block.tensor
            def _(pe):
                def logits_of(t):
                    pe.wait_ge(s_hT, t + 1)
                    if t >= 2:
                        pe.wait_ge(s_lgd, t - 1)
                    for c in range(KC):
                        m = pe.matmul(lg[:, t % 2, 0:E], hT[:, t % 2, c * P:(c + 1) * P], rw[:, c, :], start=(c == 0), stop=(c == KC - 1))
                    m.then_inc(s_lg, 1)

                pe.wait_ge(s_load, 16 * 5)
                for t in range(NX):
                    pe.wait_ge(s_h, t + 1)
                    if t >= 2:
                        pe.wait_ge(s_hT, t - 1)
                    for c in range(KC):
                        m = pe.transpose(tr[:, t % 2, c * P:(c + 1) * P], h_all[:, t, c * P:(c + 1) * P], ident)
                    m.then_inc(s_tr, 1)
                    if t:
                        logits_of(t - 1)
                logits_of(NX - 1)
                pe.wait_ge(s_hot, 1)
                pe.wait_ge(s_set, 2)
                flat = hot[:, :, :].rearrange("p t e -> p (t e)")
                pe.matmul(pre[:, 0:NX * E], later[:, :], flat, start=True, stop=True).then_inc(s_cnt, 1)
                pe.matmul(tot[:, 0:NX * E], ones[:, :], flat, start=True, stop=True).then_inc(s_cnt, 1)

            @block.scalar
            def _(act):
                for t in range(NX):
                    act.wait_ge(s_tr, t + 1)
                    if t >= 2:
                        act.wait_ge(s_lg, t - 1)
                    act.copy(hT[:, t % 2, :], tr[:, t % 2, 0:C]).then_inc(s_hT, 1)
                act.wait_ge(s_exp, 1)
                act.activation(t1[:, :, :], t0[:, :, :], ACT.Exp).then_inc(s_exp, 1)
        s.clear()



def experts(nc, s, consts, a, sorted_h, sorted_y, W1, W2, owner, s_w):
    ident = consts["ident"]
    xs, xT = s.sb("xs", [P, C]), s.sb("xT", [P, C])
    hid, hidT = s.sb("hid", [P, D_FF]), s.sb("hidT", [P, FF, P])
    y = s.sb("y", [P, C])
    b1T, b2B = s.sb("b1T", [P, EXPERTS * FF]), s.sb("b2B", [P, EXPERTS * C])
    A = s.ps("A", [P, 2, 512])
    AT = s.ps("AT", [P, 2, 512])
    XP, Y = s.ps("XP", [P, 512]), s.ps("Y", [P, 512])
    s_load, s_pro, s_half = s.sem("load"), s.sem("pro"), s.sem("half")
    loaded, stored = Loop(s.sem("loaded"), 16), Loop(s.sem("stored"), 16)
    x_turned, x_moved = Loop(s.sem("x_turned"), 1), Loop(s.sem("x_moved"), 1)
    first, hid_act, hid_dve = Loop(s.sem("first"), 1), Loop(s.sem("hid_act"), 1), Loop(s.sem("hid_dve"), 1)
    turned, turned_act, turned_dve = Loop(s.sem("turned"), 2), Loop(s.sem("turned_act"), 1), Loop(s.sem("turned_dve"), 1)
    second, y_ready = Loop(s.sem("second"), 1), Loop(s.sem("y_ready"), 1)
    tiles_h = sorted_h.rearrange("(g p) c -> g p c", p=P)
    tiles_y = sorted_y.rearrange("(g p) c -> g p c", p=P)

    def turn_x(pe):
        for c in range(KC):
            m = pe.transpose(XP[:, c * P:(c + 1) * P], xs[:, c * P:(c + 1) * P], ident)
        return m

    def first_product(pe, e):
        for j in range(2):
            for c in range(KC):
                m = pe.matmul(A[:, j, :], xT[:, c * P:(c + 1) * P], W1[:, bass.ds(e * (KC * D_FF) + (c * D_FF + j * 512), 512)],
                              start=(c == 0), stop=(c == KC - 1))
        return m

    def expert_of(eng, g):
        return eng.value_load(owner[0:1, bass.ds(g, 1)], min_val=0, max_val=EXPERTS - 1)

    with nc.Block() as block:
        @block.sync
        def _(sp):
            sp.dma_start(b1T[:, :].rearrange("p (e f) -> p e f", f=FF), a["L1_ffn_b1"].rearrange("e (f p) -> p e f", p=P),
                         allow_slow_non_contiguous=True).then_inc(s_load, 16)
            sp.dma_start(b2B[:, :], a["L1_ffn_b2"].rearrange("e c -> (e c)").unsqueeze(0).partition_broadcast(P)).then_inc(s_load, 16)
            sp.wait_ge(s_load, 32)
            for g in range(3):
                if g:
                    sp.wait_ge(s_pro, 3 * g - 2)
                sp.dma_start(xs[:, :], tiles_h[g]).then_inc(s_load, 16)
                sp.wait_ge(s_load, 16 * (3 + g))

        @block.tensor
        def _(pe):
            pe.wait_ge(s_load, 48)
            turn_x(pe).then_inc(s_pro, 1)
            pe.wait_ge(s_pro, 2)
            pe.wait_ge(s_w, 32 * EXPERTS)
            first_product(pe, expert_of(pe, 0)).then_inc(s_pro, 1)
            pe.wait_ge(s_load, 64)
            turn_x(pe).then_inc(s_pro, 1)

        @block.scalar
        def _(act):
            act.wait_ge(s_pro, 1)
            act.copy(xT[:, :], XP[:, 0:C]).then_inc(s_pro, 1)
            act.wait_ge(s_pro, 4)
            act.copy(xT[:, :], XP[:, 0:C]).then_inc(s_pro, 1)
            act.copy(hid[:, 0:512], A[:, 0, :]).then_inc(s_pro, 1)

        @block.vector
        def _(dve):
            dve.wait_ge(s_pro, 3)
            dve.tensor_copy(hid[:, 512:D_FF], A[:, 1, :]).then_inc(s_half, 1)

    with nc.Block() as block:
        @block.tensor
        def _(pe):
            for sem in (turned, first, x_turned, second):
                sem.credit(pe)
            with pe.Fori(0, SLOTS) as g:
                e_next, e = expert_of(pe, g + 1), expert_of(pe, g)
                for j, moved, freed in ((0, hid_act, turned_act), (1, hid_dve, turned_dve)):
                    moved.wait(pe, g, 0)
                    freed.wait(pe, g, 0)
                    for f in range(4):
                        m = pe.transpose(AT[:, j, f * P:(f + 1) * P], hid[:, (4 * j + f) * P:(4 * j + f + 1) * P], ident)
                    m.then_inc(turned.sem, 1)
                x_moved.wait(pe, g, 0)
                first_product(pe, e_next).then_inc(first.sem, 1)
                loaded.wait(pe, g, 0)
                turn_x(pe).then_inc(x_turned.sem, 1)
                turned_act.wait(pe, g, 1)
                turned_dve.wait(pe, g, 1)
                y_ready.wait(pe, g, 0)
                for f in range(FF):
                    m = pe.matmul(Y[:, 0:C], hidT[:, f, :], W2[:, bass.ds(e * (FF * C) + f * C, C)], start=(f == 0), stop=(f == FF - 1))
                m.then_inc(second.sem, 1)

        @block.scalar
        def _(act):
            for sem in (turned_act, hid_act, x_moved):
                sem.credit(act)
            with act.Fori(0, SLOTS) as g:
                e = expert_of(act, g)
                turned.wait(act, g, 1)
                second.wait(act, g, 0)
                for f in range(4):
                    m = act.activation(hidT[:, f, :], AT[:, 0, f * P:(f + 1) * P], ACT.Relu, bias=b1T[:, bass.ds(e * FF + f, 1)])
                m.then_inc(turned_act.sem, 1)
                first.wait(act, g, 1)
                act.copy(hid[:, 0:512], A[:, 0, :]).then_inc(hid_act.sem, 1)
                x_turned.wait(act, g, 1)
                act.copy(xT[:, :], XP[:, 0:C]).then_inc(x_moved.sem, 1)

        @block.vector
        def _(dve):
            for sem in (turned_dve, hid_dve, y_ready):
                sem.credit(dve)
            with dve.Fori(0, SLOTS) as g:
                e = expert_of(dve, g)
                turned.wait(dve, g, 2)
                second.wait(dve, g, 0)
                for f in range(4, FF):
                    m = dve.tensor_scalar(hidT[:, f, :], AT[:, 1, (f - 4) * P:(f - 3) * P], b1T[:, bass.ds(e * FF + f, 1)], 0.0, ALU.add, ALU.max)
                m.then_inc(turned_dve.sem, 1)
                first.wait(dve, g, 1)
                dve.tensor_copy(hid[:, 512:D_FF], A[:, 1, :]).then_inc(hid_dve.sem, 1)
                second.wait(dve, g, 1)
                stored.wait(dve, g, 0)
                dve.tensor_tensor(y[:, :], Y[:, 0:C], b2B[:, bass.ds(e * C, C)], ALU.add).then_inc(y_ready.sem, 1)

        @block.sync
        def _(sp):
            loaded.credit(sp)
            stored.credit(sp)
            with sp.Fori(0, SLOTS) as g:
                following = sp.snap(g + AHEAD)
                x_turned.wait(sp, g, 1)
                sp.dma_start(xs[:, :], tiles_h[bass.ds(following, 1), :, :].rearrange("a p c -> (a p) c")).then_inc(loaded.sem, 16)
                y_ready.wait(sp, g, 1)
                sp.dma_start(tiles_y[bass.ds(g, 1), :, :].rearrange("a p c -> (a p) c"), y[:, :]).then_inc(stored.sem, 16)
            sp.wait_ge(stored.sem, 16 * (SLOTS + 1))
            sp.wait_ge(loaded.sem, 16 * (SLOTS + 1))
    s.clear()



def combine(nc, s, x_all, position, gate, sorted_y, out):
    DEPTH = 8
    yg = s.sb("yg", [P, DEPTH, C])
    got = [s.sem(f"got{d}") for d in range(DEPTH)]
    s_done, s_out = s.sem("done"), s.sem("out")
    PART = 4
    with nc.Block() as block:
        @block.gpsimd
        def _(pool):
            for t in range(NX):
                if t >= DEPTH:
                    pool.wait_ge(s_done, t - DEPTH + 1)
                pool.indirect_dma_start(out=yg[:, t % DEPTH, :], out_offset=None, in_=sorted_y,
                                        in_offset=bass.IndirectOffsetOnAxis(ap=position[:, t:t + 1], axis=0)).then_inc(got[t % DEPTH], 16)

        @block.vector
        def _(dve):
            for t in range(NX):
                dve.wait_ge(got[t % DEPTH], 16 * (t // DEPTH + 1))
                dve.scalar_tensor_tensor(out=x_all[:, t, :], in0=yg[:, t % DEPTH, :], scalar=gate[:, t:t + 1], in1=x_all[:, t, :],
                                         op0=ALU.mult, op1=ALU.add).then_inc(s_done, 1)

        @block.sync
        def _(sp):
            for t in range(0, NX, PART):
                sp.wait_ge(s_done, t + PART)
                sp.dma_start(out[t * P:(t + PART) * P, :].rearrange("(n p) c -> p n c", p=P), x_all[:, t:t + PART, :]).then_inc(s_out, 16)
            sp.wait_ge(s_out, 16 * (NX // PART))
    s.clear()


def build(nc, a, outs, phases=("band", "cross0", "ffn", "self", "cross1", "moe")):
    with ExitStack() as ctx:
        s = Space(nc, ctx, "all")
        x_mem = s.sb("x", [P, NT + NX + NT, C])
        x_all = x_mem[:, NT:, :]
        ident, ident_bf = s.sb("ident", [P, P]), s.sb("ident_bf", [P, P], BF16)
        s_x, s_c, s_id = s.sem("x"), s.sem("c"), s.sem("ident")
        consts = {"ident": ident[:, :], "ident_bf": ident_bf[:, :], "band_d": a["window_bias"],
                  "x_loaded": s_x, "spare": x_mem[:, 0:NT, :].rearrange("p n c -> p (n c)")}
        with nc.Block() as block:
            @block.sync
            def _(sp):
                sp.dma_start(ident[:, :], a["ident"]).then_inc(s_id, 16)
                for n, (first, end) in enumerate(((0, NT), (NT, NX))):
                    sp.dma_start(x_all[:, first:end, :], a["x"][first * P:end * P, :].rearrange("(n p) c -> p n c", p=P)).then_inc(s_x, 16)
                    if n == 0:
                        sp.wait_ge(s_x, 16)
                if "band" not in phases:
                    sp.wait_ge(s_x, 32)

            @block.vector
            def _(dve):
                dve.memset(x_mem[:, 0:NT, :], 0.0).then_inc(s_c, 1)
                dve.memset(x_mem[:, NT + NX:, :], 0.0).then_inc(s_c, 1)
                dve.wait_ge(s_id, 16)
                dve.tensor_copy(ident_bf[:, :], ident[:, :]).then_inc(s_c, 1)
                dve.wait_ge(s_c, 3)

        if "band" in phases:
            band_attention(nc, x_mem, consts, a)
        if "cross0" in phases:
            attention(nc, "cross0", x_mem, consts, 16, a["L0_xattn_W_q"], a["L0_xattn_W_k"], a["L0_xattn_W_v"],
                      a["L0_xattn_W_c"], ctx_d=a["ctx_T"], mask_d=a["mask"],
                      rope=(a["cos0"], a["sin0"], a["turn0"]))
        if "ffn" in phases:
            ternary_ffn(nc, x_mem, consts, a)
        if "self" in phases:
            attention(nc, "self1", x_mem, consts, 64, a["L1_attn_W_q"], a["L1_attn_W_k"], a["L1_attn_W_v"], a["L1_attn_W_out"])
        if "cross1" in phases:
            attention(nc, "cross1", x_mem, consts, 16, a["L1_xattn_WqT"], a["L1_xattn_WkT"], a["L1_xattn_WvT"],
                      a["L1_xattn_WoT"], ctx_d=a["ctx_T"], window=True,
                      rope=(a["cos1"], a["sin1"], a["turn1"]),
                      bias_d=(a["L1_xattn_bq"], a["L1_xattn_bk"], a["L1_xattn_bv"], a["L1_xattn_bo"]))
        if "moe" in phases:
            mixture(nc, x_all, consts, a, outs)
        else:
            with nc.Block() as block:
                @block.sync
                def _(sp):
                    sp.dma_start(outs.rearrange("(n p) c -> p n c", p=P), x_all[:, 0:NX, :]).then_inc(s_x, 16)
                    sp.wait_ge(s_x, 48)


def rotation_tables():
    D = C // H
    f = np.float32
    d = np.arange(P) % D
    w = f(1.0) / f(10000.0) ** (np.arange(1, D + 1, 2, dtype=f) / f(D))
    ang = np.arange(1, T + 1, dtype=f)[None, :] * w[(d // 2)][:, None]
    sign0 = np.where(d % 2 == 0, -1.0, 1.0)[:, None]
    cos0, sin0 = np.cos(ang).astype(f), (np.sin(ang) * sign0).astype(f)
    turn0 = np.zeros((P, P), f)
    turn0[np.arange(P) ^ 1, np.arange(P)] = 1
    half = D // 2
    w = f(1.0) / f(10000.0) ** (np.arange(half, dtype=f) / f(half))
    ang = np.arange(T, dtype=f)[None, :] * w[d % half][:, None]
    sign1 = np.where(d < half, -1.0, 1.0)[:, None]
    cos1, sin1 = np.cos(ang).astype(f), (np.sin(ang) * sign1).astype(f)
    turn1 = np.zeros((P, P), f)
    turn1[np.arange(P) ^ half, np.arange(P)] = 1
    return cos0, sin0, turn0, cos1, sin1, turn1


def shape_constants():
    f = np.float32
    c = {"ident": np.eye(P, dtype=f)}
    c["cos0"], c["sin0"], c["turn0"], c["cos1"], c["sin1"], c["turn1"] = rotation_tables()
    p, k = np.arange(P)[:, None], np.arange(P)[None, :]
    c["window_bias"] = np.where(np.concatenate([k >= p, k <= p], 1), 0.0, NEG).astype(f)
    j = np.arange(BAND)[None, :]
    inside = (j >= p) & (j < p + LOOKBACK)
    c["band_bias"] = np.stack([np.where(inside & (j >= LOOKBACK), 0.0, NEG), np.where(inside, 0.0, NEG)], 1).astype(f)
    c["band_shift"] = (j == p + LOOKBACK - 1).astype(f)
    def mean_weights(tok):
        last = p - 1
        start = last // PHRASE * PHRASE
        return np.where((tok >= start) & (tok <= last), 1.0 / (last - start + 1), 0.0).astype(f)
    c["phrase"] = mean_weights(j - LOOKBACK)
    c["phrase_T"] = np.stack([mean_weights(k - P).T, mean_weights(k).T], 1)
    c["after_first"] = (p > 0).astype(f)
    c["later"] = (p < k).astype(f)
    c["rank"] = np.broadcast_to(np.arange(EXPERTS, 0, -1, dtype=f), (P, EXPERTS)).copy()
    c["slot_no"] = np.broadcast_to(np.arange(SLOTS + AHEAD, dtype=f), (P, SLOTS + AHEAD)).copy()
    return c


def laid_out(inputs):
    a = {k: np.asarray(v) for k, v in inputs.items()}
    m = shape_constants()
    m["x"] = a["x"].reshape(B * T, C)
    m["ctx_T"] = a["ctx_1024"].transpose(0, 2, 1)
    m["mask"] = a["mask_BxS2_bf1"].view(np.uint8)
    for n in ("q", "k", "v", "pk", "pv"):
        m[f"L0_attn_{n}_wT"] = a[f"L0_attn_{n}_w"].T
        m[f"L0_attn_{n}_b"] = a[f"L0_attn_{n}_b"]
    m["L0_xattn_W_q"], m["L0_xattn_W_c"] = a["L0_xattn_W_q"], a["L0_xattn_W_c"]
    m["L0_xattn_W_k"], m["L0_xattn_W_v"] = a["L0_xattn_W_kv"][:, :C], a["L0_xattn_W_kv"][:, C:]
    for n in ("gate", "up", "down"):
        m[f"L0_ffn_w_{n}T"] = a[f"L0_ffn_w_{n}"].T
    qkv = a["L1_attn_W_qkv"].reshape(C, -1, 3)
    for n, name in enumerate("qkv"):
        m[f"L1_attn_W_{name}"] = qkv[:, :, n]
    m["L1_attn_W_out"] = a["L1_attn_W_out"]
    for n in "qkvo":
        m[f"L1_xattn_W{n}T"] = a[f"L1_xattn_W{n}"].T
        m[f"L1_xattn_b{n}"] = a[f"L1_xattn_b{n}"]
    for n in ("router_W", "router_b", "W1", "b1", "W2", "b2"):
        m[f"L1_ffn_{n}"] = a[f"L1_ffn_{n}"]
    return {k: np.ascontiguousarray(v) for k, v in m.items()}


def program(nc, arrays, phases=None):
    a = {k: nc.dram_tensor(f"in_{k}", v.shape, mybir.dt.from_np(v.dtype), kind="ExternalInput").ap() for k, v in arrays.items()}
    out = nc.dram_tensor("out_x", (B * T, C), F32, kind="ExternalOutput").ap()
    build(nc, a, out, *([phases] if phases else []))


def kernel(**inputs):
    import concourse.bacc as bacc
    from concourse.bass_utils import run_bass_kernel_spmd

    arrays = laid_out(inputs)
    nc = bacc.Bacc("TRN2", target_bir_lowering=False, num_devices=1)
    program(nc, arrays)
    r = run_bass_kernel_spmd(nc, [{f"in_{k}": v for k, v in arrays.items()}], core_ids=[0])
    return r.results[0]["out_x"].reshape(B, T, C)
```
